# Optimizing a Trainium2 kernel written in Bass

```python
import numpy as np
import jax
import jax.numpy as jnp

def _softmax(x, axis=-1):
    return jax.nn.softmax(x, axis=axis)

def _gelu(x):
    return jax.nn.gelu(x, approximate=True)

def _silu(x):
    return jax.nn.silu(x)

def _sigmoid(x):
    return jax.nn.sigmoid(x)

def _layernorm(x, axis=-1, eps=1e-05):
    m = jnp.mean(x, axis=axis, keepdims=True)
    v = jnp.var(x, axis=axis, keepdims=True)
    return (x - m) / jnp.sqrt(v + eps)

def _scatter_add(tgt, idx, src, axis=0):
    return tgt.at[idx].add(src)

def _segment_sum(src, seg, n):
    return jax.ops.segment_sum(src, seg, n)
kernel_name = 'mk_xattn_ffn_d4_seqx_r8_194e41'

def setup_inputs(seed: int=0):
    np.random.seed(seed)
    _w = jnp.asarray

    def _rec_inputs():
        import jax
        import jax.numpy as jnp
        _rk = jax.random.key(seed)
        x = 7.22e-05 + 1 * jax.random.normal(jax.random.fold_in(_rk, 1), (64, 128, 128), jnp.float32)
        _lenS = 128 - jax.random.randint(jax.random.fold_in(_rk, 7), (64,), 0, max(1, 128 // 4) + 1, jnp.int32)
        _lenS2 = 120 - jax.random.randint(jax.random.fold_in(_rk, 8), (64,), 0, max(1, 120 // 4) + 1, jnp.int32)
        _ctx_1024P = jax.random.normal(jax.random.fold_in(_rk, 11), (64, 16, 128), jnp.float32)
        _ctx_1024c = jax.random.dirichlet(jax.random.fold_in(_rk, 511), 0.3 * jnp.ones((16,), jnp.float32), (64, 120))
        _ctx_1024t = jnp.einsum('bsk,bkd->bsd', _ctx_1024c, _ctx_1024P)
        _ctx_1024t = _ctx_1024t * jax.lax.rsqrt(jnp.mean(jnp.square(_ctx_1024t)) + 1e-12) * 0.953939
        ctx_1024 = 4.13588e-05 + 0.999923 * (_ctx_1024t + 0.3 * jax.random.normal(jax.random.fold_in(_rk, 611), (64, 120, 128), jnp.float32))
        fside_BxSxS2_0 = jax.random.uniform(jax.random.fold_in(_rk, 12), (64, 128, 120), jnp.float32, 0.0, 10)
        _validS = jnp.arange(128)[None, :] < _lenS[:, None]
        _validS2 = jnp.arange(120)[None, :] < _lenS2[:, None]
        _causal = jnp.tril(jnp.ones((128, 128), dtype=bool))
        mask_Bx1xSxS2_ik1 = jnp.where(jnp.broadcast_to(_validS2[:, None, None, :], (64, 1, 128, 120)), 1, 0).astype(jnp.int32)
        mask_BxSxS2_bk1 = jnp.broadcast_to(_validS2[:, None, :], (64, 128, 120))
        return (x, ctx_1024, fside_BxSxS2_0, mask_Bx1xSxS2_ik1, mask_BxSxS2_bk1)
    x, ctx_1024, fside_BxSxS2_0, mask_Bx1xSxS2_ik1, mask_BxSxS2_bk1 = _rec_inputs()

    def _L0_xattn_setup():
        import jax, jax.numpy as jnp
        import numpy as np
        EMBED_DIM = 128
        NUM_HEADS = 16
        HEAD_DIM = EMBED_DIM // NUM_HEADS
        B, SQ, SK = (4, 256, 256)

        def _xavier(key, shape):
            fan_in, fan_out = (shape[1], shape[0])
            limit = float(np.sqrt(6.0 / (fan_in + fan_out)))
            return jax.random.uniform(key, shape, jnp.float32, -limit, limit)
        key = jax.random.key(seed)
        ks = jax.random.split(key, 9)
        return {'query': jax.random.normal(ks[0], (B, SQ, EMBED_DIM), jnp.float32), 'key_': jax.random.normal(ks[1], (B, SK, EMBED_DIM), jnp.float32), 'value': jax.random.normal(ks[2], (B, SK, EMBED_DIM), jnp.float32), 'distances': jax.random.uniform(ks[3], (B, SQ, SK), jnp.float32, 0.01, 10.0), 'Wq': _xavier(ks[4], (EMBED_DIM, EMBED_DIM)), 'bq': jnp.zeros((EMBED_DIM,), jnp.float32), 'Wk': _xavier(ks[5], (EMBED_DIM, EMBED_DIM)), 'bk': jnp.zeros((EMBED_DIM,), jnp.float32), 'Wv': _xavier(ks[6], (EMBED_DIM, EMBED_DIM)), 'bv': jnp.zeros((EMBED_DIM,), jnp.float32), 'Wo': _xavier(ks[7], (EMBED_DIM, EMBED_DIM)), 'bo': jnp.zeros((EMBED_DIM,), jnp.float32), 'distance_scaling': jnp.asarray(1.0, jnp.float32)}
    _L0_xattn_all = _L0_xattn_setup()
    _L0_xattn_in = {k: v for k, v in _L0_xattn_all.items() if k in ('Wq', 'bq', 'Wk', 'bk', 'Wv', 'bv', 'Wo', 'bo', 'distance_scaling')}
    del _L0_xattn_all

    def _L0_ffn_setup():
        import jax, jax.numpy as jnp
        import numpy as np
        IN_FEATURES = 128
        ACT_BITS = 4

        def _hadamard(size: int) -> np.ndarray:
            h = np.array([[1.0]], dtype=np.float64)
            while h.shape[0] < size:
                h = np.block([[h, h], [h, -h]])
            return (h / np.sqrt(size)).astype(np.float32)

        def _quantize_activations(x, bits=ACT_BITS):
            pos = 2 ** (bits - 1) - 1
            neg = 2 ** (bits - 1)
            scale = jnp.clip(jnp.max(jnp.abs(jax.lax.stop_gradient(x)), axis=-1, keepdims=True), 1e-05) / pos
            q = jnp.clip(jnp.round(x / scale), -neg, pos) * scale
            return x + jax.lax.stop_gradient(q - x)

        def _ternary_quantize_ste(w):
            scale = jnp.clip(jnp.mean(jnp.abs(jax.lax.stop_gradient(w)), axis=1, keepdims=True), 1e-05)
            n = w / scale
            tern = jnp.where(n > 0.5, 1.0, jnp.where(n < -0.5, -1.0, 0.0))
            q = tern * scale
            return w + jax.lax.stop_gradient(q - w)
        key = jax.random.key(seed)
        k1, k2 = jax.random.split(key)
        x = jax.random.normal(k1, (8, 1024, IN_FEATURES), dtype=jnp.float32)
        bound = 1.0 / np.sqrt(IN_FEATURES)
        weight = jax.random.uniform(k2, (128, IN_FEATURES), dtype=jnp.float32, minval=-bound, maxval=bound)
        return {'x': x, 'weight': weight}
    _L0_ffn_all = _L0_ffn_setup()
    _L0_ffn_in = {k: v for k, v in _L0_ffn_all.items() if k in ('weight',)}
    del _L0_ffn_all

    def _L1_xattn_setup():
        import jax, jax.numpy as jnp
        import numpy as np
        D_MODEL = 128
        NUM_HEADS = 16
        D_K = D_MODEL // NUM_HEADS
        NEG_INF = -1000000000.0

        def _split_heads(x):
            B, S, _ = x.shape
            return x.reshape(B, S, NUM_HEADS, D_K).transpose(0, 2, 1, 3)
        key = jax.random.key(seed)
        ks = jax.random.split(key, 13)
        B, S = (2, 256)
        scale = 1.0 / np.sqrt(D_MODEL)
        inp = {'Query': jax.random.normal(ks[0], (B, S, D_MODEL), jnp.float32), 'Key': jax.random.normal(ks[1], (B, S, D_MODEL), jnp.float32), 'Values': jax.random.normal(ks[2], (B, S, D_MODEL), jnp.float32), 'Mask': jax.random.randint(ks[3], (B, 1, S, S), 0, 2, jnp.int32), 'W_q': jax.random.normal(ks[4], (D_MODEL, D_MODEL), jnp.float32) * scale, 'b_q': jnp.zeros((D_MODEL,), jnp.float32), 'W_k': jax.random.normal(ks[5], (D_MODEL, D_MODEL), jnp.float32) * scale, 'b_k': jnp.zeros((D_MODEL,), jnp.float32), 'W_v': jax.random.normal(ks[6], (D_MODEL, D_MODEL), jnp.float32) * scale, 'b_v': jnp.zeros((D_MODEL,), jnp.float32), 'W_o': jax.random.normal(ks[7], (D_MODEL, D_MODEL), jnp.float32) * scale, 'b_o': jnp.zeros((D_MODEL,), jnp.float32)}
        return inp
    _L1_xattn_all = _L1_xattn_setup()
    _L1_xattn_in = {k: v for k, v in _L1_xattn_all.items() if k in ('W_q', 'b_q', 'W_k', 'b_k', 'W_v', 'b_v', 'W_o', 'b_o')}
    del _L1_xattn_all

    def _L1_ffn_setup():
        import jax, jax.numpy as jnp
        import numpy as np
        B, S, D_MODEL, D_HIDDEN = (4, 256, 128, 512)

        def act_quant(x):
            scale = 127.0 / jnp.clip(jnp.max(jnp.abs(x), axis=-1, keepdims=True), 1e-05)
            return jnp.clip(jnp.round(x * scale), -128, 127) / scale

        def weight_quant(w):
            scale = 1.0 / jnp.clip(jnp.mean(jnp.abs(w)), 1e-05)
            return jnp.clip(jnp.round(w * scale), -1, 1) / scale

        def bit_linear(x, w):
            xq = x + jax.lax.stop_gradient(act_quant(x) - x)
            wq = w + jax.lax.stop_gradient(weight_quant(w) - w)
            return jnp.einsum('bsd,hd->bsh', xq, wq)

        def depthwise_conv1d(x_bcl, w, b):
            y = jax.lax.conv_general_dilated(x_bcl, w, window_strides=(1,), padding=[(1, 1)], dimension_numbers=('NCH', 'OIH', 'NCH'), feature_group_count=x_bcl.shape[1])
            return y + b[None, :, None]
        key = jax.random.key(seed)
        ks = jax.random.split(key, 5)
        lim1 = 1.0 / np.sqrt(D_MODEL)
        lim2 = 1.0 / np.sqrt(D_HIDDEN)
        limc = 1.0 / np.sqrt(3.0)
        return {'x': jax.random.normal(ks[0], (B, S, D_MODEL), dtype=jnp.float32), 'w1': jax.random.uniform(ks[1], (D_HIDDEN, D_MODEL), jnp.float32, -lim1, lim1), 'conv_w': jax.random.uniform(ks[2], (D_HIDDEN, 1, 3), jnp.float32, -limc, limc), 'conv_b': jax.random.uniform(ks[3], (D_HIDDEN,), jnp.float32, -limc, limc), 'w2': jax.random.uniform(ks[4], (D_MODEL, D_HIDDEN), jnp.float32, -lim2, lim2)}
    _L1_ffn_all = _L1_ffn_setup()
    _L1_ffn_in = {k: v for k, v in _L1_ffn_all.items() if k in ('w1', 'conv_w', 'conv_b', 'w2')}
    del _L1_ffn_all

    def _L2_xattn_setup():
        import jax, jax.numpy as jnp
        import numpy as np
        HIDDEN = 128
        HEADS = 16
        HEAD_DIM = HIDDEN // HEADS
        SCALE = 1.0 / np.sqrt(HEAD_DIM).astype(np.float32)
        key = jax.random.key(seed)
        ks = jax.random.split(key, 8)
        b, t = (2, 256)
        x = jax.random.normal(ks[0], (b, t, HIDDEN), dtype=jnp.float32)
        context = x
        s = 0.02
        Wq = jax.random.normal(ks[1], (HIDDEN, HIDDEN), dtype=jnp.float32) * s
        Wk = jax.random.normal(ks[2], (HIDDEN, HIDDEN), dtype=jnp.float32) * s
        Wv = jax.random.normal(ks[3], (HIDDEN, HIDDEN), dtype=jnp.float32) * s
        Wo = jax.random.normal(ks[4], (HIDDEN, HIDDEN), dtype=jnp.float32) * s
        bo = jnp.zeros((HIDDEN,), dtype=jnp.float32)
        return {'x': x, 'context': context, 'Wq': Wq, 'Wk': Wk, 'Wv': Wv, 'Wo': Wo, 'bo': bo}
    _L2_xattn_all = _L2_xattn_setup()
    _L2_xattn_in = {k: v for k, v in _L2_xattn_all.items() if k in ('Wq', 'Wk', 'Wv', 'Wo', 'bo')}
    del _L2_xattn_all

    def _L2_ffn_setup():
        import jax, jax.numpy as jnp
        import numpy as np
        E, CAP, D, F = (8, 512, 128, 512)
        key = jax.random.key(seed)
        k0, k1, k2 = jax.random.split(key, 3)
        inputs = jax.random.normal(k0, (1, E * CAP, D), dtype=jnp.float32)
        W1 = jax.random.normal(k1, (E, D, F), dtype=jnp.float32) * (1.0 / np.sqrt(D))
        b1 = jnp.zeros((E, F), dtype=jnp.float32)
        W2 = jax.random.normal(k2, (E, F, D), dtype=jnp.float32) * (1.0 / np.sqrt(F))
        b2 = jnp.zeros((E, D), dtype=jnp.float32)
        return {'inputs': inputs, 'W1': W1, 'b1': b1, 'W2': W2, 'b2': b2}
    _L2_ffn_all = _L2_ffn_setup()
    _L2_ffn_in = {k: v for k, v in _L2_ffn_all.items() if k in ('W1', 'b1', 'W2', 'b2')}
    del _L2_ffn_all

    def _L3_xattn_setup():
        import jax, jax.numpy as jnp
        import numpy as np
        B, NQ, NK, D, H = (2, 256, 256, 128, 16)
        DH = D // H

        def _split_heads(x):
            b, n, d = x.shape
            return x.reshape(b, n, H, DH).transpose(0, 2, 1, 3)

        def attention_core(q, k, v, mask):
            dk = q.shape[-1]
            qh, kh, vh = (_split_heads(q), _split_heads(k), _split_heads(v))
            m = mask[:, None, :, :]
            a = jnp.einsum('bhqd,bhkd->bhqk', qh, kh) / jnp.sqrt(jnp.float32(dk))
            a = jnp.where(m, a, -jnp.inf)
            b = jnp.max(a, axis=-1, keepdims=True)
            b = jnp.where(jnp.isinf(b), 0.0, b)
            p = jnp.exp(a - b)
            p = p / (jnp.sum(p, axis=-1, keepdims=True) + 1e-06)
            x = jnp.einsum('bhqk,bhkd->bhqd', p, vh)
            return x.transpose(0, 2, 1, 3).reshape(q.shape[0], q.shape[1], -1)
        key = jax.random.key(seed)
        ks = jax.random.split(key, 10)
        s = 1.0 / np.sqrt(D).astype(np.float32)
        return {'q': jax.random.normal(ks[0], (B, NQ, D), jnp.float32), 'k': jax.random.normal(ks[1], (B, NK, D), jnp.float32), 'v': jax.random.normal(ks[2], (B, NK, D), jnp.float32), 'mask': jax.random.randint(ks[3], (B, NQ, NK), 0, 2).astype(bool), 'Wq': jax.random.normal(ks[4], (D, D), jnp.float32) * s, 'bq': jax.random.normal(ks[5], (D,), jnp.float32) * 0.02, 'Wk': jax.random.normal(ks[6], (D, D), jnp.float32) * s, 'bk': jax.random.normal(ks[7], (D,), jnp.float32) * 0.02, 'Wv': jax.random.normal(ks[8], (D, D), jnp.float32) * s, 'bv': jax.random.normal(ks[9], (D,), jnp.float32) * 0.02}
    _L3_xattn_all = _L3_xattn_setup()
    _L3_xattn_in = {k: v for k, v in _L3_xattn_all.items() if k in ('Wq', 'bq', 'Wk', 'bk', 'Wv', 'bv')}
    del _L3_xattn_all

    def _L3_ffn_setup():
        import jax, jax.numpy as jnp
        import numpy as np
        S_LEN, BATCH, HIDDEN = (256, 2, 128)
        N_HEADS, N_KV = (16, 8)
        N_EXP, TOP_K, CAP_F = (8, 2, 1.25)
        FFN = 512
        HEAD_DIM = HIDDEN // N_HEADS
        Q_PER_KV = N_HEADS // N_KV
        EPS = 1e-05
        NEG = -1000000000.0

        def _ln(x, w, b):
            mu = jnp.mean(x, -1, keepdims=True)
            var = jnp.var(x, -1, keepdims=True)
            return (x - mu) * jax.lax.rsqrt(var + EPS) * w + b

        def _forward(hidden_states, ln1_weight, ln1_bias, ln2_weight, ln2_bias, qkv_weight, proj_weight, router_weight, moe_w1, moe_w2):
            S, B, H = hidden_states.shape
            ln1 = _ln(hidden_states, ln1_weight, ln1_bias)
            qkv = (ln1 @ qkv_weight.T).reshape(S, B, N_KV, (Q_PER_KV + 2) * HEAD_DIM)
            q_dim = Q_PER_KV * HEAD_DIM
            q = qkv[..., :q_dim].reshape(S, B, N_HEADS, HEAD_DIM)
            k = jnp.repeat(qkv[..., q_dim:q_dim + HEAD_DIM], Q_PER_KV, axis=2)
            v = jnp.repeat(qkv[..., q_dim + HEAD_DIM:], Q_PER_KV, axis=2)
            scores = jnp.einsum('sbhd,tbhd->bhst', q, k) / jnp.sqrt(jnp.float32(HEAD_DIM))
            causal = jnp.tril(jnp.ones((S, S), bool))
            attn = jax.nn.softmax(jnp.where(causal[None, None], scores, NEG), axis=-1)
            attn_out = jnp.einsum('bhst,tbhd->sbhd', attn, v).reshape(S, B, H)
            hidden_after_attn = hidden_states + attn_out @ proj_weight.T
            x = _ln(hidden_after_attn, ln2_weight, ln2_bias).reshape(-1, H)
            N = S * B
            probs = jax.nn.softmax(x.astype(jnp.float32) @ router_weight, axis=-1)
            top_p, top_i = jax.lax.top_k(probs, TOP_K)
            top_p = top_p / jnp.sum(top_p, -1, keepdims=True)
            flat_exp = top_i.reshape(-1)
            order = jnp.argsort(flat_exp)
            sorted_exp = flat_exp[order]
            counts = jnp.bincount(sorted_exp, length=N_EXP)
            offsets = jnp.concatenate([jnp.zeros((1,), counts.dtype), jnp.cumsum(counts)])
            within = jnp.arange(N * TOP_K) - offsets[sorted_exp]
            cap = int(np.ceil(N * TOP_K / N_EXP * CAP_F))
            keep = within < cap
            slot = jnp.where(keep, sorted_exp * cap + within, N_EXP * cap)
            tok_id = order // TOP_K
            padded_tokens = jnp.zeros((N_EXP * cap + 1, H), x.dtype).at[slot].set(x[tok_id])[:-1]
            padded_probs = jnp.zeros((N_EXP * cap + 1,), jnp.float32).at[slot].set(top_p.reshape(-1)[order])[:-1]
            padded_ids = jnp.zeros((N_EXP * cap + 1,), jnp.int32).at[slot].set(tok_id.astype(jnp.int32))[:-1]
            exp_in = padded_tokens.reshape(N_EXP, cap, H)
            act = jax.nn.gelu(jnp.einsum('ech,ehf->ecf', exp_in, moe_w1), approximate=False)
            exp_out = jnp.einsum('ecf,efh->ech', act, moe_w2).reshape(N_EXP * cap, H)
            weighted = exp_out * padded_probs[:, None].astype(exp_out.dtype)
            moe = jnp.zeros((N, H), exp_out.dtype).at[padded_ids].add(weighted)
            return hidden_after_attn + moe.reshape(S, B, H)
        ks = jax.random.split(jax.random.key(seed), 6)
        qkv_out = N_KV * (Q_PER_KV + 2) * HEAD_DIM
        sc = 0.02
        return {'hidden_states': jax.random.normal(ks[0], (S_LEN, BATCH, HIDDEN), jnp.float32), 'ln1_weight': jnp.ones((HIDDEN,), jnp.float32), 'ln1_bias': jnp.zeros((HIDDEN,), jnp.float32), 'ln2_weight': jnp.ones((HIDDEN,), jnp.float32), 'ln2_bias': jnp.zeros((HIDDEN,), jnp.float32), 'qkv_weight': jax.random.normal(ks[1], (qkv_out, HIDDEN), jnp.float32) * sc, 'proj_weight': jax.random.normal(ks[2], (HIDDEN, HIDDEN), jnp.float32) * sc, 'router_weight': jax.random.normal(ks[3], (HIDDEN, N_EXP), jnp.float32) * sc, 'moe_w1': jax.random.normal(ks[4], (N_EXP, HIDDEN, FFN), jnp.float32) * sc, 'moe_w2': jax.random.normal(ks[5], (N_EXP, FFN, HIDDEN), jnp.float32) * sc}
    _L3_ffn_all = _L3_ffn_setup()
    _L3_ffn_in = {k: v for k, v in _L3_ffn_all.items() if k in ('ln1_weight', 'ln1_bias', 'ln2_weight', 'ln2_bias', 'qkv_weight', 'proj_weight', 'router_weight', 'moe_w1', 'moe_w2')}
    del _L3_ffn_all
    return {'x': x, 'ctx_1024': ctx_1024, 'fside_BxSxS2_0': fside_BxSxS2_0, 'mask_Bx1xSxS2_ik1': mask_Bx1xSxS2_ik1, 'mask_BxSxS2_bk1': mask_BxSxS2_bk1, 'L0_xattn_Wq': _L0_xattn_in['Wq'], 'L0_xattn_bq': _L0_xattn_in['bq'], 'L0_xattn_Wk': _L0_xattn_in['Wk'], 'L0_xattn_bk': _L0_xattn_in['bk'], 'L0_xattn_Wv': _L0_xattn_in['Wv'], 'L0_xattn_bv': _L0_xattn_in['bv'], 'L0_xattn_Wo': _L0_xattn_in['Wo'], 'L0_xattn_bo': _L0_xattn_in['bo'], 'L0_xattn_distance_scaling': _L0_xattn_in['distance_scaling'], 'L0_ffn_weight': _L0_ffn_in['weight'], 'L1_xattn_W_q': _L1_xattn_in['W_q'], 'L1_xattn_b_q': _L1_xattn_in['b_q'], 'L1_xattn_W_k': _L1_xattn_in['W_k'], 'L1_xattn_b_k': _L1_xattn_in['b_k'], 'L1_xattn_W_v': _L1_xattn_in['W_v'], 'L1_xattn_b_v': _L1_xattn_in['b_v'], 'L1_xattn_W_o': _L1_xattn_in['W_o'], 'L1_xattn_b_o': _L1_xattn_in['b_o'], 'L1_ffn_w1': _L1_ffn_in['w1'], 'L1_ffn_conv_w': _L1_ffn_in['conv_w'], 'L1_ffn_conv_b': _L1_ffn_in['conv_b'], 'L1_ffn_w2': _L1_ffn_in['w2'], 'L2_xattn_Wq': _L2_xattn_in['Wq'], 'L2_xattn_Wk': _L2_xattn_in['Wk'], 'L2_xattn_Wv': _L2_xattn_in['Wv'], 'L2_xattn_Wo': _L2_xattn_in['Wo'], 'L2_xattn_bo': _L2_xattn_in['bo'], 'L2_ffn_W1': _L2_ffn_in['W1'], 'L2_ffn_b1': _L2_ffn_in['b1'], 'L2_ffn_W2': _L2_ffn_in['W2'], 'L2_ffn_b2': _L2_ffn_in['b2'], 'L3_xattn_Wq': _L3_xattn_in['Wq'], 'L3_xattn_bq': _L3_xattn_in['bq'], 'L3_xattn_Wk': _L3_xattn_in['Wk'], 'L3_xattn_bk': _L3_xattn_in['bk'], 'L3_xattn_Wv': _L3_xattn_in['Wv'], 'L3_xattn_bv': _L3_xattn_in['bv'], 'L3_ffn_ln1_weight': _L3_ffn_in['ln1_weight'], 'L3_ffn_ln1_bias': _L3_ffn_in['ln1_bias'], 'L3_ffn_ln2_weight': _L3_ffn_in['ln2_weight'], 'L3_ffn_ln2_bias': _L3_ffn_in['ln2_bias'], 'L3_ffn_qkv_weight': _L3_ffn_in['qkv_weight'], 'L3_ffn_proj_weight': _L3_ffn_in['proj_weight'], 'L3_ffn_router_weight': _L3_ffn_in['router_weight'], 'L3_ffn_moe_w1': _L3_ffn_in['moe_w1'], 'L3_ffn_moe_w2': _L3_ffn_in['moe_w2']}

def reference(x, ctx_1024, fside_BxSxS2_0, mask_Bx1xSxS2_ik1, mask_BxSxS2_bk1, L0_xattn_Wq, L0_xattn_bq, L0_xattn_Wk, L0_xattn_bk, L0_xattn_Wv, L0_xattn_bv, L0_xattn_Wo, L0_xattn_bo, L0_xattn_distance_scaling, L0_ffn_weight, L1_xattn_W_q, L1_xattn_b_q, L1_xattn_W_k, L1_xattn_b_k, L1_xattn_W_v, L1_xattn_b_v, L1_xattn_W_o, L1_xattn_b_o, L1_ffn_w1, L1_ffn_conv_w, L1_ffn_conv_b, L1_ffn_w2, L2_xattn_Wq, L2_xattn_Wk, L2_xattn_Wv, L2_xattn_Wo, L2_xattn_bo, L2_ffn_W1, L2_ffn_b1, L2_ffn_W2, L2_ffn_b2, L3_xattn_Wq, L3_xattn_bq, L3_xattn_Wk, L3_xattn_bk, L3_xattn_Wv, L3_xattn_bv, L3_ffn_ln1_weight, L3_ffn_ln1_bias, L3_ffn_ln2_weight, L3_ffn_ln2_bias, L3_ffn_qkv_weight, L3_ffn_proj_weight, L3_ffn_router_weight, L3_ffn_moe_w1, L3_ffn_moe_w2):
    import jax
    import jax.numpy as jnp

    def _L0_xattn_ref(query, key_, value, distances, Wq, bq, Wk, bk, Wv, bv, Wo, bo, distance_scaling):
        import jax, jax.numpy as jnp
        import numpy as np
        EMBED_DIM = 128
        NUM_HEADS = 16
        HEAD_DIM = EMBED_DIM // NUM_HEADS
        B, SQ, SK = (4, 256, 256)

        def _xavier(key, shape):
            fan_in, fan_out = (shape[1], shape[0])
            limit = float(np.sqrt(6.0 / (fan_in + fan_out)))
            return jax.random.uniform(key, shape, jnp.float32, -limit, limit)
        b, sq, e = query.shape
        sk = key_.shape[1]
        h, d = (NUM_HEADS, HEAD_DIM)
        q = (query @ Wq.T + bq) * d ** (-0.5)
        k = key_ @ Wk.T + bk
        v = value @ Wv.T + bv
        q = q.reshape(b, sq, h, d).transpose(0, 2, 1, 3)
        k = k.reshape(b, sk, h, d).transpose(0, 2, 1, 3)
        v = v.reshape(b, sk, h, d).transpose(0, 2, 1, 3)
        scores = jnp.einsum('bhqd,bhkd->bhqk', q, k)
        distance_bias = -jnp.log(distances + 1e-09) * jnp.abs(distance_scaling)
        scores = scores + distance_bias[:, None, :, :]
        attn = jax.nn.softmax(scores, axis=-1)
        out = jnp.einsum('bhqk,bhkd->bhqd', attn, v)
        out = out.transpose(0, 2, 1, 3).reshape(b, sq, e)
        return out @ Wo.T + bo

    def _L0_ffn_ref(x, weight):
        import jax, jax.numpy as jnp
        import numpy as np
        IN_FEATURES = 128
        ACT_BITS = 4

        def _hadamard(size: int) -> np.ndarray:
            h = np.array([[1.0]], dtype=np.float64)
            while h.shape[0] < size:
                h = np.block([[h, h], [h, -h]])
            return (h / np.sqrt(size)).astype(np.float32)

        def _quantize_activations(x, bits=ACT_BITS):
            pos = 2 ** (bits - 1) - 1
            neg = 2 ** (bits - 1)
            scale = jnp.clip(jnp.max(jnp.abs(jax.lax.stop_gradient(x)), axis=-1, keepdims=True), 1e-05) / pos
            q = jnp.clip(jnp.round(x / scale), -neg, pos) * scale
            return x + jax.lax.stop_gradient(q - x)

        def _ternary_quantize_ste(w):
            scale = jnp.clip(jnp.mean(jnp.abs(jax.lax.stop_gradient(w)), axis=1, keepdims=True), 1e-05)
            n = w / scale
            tern = jnp.where(n > 0.5, 1.0, jnp.where(n < -0.5, -1.0, 0.0))
            q = tern * scale
            return w + jax.lax.stop_gradient(q - w)
        H = jnp.asarray(_hadamard(IN_FEATURES))
        xh = x @ H
        xq = _quantize_activations(xh)
        wq = _ternary_quantize_ste(weight)
        return jnp.einsum('bsi,oi->bso', xq, wq)

    def _L1_xattn_ref(Query, Key, Values, Mask, W_q, b_q, W_k, b_k, W_v, b_v, W_o, b_o):
        import jax, jax.numpy as jnp
        import numpy as np
        D_MODEL = 128
        NUM_HEADS = 16
        D_K = D_MODEL // NUM_HEADS
        NEG_INF = -1000000000.0

        def _split_heads(x):
            B, S, _ = x.shape
            return x.reshape(B, S, NUM_HEADS, D_K).transpose(0, 2, 1, 3)
        q = _split_heads(Query @ W_q.T + b_q)
        k = _split_heads(Key @ W_k.T + b_k)
        v = _split_heads(Values @ W_v.T + b_v)
        scores = jnp.einsum('bhqd,bhkd->bhqk', q, k) / jnp.sqrt(jnp.float32(D_K))
        scores = jnp.where(Mask == 0, jnp.float32(NEG_INF), scores)
        attn = jax.nn.softmax(scores, axis=-1)
        out = jnp.einsum('bhqk,bhkd->bhqd', attn, v)
        B, H, S, Dk = out.shape
        out = out.transpose(0, 2, 1, 3).reshape(B, S, H * Dk)
        return out @ W_o.T + b_o

    def _L1_ffn_ref(x, w1, conv_w, conv_b, w2):
        import jax, jax.numpy as jnp
        import numpy as np
        B, S, D_MODEL, D_HIDDEN = (4, 256, 128, 512)

        def act_quant(x):
            scale = 127.0 / jnp.clip(jnp.max(jnp.abs(x), axis=-1, keepdims=True), 1e-05)
            return jnp.clip(jnp.round(x * scale), -128, 127) / scale

        def weight_quant(w):
            scale = 1.0 / jnp.clip(jnp.mean(jnp.abs(w)), 1e-05)
            return jnp.clip(jnp.round(w * scale), -1, 1) / scale

        def bit_linear(x, w):
            xq = x + jax.lax.stop_gradient(act_quant(x) - x)
            wq = w + jax.lax.stop_gradient(weight_quant(w) - w)
            return jnp.einsum('bsd,hd->bsh', xq, wq)

        def depthwise_conv1d(x_bcl, w, b):
            y = jax.lax.conv_general_dilated(x_bcl, w, window_strides=(1,), padding=[(1, 1)], dimension_numbers=('NCH', 'OIH', 'NCH'), feature_group_count=x_bcl.shape[1])
            return y + b[None, :, None]
        h = bit_linear(x, w1)
        h = depthwise_conv1d(h.transpose(0, 2, 1), conv_w, conv_b)
        h = h.transpose(0, 2, 1)
        h = jax.nn.silu(h)
        return bit_linear(h, w2)

    def _L2_xattn_ref(x, context, Wq, Wk, Wv, Wo, bo):
        import jax, jax.numpy as jnp
        import numpy as np
        HIDDEN = 128
        HEADS = 16
        HEAD_DIM = HIDDEN // HEADS
        SCALE = 1.0 / np.sqrt(HEAD_DIM).astype(np.float32)
        b, t, c = x.shape
        kv_t = context.shape[1]
        q = x @ Wq.T
        k = context @ Wk.T
        v = context @ Wv.T
        q = q.reshape(b, t, HEADS, HEAD_DIM).transpose(0, 2, 1, 3)
        k = k.reshape(b, kv_t, HEADS, HEAD_DIM).transpose(0, 2, 1, 3)
        v = v.reshape(b, kv_t, HEADS, HEAD_DIM).transpose(0, 2, 1, 3)
        scores = jnp.einsum('bhqd,bhkd->bhqk', q, k) * SCALE
        causal = jnp.tril(jnp.ones((t, kv_t), dtype=bool))
        scores = jnp.where(causal[None, None, :, :], scores, -jnp.inf)
        probs = jax.nn.softmax(scores, axis=-1)
        y = jnp.einsum('bhqk,bhkd->bhqd', probs, v)
        y = y.transpose(0, 2, 1, 3).reshape(b, t, c)
        return y @ Wo.T + bo

    def _L2_ffn_ref(inputs, W1, b1, W2, b2):
        import jax, jax.numpy as jnp
        import numpy as np
        E, CAP, D, F = (8, 512, 128, 512)
        B, T, D_ = inputs.shape
        x = inputs.reshape(B, E, T // E, D_)
        h = jax.nn.gelu(jnp.einsum('becd,edf->becf', x, W1) + b1[None, :, None, :])
        y = jnp.einsum('becf,efd->becd', h, W2) + b2[None, :, None, :]
        return y.reshape(B, T, D_)

    def _L3_xattn_ref(q, k, v, mask, Wq, bq, Wk, bk, Wv, bv):
        import jax, jax.numpy as jnp
        import numpy as np
        B, NQ, NK, D, H = (2, 256, 256, 128, 16)
        DH = D // H

        def _split_heads(x):
            b, n, d = x.shape
            return x.reshape(b, n, H, DH).transpose(0, 2, 1, 3)

        def attention_core(q, k, v, mask):
            dk = q.shape[-1]
            qh, kh, vh = (_split_heads(q), _split_heads(k), _split_heads(v))
            m = mask[:, None, :, :]
            a = jnp.einsum('bhqd,bhkd->bhqk', qh, kh) / jnp.sqrt(jnp.float32(dk))
            a = jnp.where(m, a, -jnp.inf)
            b = jnp.max(a, axis=-1, keepdims=True)
            b = jnp.where(jnp.isinf(b), 0.0, b)
            p = jnp.exp(a - b)
            p = p / (jnp.sum(p, axis=-1, keepdims=True) + 1e-06)
            x = jnp.einsum('bhqk,bhkd->bhqd', p, vh)
            return x.transpose(0, 2, 1, 3).reshape(q.shape[0], q.shape[1], -1)
        qt = q @ Wq.T + bq
        kt = k @ Wk.T + bk
        vt = v @ Wv.T + bv
        return attention_core(qt, kt, vt, mask)

    def _L3_ffn_ref(hidden_states, ln1_weight, ln1_bias, ln2_weight, ln2_bias, qkv_weight, proj_weight, router_weight, moe_w1, moe_w2):
        import jax, jax.numpy as jnp
        import numpy as np
        S_LEN, BATCH, HIDDEN = (256, 2, 128)
        N_HEADS, N_KV = (16, 8)
        N_EXP, TOP_K, CAP_F = (8, 2, 1.25)
        FFN = 512
        HEAD_DIM = HIDDEN // N_HEADS
        Q_PER_KV = N_HEADS // N_KV
        EPS = 1e-05
        NEG = -1000000000.0

        def _ln(x, w, b):
            mu = jnp.mean(x, -1, keepdims=True)
            var = jnp.var(x, -1, keepdims=True)
            return (x - mu) * jax.lax.rsqrt(var + EPS) * w + b

        def _forward(hidden_states, ln1_weight, ln1_bias, ln2_weight, ln2_bias, qkv_weight, proj_weight, router_weight, moe_w1, moe_w2):
            S, B, H = hidden_states.shape
            ln1 = _ln(hidden_states, ln1_weight, ln1_bias)
            qkv = (ln1 @ qkv_weight.T).reshape(S, B, N_KV, (Q_PER_KV + 2) * HEAD_DIM)
            q_dim = Q_PER_KV * HEAD_DIM
            q = qkv[..., :q_dim].reshape(S, B, N_HEADS, HEAD_DIM)
            k = jnp.repeat(qkv[..., q_dim:q_dim + HEAD_DIM], Q_PER_KV, axis=2)
            v = jnp.repeat(qkv[..., q_dim + HEAD_DIM:], Q_PER_KV, axis=2)
            scores = jnp.einsum('sbhd,tbhd->bhst', q, k) / jnp.sqrt(jnp.float32(HEAD_DIM))
            causal = jnp.tril(jnp.ones((S, S), bool))
            attn = jax.nn.softmax(jnp.where(causal[None, None], scores, NEG), axis=-1)
            attn_out = jnp.einsum('bhst,tbhd->sbhd', attn, v).reshape(S, B, H)
            hidden_after_attn = hidden_states + attn_out @ proj_weight.T
            x = _ln(hidden_after_attn, ln2_weight, ln2_bias).reshape(-1, H)
            N = S * B
            probs = jax.nn.softmax(x.astype(jnp.float32) @ router_weight, axis=-1)
            top_p, top_i = jax.lax.top_k(probs, TOP_K)
            top_p = top_p / jnp.sum(top_p, -1, keepdims=True)
            flat_exp = top_i.reshape(-1)
            order = jnp.argsort(flat_exp)
            sorted_exp = flat_exp[order]
            counts = jnp.bincount(sorted_exp, length=N_EXP)
            offsets = jnp.concatenate([jnp.zeros((1,), counts.dtype), jnp.cumsum(counts)])
            within = jnp.arange(N * TOP_K) - offsets[sorted_exp]
            cap = int(np.ceil(N * TOP_K / N_EXP * CAP_F))
            keep = within < cap
            slot = jnp.where(keep, sorted_exp * cap + within, N_EXP * cap)
            tok_id = order // TOP_K
            padded_tokens = jnp.zeros((N_EXP * cap + 1, H), x.dtype).at[slot].set(x[tok_id])[:-1]
            padded_probs = jnp.zeros((N_EXP * cap + 1,), jnp.float32).at[slot].set(top_p.reshape(-1)[order])[:-1]
            padded_ids = jnp.zeros((N_EXP * cap + 1,), jnp.int32).at[slot].set(tok_id.astype(jnp.int32))[:-1]
            exp_in = padded_tokens.reshape(N_EXP, cap, H)
            act = jax.nn.gelu(jnp.einsum('ech,ehf->ecf', exp_in, moe_w1), approximate=False)
            exp_out = jnp.einsum('ecf,efh->ech', act, moe_w2).reshape(N_EXP * cap, H)
            weighted = exp_out * padded_probs[:, None].astype(exp_out.dtype)
            moe = jnp.zeros((N, H), exp_out.dtype).at[padded_ids].add(weighted)
            return hidden_after_attn + moe.reshape(S, B, H)
        return _forward(hidden_states, ln1_weight, ln1_bias, ln2_weight, ln2_bias, qkv_weight, proj_weight, router_weight, moe_w1, moe_w2)
    x = x + _L0_xattn_ref(_layernorm(x, axis=-1), ctx_1024, ctx_1024, fside_BxSxS2_0, L0_xattn_Wq, L0_xattn_bq, L0_xattn_Wk, L0_xattn_bk, L0_xattn_Wv, L0_xattn_bv, L0_xattn_Wo, L0_xattn_bo, L0_xattn_distance_scaling)
    x = x + _L0_ffn_ref(_layernorm(x, axis=-1), L0_ffn_weight)
    x = x + _L1_xattn_ref(_layernorm(x, axis=-1), ctx_1024, ctx_1024, mask_Bx1xSxS2_ik1, L1_xattn_W_q, L1_xattn_b_q, L1_xattn_W_k, L1_xattn_b_k, L1_xattn_W_v, L1_xattn_b_v, L1_xattn_W_o, L1_xattn_b_o)
    x = x + _L1_ffn_ref(_layernorm(x, axis=-1), L1_ffn_w1, L1_ffn_conv_w, L1_ffn_conv_b, L1_ffn_w2)
    x = x + _L2_xattn_ref(_layernorm(x, axis=-1), ctx_1024, L2_xattn_Wq, L2_xattn_Wk, L2_xattn_Wv, L2_xattn_Wo, L2_xattn_bo)
    x = x + _L2_ffn_ref(_layernorm(x, axis=-1), L2_ffn_W1, L2_ffn_b1, L2_ffn_W2, L2_ffn_b2)
    x = x + _L3_xattn_ref(_layernorm(x, axis=-1), ctx_1024, ctx_1024, mask_BxSxS2_bk1, L3_xattn_Wq, L3_xattn_bq, L3_xattn_Wk, L3_xattn_bk, L3_xattn_Wv, L3_xattn_bv)
    x = x + _L3_ffn_ref(_layernorm(x, axis=-1), L3_ffn_ln1_weight, L3_ffn_ln1_bias, L3_ffn_ln2_weight, L3_ffn_ln2_bias, L3_ffn_qkv_weight, L3_ffn_proj_weight, L3_ffn_router_weight, L3_ffn_moe_w1, L3_ffn_moe_w2)
    return x

_drawn_inputs = setup_inputs


def setup_inputs(seed=0):
    import zlib

    import numpy as np

    out = dict(_drawn_inputs(seed))
    spreads = {'L0_xattn_bq': (0.0, 0.1),
     'L0_xattn_bk': (0.0, 2.0),
     'L0_xattn_bv': (0.0, 0.1),
     'L0_xattn_bo': (0.0, 0.1),
     'L1_xattn_b_q': (0.0, 0.627),
     'L1_xattn_b_k': (0.0, 2.0),
     'L1_xattn_b_v': (0.0, 0.1),
     'L1_xattn_b_o': (0.0, 0.1),
     'L2_xattn_bo': (0.0, 0.1),
     'L2_ffn_b1': (0.0, 0.1),
     'L2_ffn_b2': (0.0, 0.1),
     'L3_ffn_ln1_weight': (1.0, 0.6),
     'L3_ffn_ln1_bias': (0.0, 0.8),
     'L3_ffn_ln2_weight': (1.0, 0.6),
     'L3_ffn_ln2_bias': (0.0, 0.8)}
    factors = {'L2_xattn_Wq': 8.0,
     'L2_xattn_Wk': 8.0,
     'L2_xattn_Wv': 3.396,
     'L2_xattn_Wo': 3.414,
     'L3_xattn_bq': 22.941,
     'L3_xattn_bk': 64.0,
     'L3_xattn_bv': 4.487,
     'L3_ffn_qkv_weight': 8.0,
     'L3_ffn_proj_weight': 8.0,
     'L3_ffn_router_weight': 4.716,
     'L3_ffn_moe_w1': 4.101,
     'L3_ffn_moe_w2': 4.06}
    for name, (base, spread) in spreads.items():
        noise = np.random.default_rng([zlib.crc32(name.encode()), seed]).standard_normal(out[name].shape)
        drawn = base * np.exp(spread * noise) if base else spread * noise
        out[name] = jnp.asarray(drawn.astype(out[name].dtype))
    for name, factor in factors.items():
        out[name] = (out[name] * factor).astype(out[name].dtype)
    return out
```

```python
from contextlib import ExitStack

import numpy as np

import concourse.bass as bass
from concourse import mybir

F32 = mybir.dt.float32
BF16 = mybir.dt.bfloat16
I32 = mybir.dt.int32
U8 = mybir.dt.uint8
ALU = mybir.AluOpType
ACT = mybir.ActivationFunctionType
AX = mybir.AxisListType

P = 128
NB = 64
NC = 120
NH = 16
DH = P // NH
HG = 4
NG = NH // HG
NE = 8
FF = 512
FC = FF // P
CAP = 2560
EPS = 1e-5
QSCALE = [float(1.0 / np.sqrt(np.float32(w))) for w in (DH, DH, DH, P, DH)]
MASKED = -(2.0 ** 100)
ROUND = 1.5 * 2.0 ** 23

LAST = 4

_ORDER = [0, 10, 1, 11, 2, 12, 3, "ln1", "ln1b", 4, 13, "end"]
GO = {s: k + 1 for k, s in enumerate(_ORDER)}
if LAST < 4:
    GO["end"] = int(2 * LAST) + 2
W_IN = {0: 32, 1: 64, 2: 96, 3: 128, "ln1": 144, 4: 176, "ln2": 192}
G0 = 2 * NE * FC


def build(nc, d, out, last_stage=99):
    with ExitStack() as ctx:
        def sb(name, shape, dt=F32):
            return ctx.enter_context(nc.sbuf_tensor(name, shape, dt))

        x = sb("x", [P, NB, P])
        h_all = sb("h_all", [P, NB, P])
        xT_all = sb("xT_all", [P, NB, P])
        w1_sb = sb("w1_sb", [P, NE, FF])
        w2_sb = sb("w2_sb", [P, NE, FC, P])
        cpack = sb("cpack", [P, 3 * P + HG + NE])
        ident, hada, onesf = cpack[:, 0:P], cpack[:, P:2 * P], cpack[:, 2 * P:3 * P]
        headmask = cpack[:, 3 * P:3 * P + HG]
        descend = cpack[:, 3 * P + HG:3 * P + HG + NE]
        identb = sb("identb", [P, P], BF16)
        causalb = sb("causalb", [P, 2, P], BF16)
        trib = sb("trib", [P, P], BF16)
        onesb = sb("onesb", [P, P], BF16)
        selb = sb("selb", [P, HG, P], BF16)
        wm = sb("wm", [P, 4, P])
        cols = sb("cols", [P, 10])
        rows = sb("rows", [P, 2, P])
        stats = sb("stats", [P, NB, 6])
        rstd = sb("rstd", [P, NB])
        nmr = sb("nmr", [P, NB])
        t1 = sb("t1", [P, NB])
        t2 = sb("t2", [P, NB])
        dscale = sb("dscale", [P, 1])
        xn = sb("xn", [P, 4, P])
        ctx_sb = sb("ctx_sb", [NC, 2, P])
        braw = sb("braw", [P, 2, NC])
        bln = sb("bln", [P, 2, NC])
        braw_u = sb("braw_u", [P, 2, NC], U8)
        biasf = sb("biasf", [P, 2, NC])
        biasb = sb("biasb", [P, 2, NC], BF16)
        xcT = sb("xcT", [P, 2, 2 * P])
        qf = sb("qf", [P, 2, P])
        kblk = sb("kblk", [P, 2, HG * P])
        qb = sb("qb", [P, 2, P], BF16)
        kb = sb("kb", [P, 2, HG * P], BF16)
        vaug = sb("vaug", [P, 2, NH, DH + 1])
        negmax = sb("negmax", [P, 2, NH])
        mparts = sb("mparts", [P, 2, NG, 32], BF16)
        mT = sb("mT", [P, 2, P], BF16)
        ex = sb("ex", [P, 2, NH * P])
        rec = sb("rec", [P, 2, NH])
        o_sb = sb("o_sb", [P, 2, P])
        oT = sb("oT", [P, 2, P])
        y_sb = sb("y_sb", [P, 2, P])
        work = sb("work", [P, 4, FF])
        workb = sb("workb", [P, 4, FF], BF16)
        qT = sb("qT", [P, 4, FF], BF16)
        xqT = sb("xqT", [P, 4, P + 2])
        sc = sb("sc", [P, 4, 4])
        ternT = sb("ternT", [P, P], BF16)
        wscale = sb("wscale", [P, P])
        wconv = sb("wconv", [P, 3, FF])
        convb = sb("convb", [1, FF])
        w2q = sb("w2q", [P, FC, P], BF16)
        sm = sb("sm", [P, 12])
        b1c = sb("b1c", [P, NE, FC])
        b2c = sb("b2c", [P, NE])
        router = sb("router", [P, NE])
        coef = sb("coef", [P, NB, NE])
        hid = ex[:, :, :].rearrange("p a (c n) -> p a c n", c=FC)
        ra, rb, rc_, rd = (work[:, k, :].rearrange("p (s e) -> p s e", e=NE) for k in range(4))
        selbf = workb[:, 0, :]

        ps = ctx.enter_context(nc.psum_tensor("ps", [P, 8, 512], F32))
        a_ps = [ps[:, 0, :], ps[:, 1, :]]
        b_ps = [ps[:, 2:4, :].rearrange("p a n -> p (a n)"), ps[:, 4:6, :].rearrange("p a n -> p (a n)")]
        front, back = ps[:, 6, :], ps[:, 7, :]
        mT_ps = ps[:, 0, 0:64].bitcast(BF16)

        u_dram = nc.dram_tensor("u_dram", [NB, P, P], F32, kind="Internal").ap()
        y_dram = nc.dram_tensor("y_dram", [NB, P, P], F32, kind="Internal").ap()

        names = """consts_in weights_in stage_w_in u_out ctx_in0 ctx_in1 bias_in0 bias_in1 u_in0 u_in1
            y_out0 y_out1 y_in moe_w_in out_done stage_go sq_in sq_out dve_step setup_dve setup_pe
            xn_ready T_ready xcT_ready proj_ready q_ready k_ready v_ready qb_ready kb_ready bln_ready
            biasf_ready bias_ready a_ready max_ready mparts_ready mT_out mT_ready b_ready e_ready pv_ready rec_ready eps_ready
            o_ready oT_out oT_ready wo_ready xbo_ready x_done
            f_xn f_T f_xT f_mm f_q f_qT f_qTs f_out f_act f_up f_gelu f_down f_acc f_cp f_back f_backT
            f_lg f_copied u_made y_added x_init pool_step route_dve route_pe route_act ffn2_done sp_step""".split()
        S = {n: ctx.enter_context(nc.semaphore(n)) for n in names}

        ATT = [0, 1, 2, 3, 4]
        USES = {n: ATT for n in names}
        USES.update({n: [0, 1, 2, 3] for n in ("xn_ready", "xbo_ready", "ctx_in0", "ctx_in1")})
        USES.update({n: [0, 1, 3] for n in ("bias_ready", "bias_in0", "bias_in1")})
        USES.update({n: [0] for n in ("bln_ready", "biasf_ready")})
        USES.update({n: [0, 1, 2, 4] for n in ("oT_out", "oT_ready", "wo_ready", "rec_ready")})
        USES.update({n: [4] for n in ("u_in0", "u_in1", "y_out0", "y_out1")})
        USES.update({n: [10, 11, 12, 13] for n in ("f_xn", "f_T", "f_xT")})
        USES.update({n: [10, 11] for n in ("f_mm", "f_q", "f_qT", "f_qTs", "f_out")})
        USES.update({n: [11] for n in ("f_act",)})

        def nth(name, s, i, k=1, n=1):
            return (USES[name].index(s) * NB + i) * n + k

        def nth_dma(name, s, t):
            return 16 * (USES[name].index(s) * (NB // 2) + t + 1)

        def bc(ap, n):
            return ap.unsqueeze(1).to_broadcast([ap.shape[0], n, ap.shape[1]])

        def bl(ap, n):
            return ap.unsqueeze(2).to_broadcast([ap.shape[0], ap.shape[1], n])

        def item(I, k):
            t, j = I
            return t + (j + k) // 2, (j + k) % 2

        def num(I):
            return 2 * I[0] + I[1]

        def at(tensor, i):
            if isinstance(i, int):
                return tensor[:, i, :]
            return tensor[:, bass.ds(i, 1), :].rearrange("p a n -> p (a n)")

        def at4(tensor, t):
            return tensor[:, bass.ds(4 * t, 4), :]

        def col(tensor, i):
            return tensor[:, bass.ds(i, 1)]

        def steps(eng, body):
            body((0, 0), False, True, True)
            body((0, 1), True, True, True)
            with eng.Fori(1, NB // 2 - 1) as t:
                for j in range(2):
                    body((t, j), True, True, True)
            body((NB // 2 - 1, 0), True, True, False)
            body((NB // 2 - 1, 1), True, False, False)

        def nkeys(s):
            return P if s == 4 else NC

        block = ctx.enter_context(nc.Block())

        N_CONSTS, N_WEIGHTS = 6, 10

        @block.sync
        def _(sp):
            sp.dma_start(x[:], d["x"].rearrange("b s n -> s b n")).then_inc(S["x_init"], 16)
            sp.dma_start(cpack[:], d["cpack"]).then_inc(S["consts_in"], 16)
            sp.dma_start(xT_all[:, 0:4, :], d["bpack"]).then_inc(S["consts_in"], 16)
            sp.dma_start(xT_all[:, 4:4 + HG, :], d["selpack"]).then_inc(S["consts_in"], 16)
            sp.dma_start(cols[:], d["cols"]).then_inc(S["consts_in"], 16)
            sp.dma_start(dscale[:], d["dscale"].to_broadcast([P, 1])).then_inc(S["consts_in"], 16)
            sp.dma_start(router[:], d["router"]).then_inc(S["consts_in"], 16)
            sp.dma_start(work[:, 0, 0:P], d["L0_w"]).then_inc(S["weights_in"], 16)
            sp.dma_start(work[:, 1, :], d["w1T"]).then_inc(S["weights_in"], 16)
            sp.dma_start(work[:, 2, :].rearrange("p (c n) -> p c n", c=FC), d["w2T"]).then_inc(S["weights_in"], 16)
            for k in range(3):
                sp.dma_start(ex[:, 0, k * FF:(k + 1) * FF],
                             d["convT"][k:k + 1, :].to_broadcast([P, FF])).then_inc(S["weights_in"], 16)
            sp.dma_start(convb[:], d["convb"]).then_inc(S["weights_in"], 16)
            sp.dma_start(b1c[:], d["b1c"]).then_inc(S["weights_in"], 16)
            sp.dma_start(b2c[:], d["b2c"]).then_inc(S["weights_in"], 16)
            sp.dma_start(w1_sb[:], d["L2_W1"].rearrange("e p f -> p e f")).then_inc(S["weights_in"], 16)
            for e in range(NE):
                sp.dma_start(w2_sb[:, e, :, :],
                             d["L2_W2"][e].rearrange("(c p) n -> p c n", p=P)).then_inc(S["moe_w_in"], 16)

            def att_loads(s, I):
                t, j = I
                if s < 4:
                    sp.dma_start(ctx_sb[:, j, :], d["ctx"][bass.ds(num(I), 1)].rearrange("a k n -> (a k) n")
                                 ).then_inc(S[f"ctx_in{j}"], 16)
                if s == 0:
                    sp.dma_start(braw[:, j, :], d["dist"][bass.ds(num(I), 1)].rearrange("a q k -> (a q) k")
                                 ).then_inc(S[f"bias_in{j}"], 16)
                if s == 1:
                    sp.dma_start(braw[:, j, :].bitcast(I32), d["mask1"][bass.ds(num(I), 1)].rearrange("a q k -> (a q) k")
                                 ).then_inc(S[f"bias_in{j}"], 16)
                if s == 3:
                    sp.dma_start(braw_u[:, j, :], d["mask3"][bass.ds(num(I), 1)].rearrange("a q k -> (a q) k")
                                 ).then_inc(S[f"bias_in{j}"], 16)
                if s == 4:
                    for c in range(2):
                        sp.dma_start(xn[c * NB:(c + 1) * NB, j, :],
                                     u_dram[:, bass.ds(2 * num(I) + c, 1), :].rearrange("s a n -> s (a n)")
                                     ).then_inc(S[f"u_in{j}"], 16)

            def attention(s):
                if s:
                    sp.wait_ge(S["stage_go"], GO[s])
                sp.dma_start(wm[:], d["wm"][s].rearrange("m p n -> p m n")).then_inc(S["stage_w_in"], 16)
                sp.dma_start(rows[:], d["rows"][s].unsqueeze(0).to_broadcast([P, 2, P])).then_inc(S["stage_w_in"], 16)
                if s == 4:
                    sp.wait_ge(S["u_out"], 16)
                att_loads(s, (0, 0))
                att_loads(s, (0, 1))

                def body(I, prev, nxt, nxt2):
                    i = num(I)
                    if nxt2:
                        sp.wait_ge(S["T_ready"], nth("T_ready", s, i))
                        sp.sem_inc(S["sp_step"], 1)
                        if s in (0, 1, 3):
                            sp.wait_ge(S["bias_ready"], nth("bias_ready", s, i))
                        sp.sem_inc(S["sp_step"], 1)
                        att_loads(s, item(I, 2))
                    if prev and s == 4:
                        store_y(item(I, -1))

                def store_y(I):
                    sp.wait_ge(S["x_done"], nth("x_done", s, num(I)))
                    sp.sem_inc(S["sp_step"], 1)
                    for c in range(2):
                        sp.dma_start(y_dram[:, bass.ds(2 * num(I) + c, 1), :].rearrange("s a n -> s (a n)"),
                                     y_sb[c * NB:(c + 1) * NB, I[1], :]).then_inc(S[f"y_out{I[1]}"], 16)

                steps(sp, body)
                if s == 4:
                    store_y((NB // 2 - 1, 1))

            for s in range(4):
                if s <= LAST:
                    attention(s)
            if LAST >= 4:
                sp.wait_ge(S["ffn2_done"], 1)
                sp.dma_start(w1_sb[:], d["L3_W1"].rearrange("e p f -> p e f")).then_inc(S["moe_w_in"], 16)
                for e in range(NE):
                    sp.dma_start(w2_sb[:, e, :, :],
                                 d["L3_W2"][e].rearrange("(c p) n -> p c n", p=P)).then_inc(S["moe_w_in"], 16)
                sp.wait_ge(S["stage_go"], GO["ln1"])
                sp.dma_start(rows[:], d["rows"][5].unsqueeze(0).to_broadcast([P, 2, P])).then_inc(S["stage_w_in"], 16)
                sp.wait_ge(S["u_made"], 1)
                sp.dma_start(u_dram.rearrange("s b n -> b s n"), xT_all[:]).then_inc(S["u_out"], 16)
                attention(4)
                for j in range(2):
                    sp.wait_ge(S[f"y_out{j}"], 2 * nth_dma("y_out0", 4, NB // 2 - 1))
                sp.dma_start(rows[:], d["rows"][6].unsqueeze(0).to_broadcast([P, 2, P])).then_inc(S["stage_w_in"], 16)
                sp.dma_start(xT_all[:], y_dram.rearrange("s b n -> b s n")).then_inc(S["y_in"], 16)
            sp.wait_ge(S["stage_go"], GO["end"])
            sp.dma_start(out.rearrange("b s n -> s b n"), x[:]).then_inc(S["out_done"], 16)
            sp.wait_ge(S["out_done"], 16)

        @block.tensor
        def _(pe):
            pe.wait_ge(S["setup_dve"], 1)
            pe.transpose(ps[:, 0, 0:64].bitcast(BF16), workb[:, 0, 0:P], identb[:]).then_inc(S["setup_pe"], 1)
            pe.matmul(ps[:, 1, 0:P], onesf, work[:, 3, 0:P], start=True, stop=True)
            pe.matmul(ps[:, 2, 0:2], onesf, sm[:, 0:2], start=True, stop=True).then_inc(S["setup_pe"], 1)

            def attention(s):
                nk = nkeys(s)
                bias = {0: biasb, 1: biasb, 3: biasb}.get(s)

                def turn(I):
                    t, j = I
                    i = num(I)
                    if s < 4:
                        pe.wait_ge(S["xn_ready"], nth("xn_ready", s, i))
                        pe.wait_ge(S[f"ctx_in{j}"], nth_dma("ctx_in0", s, t))
                    else:
                        pe.wait_ge(S[f"u_in{j}"], 2 * nth_dma("u_in0", s, t))
                    mm = pe.transpose(front[:, 0:P], xn[:, j, :], ident)
                    if s < 4:
                        mm = pe.transpose(front[:, P:P + NC], ctx_sb[:, j, :], ident[0:NC, 0:NC])
                    mm.then_inc(S["T_ready"], 1)

                def front_free(I):
                    pe.wait_ge(S["q_ready"], nth("q_ready", s, num(I)))
                    pe.wait_ge(S["v_ready"], nth("v_ready", s, num(I)))

                def project(I):
                    t, j = I
                    src = xcT[:, j, 0:P] if s == 4 else xcT[:, j, P:P + NC]
                    pe.wait_ge(S["xcT_ready"], nth("xcT_ready", s, num(I)))
                    pe.matmul(front[:, 0:P], wm[:, 0, :], xcT[:, j, 0:P], start=True, stop=True)
                    pe.matmul(front[:, P:P + nk], wm[:, 1, :], src, start=True, stop=True)
                    pe.matmul(front[0:nk, 2 * P:3 * P], src, wm[:, 2, :], start=True, stop=True
                              ).then_inc(S["proj_ready"], 1)

                def scores_by_query(I, first):
                    t, j = I
                    i = num(I)
                    pe.wait_ge(S["qb_ready"], nth("qb_ready", s, i))
                    pe.wait_ge(S["kb_ready"], nth("kb_ready", s, i))
                    if bias is not None:
                        pe.wait_ge(S["bias_ready"], nth("bias_ready", s, i))
                    b = biasb[:, j, 0:nk] if bias is not None else causalb[:, (0 if s == 2 else 1), 0:nk]
                    for g in range(NG):
                        if not (first and g < 2):
                            pe.wait_ge(S["max_ready"], nth("max_ready", s, i, g - 1, NG))
                        pe.matmul(a_ps[g % 2][:, 0:HG * nk], identb[:], bc(b, HG), start=True, stop=False)
                        pe.matmul(a_ps[g % 2][:, 0:HG * nk], qb[32 * g:32 * g + 32, j, :],
                                  kb[32 * g:32 * g + 32, j, 0:HG * nk], start=False, stop=True
                                  ).then_inc(S["a_ready"], 1)

                def turn_max(I):
                    t, j = I
                    pe.wait_ge(S["mparts_ready"], nth("mparts_ready", s, num(I), 2, 2))
                    pe.transpose(mT_ps, mparts[:, j, :, :].rearrange("p g r -> p (g r)"), identb[:]).then_inc(S["mT_out"], 1)

                def scores_by_key(I, first):
                    t, j = I
                    i = num(I)
                    pe.wait_ge(S["mT_ready"], nth("mT_ready", s, i))
                    if s == 0:
                        pe.wait_ge(S["biasf_ready"], nth("biasf_ready", s, i))
                    for c in range(2):
                        if not first:
                            pe.wait_ge(S["e_ready"], nth("e_ready", s, i - 1, c + 1, 2))
                        for g in range(2 * c, 2 * c + 2):
                            o = b_ps[c][0:nk, (g % 2) * 512:(g % 2) * 512 + 512]
                            if s == 0:
                                pe.matmul(o, biasf[:, j, 0:nk], bc(ident, HG), start=True, stop=False,
                                          skip_group_check=True)
                            else:
                                b = biasb[:, j, 0:nk] if bias is not None else causalb[:, (0 if s == 2 else 1), 0:nk]
                                pe.matmul(o, b, bc(identb[:], HG), start=True, stop=False,
                                          skip_group_check=True)
                            for k in range(HG):
                                pe.matmul(o[:, k * P:(k + 1) * P], kblk[32 * g:32 * g + 32, j, k * nk:(k + 1) * nk],
                                          qf[32 * g:32 * g + 32, j, :], start=False, stop=False,
                                          skip_group_check=True)
                            for k in range(HG):
                                mm = pe.matmul(o[:, k * P:(k + 1) * P], selb[32 * g:32 * g + 32, k, 0:nk], mT[32 * g:32 * g + 32, j, :],
                                               start=False, stop=True, skip_group_check=True)
                        mm.then_inc(S["b_ready"], 1)

                def values(I, first):
                    t, j = I
                    i = num(I)
                    pe.wait_ge(S["e_ready"], nth("e_ready", s, i, 2, 2))
                    if not first:
                        pe.wait_ge(S["x_done"], nth("x_done", s, i - 1))
                    for h in range(NH):
                        mm = pe.matmul(back[:, h * 9:h * 9 + 9], ex[0:nk, j, h * P:(h + 1) * P],
                                       vaug[0:nk, j, h, :], start=True, stop=True)
                    mm.then_inc(S["pv_ready"], 1)

                def turn_out(I):
                    if s == 3:
                        return
                    t, j = I
                    pe.wait_ge(S["o_ready"], nth("o_ready", s, num(I)))
                    pe.transpose(back[:, 144:144 + P], o_sb[:, j, :], ident).then_inc(S["oT_out"], 1)

                def project_out(I):
                    if s == 3:
                        return
                    t, j = I
                    pe.wait_ge(S["oT_ready"], nth("oT_ready", s, num(I)))
                    pe.matmul(back[:, 272:272 + P], oT[:, j, :], wm[:, 3, :], start=True, stop=True
                              ).then_inc(S["wo_ready"], 1)

                def body(I, prev, nxt, nxt2):
                    if nxt:
                        front_free(I)
                        turn(item(I, 1))
                    if prev:
                        values(item(I, -1), num(I) == 1 if isinstance(I[0], int) else False)
                    turn_max(I)
                    if nxt:
                        project(item(I, 1))
                    scores_by_key(I, not prev)
                    if prev:
                        turn_out(item(I, -1))
                    if nxt:
                        scores_by_query(item(I, 1), False)
                    if prev:
                        project_out(item(I, -1))

                pe.wait_ge(S["stage_go"], GO[s])
                pe.wait_ge(S["stage_w_in"], W_IN[s])
                turn((0, 0))
                project((0, 0))
                scores_by_query((0, 0), True)
                steps(pe, body)
                end = (NB // 2 - 1, 1)
                values(end, False)
                turn_out(end)
                project_out(end)

            def wait4(name, s, t, j, back_by=0):
                pe.wait_ge(S[name], nth(name, s, 4 * t + j - back_by))

            def hadamard_ffn():
                pe.wait_ge(S["stage_go"], GO[10])
                with pe.Fori(0, NB // 4) as t:
                    for j in range(4):
                        wait4("f_xn", 10, t, j)
                        pe.transpose(ps[:, j, 0:P], xn[:, j, :], ident).then_inc(S["f_T"], 1)
                    for j in range(4):
                        wait4("f_xT", 10, t, j)
                        pe.matmul(ps[:, j, P:2 * P], work[:, j, 0:P], hada, start=True, stop=True
                                  ).then_inc(S["f_mm"], 1)
                    for j in range(4):
                        wait4("f_q", 10, t, j)
                        pe.transpose(ps[:, j, 256:320].bitcast(BF16), workb[:, j, 0:P], identb[:]
                                     ).then_inc(S["f_qT"], 1)
                    for j in range(4):
                        wait4("f_qTs", 10, t, j)
                        pe.matmul(ps[:, j, 384:512], qT[:, j, 0:P], ternT[:], start=True, stop=True
                                  ).then_inc(S["f_out"], 1)

            def conv_ffn():
                pe.wait_ge(S["stage_go"], GO[11])
                with pe.Fori(0, NB // 4) as t:
                    for j in range(4):
                        wait4("f_xn", 11, t, j)
                        pe.transpose(ps[:, j, 0:P], xn[:, j, :], ident).then_inc(S["f_T"], 1)
                    for j in range(4):
                        wait4("f_xT", 11, t, j)
                        pe.matmul(ps[:, j, :], onesf[0:1, :], convb[:], start=True, stop=False)
                        for k in range(3):
                            mm = pe.matmul(ps[:, j, :], xqT[:, j, k:k + P], wconv[:, k, :],
                                           start=False, stop=k == 2)
                        mm.then_inc(S["f_mm"], 1)
                    for j in range(4):
                        wait4("f_q", 11, t, j)
                        for c in range(FC):
                            mm = pe.transpose(ps[:, j, 64 * c:64 * c + 64].bitcast(BF16),
                                              workb[:, j, c * P:(c + 1) * P], identb[:])
                        mm.then_inc(S["f_qT"], 1)
                    for j in range(4):
                        wait4("f_qTs", 11, t, j)
                        for c in range(FC):
                            mm = pe.matmul(ps[:, j, 384:512], qT[:, j, c * P:(c + 1) * P], w2q[:, c, :],
                                           start=c == 0, stop=c == FC - 1)
                        mm.then_inc(S["f_out"], 1)

            def turn_all(s):
                with pe.Fori(0, NB // 4) as t:
                    for j in range(4):
                        wait4("f_xn", s, t, j)
                        wait4("f_xT", s, t, j, 4)
                        pe.transpose(ps[:, j, 0:P], xn[:, j, :], ident).then_inc(S["f_T"], 1)

            def expert_ffn():
                pe.wait_ge(S["stage_go"], GO[12])
                turn_all(12)
                pe.wait_ge(S["f_xT"], nth("f_xT", 12, NB - 1))
                pe.wait_ge(S["moe_w_in"], 16 * NE)
                units = [(e, half) for e in range(NE) for half in range(2)]

                def up(u):
                    e, half = units[u]
                    rhs = xT_all[:, half * 32:half * 32 + 32, e * 16:e * 16 + 16]
                    for c in range(FC):
                        if u:
                            pe.wait_ge(S["f_gelu"], (u - 1) * FC + c + 1)
                        pe.matmul(ps[:, c, :], w1_sb[:, e, c * P:(c + 1) * P], rhs, start=True, stop=True
                                  ).then_inc(S["f_up"], 1)

                def down(u):
                    e, half = units[u]
                    if u >= 2:
                        pe.wait_ge(S["f_acc"], u - 1)
                    for c in range(FC):
                        pe.wait_ge(S["f_gelu"], u * FC + c + 1)
                        mm = pe.matmul(ps[:, 4 + u % 2, :], w2_sb[:, e, c, :], hid[:, u % 2, c, :],
                                       start=c == 0, stop=c == FC - 1)
                    mm.then_inc(S["f_down"], 1)

                up(0)
                for u in range(len(units)):
                    if u + 1 < len(units):
                        up(u + 1)
                    down(u)
                with pe.Fori(0, NB // 4) as t:
                    for j in range(4):
                        pe.wait_ge(S["f_cp"], 4 * t + j + 1)
                        pe.transpose(ps[:, j, 0:P], work[:, j, 0:P], ident).then_inc(S["f_backT"], 1)

            def moe():
                turn_all_moe()
                pe.wait_ge(S["route_dve"], 1)
                pe.matmul(ps[:, 0, :], trib[:], selbf, start=True, stop=True)
                pe.matmul(ps[:, 1, :], onesb[:], selbf, start=True, stop=True).then_inc(S["route_pe"], 1)
                pe.wait_ge(S["route_dve"], 2)
                pe.wait_ge(S["moe_w_in"], 16 * (2 * NE + 1))

                def up(t, e):
                    rhs = at4(xT_all, t).rearrange("p a n -> p (a n)")
                    n = t * (NE * FC) + e * FC
                    for c in range(FC):
                        pe.wait_ge(S["f_gelu"], G0 + n + c + 1 - FC)
                        pe.matmul(ps[:, c, :], w1_sb[:, e, c * P:(c + 1) * P], rhs, start=True, stop=True
                                  ).then_inc(S["f_up"], 1)

                def down(t, e):
                    n = t * NE + e
                    pe.wait_ge(S["f_acc"], G0 // FC + n - 1)
                    pe.wait_ge(S["f_gelu"], G0 + (n + 1) * FC)
                    for r in range(4):
                        for c in range(FC):
                            mm = pe.matmul(ps[:, 4 + e % 2, r * P:(r + 1) * P], hid[:, e % 2, c, r * P:(r + 1) * P],
                                           w2_sb[:, e, c, :], start=c == 0, stop=c == FC - 1)
                    mm.then_inc(S["f_down"], 1)

                with pe.Fori(0, NB // 4) as t:
                    up(t, 0)
                    for e in range(NE):
                        if e + 1 < NE:
                            up(t, e + 1)
                        down(t, e)

            def turn_all_moe():
                with pe.Fori(0, NB // 4) as t:
                    for j in range(4):
                        wait4("f_xn", 13, t, j)
                        wait4("f_xT", 13, t, j, 4)
                        pe.transpose(ps[:, j, 0:P], xn[:, j, :], ident).then_inc(S["f_T"], 1)
                    for j in range(4):
                        wait4("f_xT", 13, t, j)
                        pe.matmul(ps[:, 7, bass.ds((4 * t + j) * NE, NE)], work[:, j, 0:P], router[:],
                                  start=True, stop=True).then_inc(S["f_lg"], 1)

            if LAST >= 0:
                attention(0)
            if LAST >= 0.5:
                hadamard_ffn()
            if LAST >= 1:
                attention(1)
            if LAST >= 1.5:
                conv_ffn()
            if LAST >= 2:
                attention(2)
            if LAST >= 2.5:
                expert_ffn()
            if LAST >= 3:
                attention(3)
            if LAST >= 4:
                attention(4)
                moe()

        @block.scalar
        def _(act):
            def sqrt_stats(n):
                act.wait_ge(S["sq_in"], n)
                act.activation(t1[:], t1[:], ACT.Sqrt).then_inc(S["sq_out"], 1)

            def attention(s):
                nk = nkeys(s)

                def copy_turned(I):
                    t, j = I
                    act.wait_ge(S["T_ready"], nth("T_ready", s, num(I)))
                    w = P if s == 4 else P + NC
                    act.copy(xcT[:, j, 0:w], front[:, 0:w]).then_inc(S["xcT_ready"], 1)

                def scale_q(I):
                    t, j = I
                    act.wait_ge(S["proj_ready"], nth("proj_ready", s, num(I)))
                    act.activation(qf[:, j, :], front[:, 0:P], ACT.Identity, bias=cols[:, 2 * s:2 * s + 1],
                                   scale=QSCALE[s]).then_inc(S["q_ready"], 1)

                def log_dist(I):
                    t, j = I
                    if s == 0:
                        act.wait_ge(S[f"bias_in{j}"], nth_dma("bias_in0", s, t))
                        act.activation(bln[:, j, :], braw[:, j, :], ACT.Ln, bias=sm[:, 11:12]
                                       ).then_inc(S["bln_ready"], 1)

                def copy_max(I):
                    t, j = I
                    act.wait_ge(S["mT_out"], nth("mT_out", s, num(I)))
                    act.copy(mT[:, j, :], mT_ps).then_inc(S["mT_ready"], 1)

                def exps(I):
                    t, j = I
                    for c in range(2):
                        act.wait_ge(S["b_ready"], nth("b_ready", s, num(I), c + 1, 2))
                        act.activation(ex[0:nk, j, c * 1024:(c + 1) * 1024], b_ps[c][0:nk, :], ACT.Exp
                                       ).then_inc(S["e_ready"], 1)

                def copy_out(I):
                    t, j = I
                    if s == 3:
                        return
                    act.wait_ge(S["oT_out"], nth("oT_out", s, num(I)))
                    act.copy(oT[:, j, :], back[:, 144:144 + P]).then_inc(S["oT_ready"], 1)

                def body(I, prev, nxt, nxt2):
                    if nxt:
                        if s == 0 and prev:
                            act.wait_ge(S["biasf_ready"], nth("biasf_ready", s, num(I) - 1))
                        log_dist(item(I, 1))
                        copy_turned(item(I, 1))
                    copy_max(I)
                    if nxt:
                        scale_q(item(I, 1))
                    exps(I)
                    if prev:
                        copy_out(item(I, -1))

                act.wait_ge(S["stage_go"], GO[s])
                log_dist((0, 0))
                copy_turned((0, 0))
                scale_q((0, 0))
                steps(act, body)
                copy_out((NB // 2 - 1, 1))

            def turned(s, dst, pad=0):
                def f(t):
                    for j in range(4):
                        act.wait_ge(S["f_T"], nth("f_T", s, 4 * t + j))
                        act.copy(dst(t, j), ps[:, j, 0:P]).then_inc(S["f_xT"], 1)
                return f

            def quant_turned(s, t, w):
                for j in range(4):
                    act.wait_ge(S["f_qT"], nth("f_qT", s, 4 * t + j))
                    act.copy(qT[:, j, 0:w], ps[:, j, 0 if w == FF else 256:][:, 0:w // 2].bitcast(BF16)
                             ).then_inc(S["f_qTs"], 1)

            def hadamard_ffn():
                act.wait_ge(S["stage_go"], GO[10])
                copy = turned(10, lambda t, j: work[:, j, 0:P])
                with act.Fori(0, NB // 4) as t:
                    copy(t)
                    quant_turned(10, t, P)

            def conv_ffn():
                act.wait_ge(S["stage_go"], GO[11])
                copy = turned(11, lambda t, j: xqT[:, j, 1:1 + P])
                with act.Fori(0, NB // 4) as t:
                    copy(t)
                    for j in range(4):
                        act.wait_ge(S["f_mm"], nth("f_mm", 11, 4 * t + j))
                        act.activation(work[:, j, :], ps[:, j, :], ACT.Silu).then_inc(S["f_act"], 1)
                    quant_turned(11, t, FF)

            def expert_ffn():
                act.wait_ge(S["stage_go"], GO[12])
                copy = turned(12, lambda t, j: at(xT_all, 4 * t + j))
                with act.Fori(0, NB // 4) as t:
                    copy(t)
                for u in range(2 * NE):
                    if u >= 2:
                        act.wait_ge(S["f_down"], u - 1)
                    for c in range(FC):
                        act.wait_ge(S["f_up"], u * FC + c + 1)
                        act.activation(hid[:, u % 2, c, :], ps[:, c, :], ACT.Gelu_apprx_tanh,
                                       bias=b1c[:, u // 2, c:c + 1]).then_inc(S["f_gelu"], 1)

            def moe():
                copy = turned(13, lambda t, j: work[:, j, 0:P])
                with act.Fori(0, NB // 4) as t:
                    act.wait_ge(S["f_copied"], 4 * t + 4)
                    copy(t)
                act.wait_ge(S["route_act"], 1)
                act.activation(t2[:], t2[:], ACT.Exp).then_inc(S["route_act"], 1)
                with act.Fori(0, NB // 4) as t:
                    for e in range(NE):
                        n = t * NE + e
                        act.wait_ge(S["f_down"], G0 // FC + n - 1)
                        for c in range(FC):
                            act.wait_ge(S["f_up"], G0 + n * FC + c + 1)
                            act.activation(hid[:, e % 2, c, :], ps[:, c, :], ACT.Gelu).then_inc(S["f_gelu"], 1)

            sqrt_stats(1)
            if LAST >= 0:
                attention(0)
                sqrt_stats(2)
            if LAST >= 0.5:
                hadamard_ffn()
                sqrt_stats(3)
            if LAST >= 1:
                attention(1)
                sqrt_stats(4)
            if LAST >= 1.5:
                conv_ffn()
                sqrt_stats(5)
            if LAST >= 2:
                attention(2)
                sqrt_stats(6)
            if LAST >= 2.5:
                expert_ffn()
                sqrt_stats(7)
            if LAST >= 3:
                attention(3)
                sqrt_stats(8)
            if LAST >= 4:
                sqrt_stats(9)
                attention(4)
                sqrt_stats(10)
                moe()

        @block.vector
        def _(dve):
            chain = [0]

            def link(ins):
                chain[0] += 1
                ins.then_inc(S["dve_step"], 1)
                dve.wait_ge(S["dve_step"], chain[0])

            class Loop:
                def __init__(self, times, per):
                    self.times, self.per, self.base = times, per, chain[0]
                    chain[0] += times * per

                def turn(self, t):
                    self.t, self.k = t, 0

                def mark(self, ins):
                    self.k += 1
                    ins.then_inc(S["dve_step"], 1)

                def hold(self):
                    dve.wait_ge(S["dve_step"], self.base + self.t * self.per + self.k)

                def end(self):
                    assert self.k == self.per, (self.k, self.per)

            go = [0]

            def let_go(ins):
                go[0] += 1
                ins.then_inc(S["stage_go"], 1)

            def finish_stats(n):
                me, mo, ve, vo = stats[:, :, 1], stats[:, :, 4], stats[:, :, 2], stats[:, :, 5]
                link(dve.tensor_tensor(t1[:], ve, vo, ALU.add))
                link(dve.tensor_tensor(t2[:], me, mo, ALU.subtract))
                link(dve.tensor_tensor(t2[:], t2[:], t2[:], ALU.mult))
                link(dve.tensor_scalar(t1[:], t1[:], 1.0 / P, EPS, ALU.mult, ALU.add))
                link(dve.scalar_tensor_tensor(t1[:], t2[:], 0.25, t1[:], ALU.mult, ALU.add))
                dve.tensor_tensor(t2[:], me, mo, ALU.add).then_inc(S["sq_in"], 1)
                dve.wait_ge(S["sq_in"], n)
                dve.wait_ge(S["sq_out"], n)
                link(dve.reciprocal(rstd[:], t1[:]))
                ins = dve.scalar_tensor_tensor(nmr[:], t2[:], -0.5, rstd[:], ALU.mult, ALU.mult)
                link_go(ins)

            def link_go(ins):
                go[0] += 1
                ins.then_inc(S["stage_go"], 1)
                dve.wait_ge(S["stage_go"], go[0])

            def normalise(dst, i, src=x):
                return dve.tensor_scalar(dst, at(src, i), col(rstd, i), col(nmr, i), ALU.mult, ALU.add)

            def bn(i, src=x):
                o = stats[:, i, :] if isinstance(i, int) else stats[:, bass.ds(i, 1), :].rearrange("p a n -> p (a n)")
                return dve.bn_stats(o, at(src, i))

            def all_stats(src):
                with dve.Fori(0, NB) as t:
                    bn(t, src).then_inc(S["dve_step"], 1)
                chain[0] += NB
                dve.wait_ge(S["dve_step"], chain[0])

            dve.wait_ge(S["consts_in"], 16 * N_CONSTS)
            link(dve.tensor_copy(identb[:], cpack[:, 0:P]))
            dve.tensor_copy(causalb[:], xT_all[:, 0:2, :])
            dve.tensor_copy(trib[:], xT_all[:, 2, :])
            dve.tensor_copy(onesb[:], xT_all[:, 3, :])
            dve.tensor_copy(selb[:], xT_all[:, 4:4 + HG, :])
            dve.memset(mparts[:], 0.0)
            dve.memset(vaug[:], 1.0)
            dve.memset(xqT[:], 0.0)
            dve.memset(sm[:, 11:12], 1e-9)
            for s in range(5):
                dve.tensor_scalar(cols[:, 2 * s:2 * s + 1], cols[:, 2 * s:2 * s + 1], QSCALE[s], None, ALU.mult)
            link(dve.scalar_tensor_tensor(dscale[:], dscale[:], -1.0, dscale[:], ALU.mult, ALU.min))
            dve.wait_ge(S["weights_in"], 16 * N_WEIGHTS)
            w0, w1, w2 = work[:, 0, 0:P], work[:, 1, :], work[:, 2, :]
            dve.tensor_reduce(sm[:, 0:1], w1, AX.X, ALU.add, apply_absolute_value=True)
            dve.tensor_reduce(sm[:, 1:2], w2, AX.X, ALU.add, apply_absolute_value=True)
            link(dve.tensor_reduce(sm[:, 2:3], w0, AX.X, ALU.add, apply_absolute_value=True))
            link(dve.tensor_scalar(sm[:, 2:3], sm[:, 2:3], 1.0 / P, 1e-5, ALU.mult, ALU.max))
            link(dve.reciprocal(sm[:, 3:4], sm[:, 2:3]))
            dve.tensor_scalar(work[:, 3, 0:P], ident, sm[:, 2:3], None, ALU.mult)
            link(dve.tensor_scalar(work[:, 3, P:2 * P], w0, sm[:, 3:4], 0.5, ALU.mult, ALU.is_gt))
            link(dve.tensor_scalar(work[:, 3, 2 * P:3 * P], w0, sm[:, 3:4], -0.5, ALU.mult, ALU.is_lt))
            dve.tensor_tensor(workb[:, 0, 0:P], work[:, 3, P:2 * P], work[:, 3, 2 * P:3 * P], ALU.subtract
                              ).then_inc(S["setup_dve"], 1)
            dve.wait_ge(S["setup_pe"], 2)
            dve.tensor_copy(ternT[:], ps[:, 0, 0:64].bitcast(BF16))
            dve.tensor_copy(wscale[:], ps[:, 1, 0:P])
            link(dve.tensor_scalar(sm[:, 4:6], ps[:, 2, 0:2], 1.0 / (P * FF), 1e-5, ALU.mult, ALU.max))
            link(dve.reciprocal(sm[:, 6:8], sm[:, 4:6]))
            for k, w in ((0, w1), (1, w2)):
                link(dve.tensor_scalar(w, w, sm[:, 6 + k:7 + k], ROUND, ALU.mult, ALU.add))
                link(dve.tensor_scalar(w, w, -ROUND, -1.0, ALU.add, ALU.max))
            link(dve.tensor_scalar(w1, w1, 1.0, sm[:, 4:5], ALU.min, ALU.mult))
            link(dve.tensor_scalar(w2q[:].rearrange("p c n -> p (c n)"), w2, 1.0, None, ALU.min))
            for k in range(3):
                link(dve.tensor_tensor(wconv[:, k, :], w1, ex[:, 0, k * FF:(k + 1) * FF], ALU.mult))
            dve.wait_ge(S["x_init"], 16)
            all_stats(x)
            finish_stats(1)

            def attention(s):
                nk = nkeys(s)

                def norm_in(I, wait):
                    t, j = I
                    if s == 4:
                        return
                    if wait:
                        dve.wait_ge(S["T_ready"], nth("T_ready", s, num(I) - 2))
                    normalise(xn[:, j, :], num(I)).then_inc(S["xn_ready"], 1)

                def keys_values(I):
                    t, j = I
                    dve.wait_ge(S["q_ready"], nth("q_ready", s, num(I)))
                    dve.wait_ge(S["proj_ready"], nth("proj_ready", s, num(I)))
                    dve.scalar_tensor_tensor(
                        kblk[:, j, 0:HG * nk].rearrange("p (a n) -> p a n", a=HG), bc(front[:, P:P + nk], HG),
                        cols[:, 2 * s + 1:2 * s + 2], bl(headmask, nk), ALU.add, ALU.mult
                    ).then_inc(S["k_ready"], 1)
                    dve.tensor_tensor(
                        vaug[0:nk, j, :, 0:DH], front[0:nk, 2 * P:3 * P].rearrange("p (h e) -> p h e", e=DH),
                        rows[0:nk, 0, :].rearrange("p (h e) -> p h e", e=DH), ALU.add).then_inc(S["v_ready"], 1)

                def maxima(I):
                    t, j = I
                    i = num(I)
                    for g in range(NG):
                        dve.wait_ge(S["a_ready"], nth("a_ready", s, i, g + 1, NG))
                        dve.tensor_reduce(negmax[:, j, HG * g:HG * g + HG],
                                          a_ps[g % 2][:, 0:HG * nk].rearrange("p (a n) -> p a n", a=HG),
                                          AX.X, ALU.max, negate=True).then_inc(S["max_ready"], 1)
                    dve.wait_ge(S["max_ready"], nth("max_ready", s, i, NG, NG))
                    high, low = mparts[:, j, :, 0:HG], mparts[:, j, :, HG:2 * HG]
                    whole = negmax[:, j, :].rearrange("p (g k) -> p g k", k=HG)
                    dve.tensor_copy(high, whole).then_inc(S["mparts_ready"], 1)
                    dve.wait_ge(S["mparts_ready"], nth("mparts_ready", s, i, 1, 2))
                    dve.tensor_tensor(low, whole, high, ALU.subtract
                                      ).then_inc(S["mparts_ready"], 1)

                def divide(I):
                    t, j = I
                    i = num(I)
                    pv = back[:, 0:NH * 9].rearrange("p (h e) -> p h e", e=9)
                    dve.wait_ge(S["pv_ready"], nth("pv_ready", s, i))
                    if s == 3:
                        dve.tensor_scalar(rec[:, j, :], pv[:, :, 8], 1e-6, None, ALU.add).then_inc(S["eps_ready"], 1)
                        dve.wait_ge(S["eps_ready"], nth_o(i, 1))
                        dve.reciprocal(rec[:, j, :], rec[:, j, :]).then_inc(S["eps_ready"], 1)
                        dve.wait_ge(S["eps_ready"], nth_o(i, 2))
                        dve.scalar_tensor_tensor(rec[:, j, :], negmax[:, j, :], -MASKED / 2, rec[:, j, :],
                                                 ALU.is_lt, ALU.mult).then_inc(S["eps_ready"], 1)
                        dve.wait_ge(S["eps_ready"], nth_o(i, 3))
                    else:
                        dve.reciprocal(rec[:, j, :], pv[:, :, 8]).then_inc(S["rec_ready"], 1)
                        dve.wait_ge(S["rec_ready"], nth("rec_ready", s, i))
                    dve.tensor_tensor(o_sb[:, j, :].rearrange("p (h e) -> p h e", e=DH), pv[:, :, 0:DH],
                                      bl(rec[:, j, :], DH), ALU.mult).then_inc(S["o_ready"], 1)

                def nth_o(i, k):
                    return i * 3 + k

                def add_out(I):
                    t, j = I
                    i = num(I)
                    if s == 3:
                        dve.wait_ge(S["o_ready"], nth("o_ready", s, i))
                        ins = dve.tensor_tensor(at(x, i), o_sb[:, j, :], at(x, i), ALU.add)
                    elif s < 3:
                        dve.wait_ge(S["wo_ready"], nth("wo_ready", s, i))
                        dve.wait_ge(S["xbo_ready"], nth("xbo_ready", s, i))
                        ins = dve.tensor_tensor(at(x, i), back[:, 272:272 + P], at(x, i), ALU.add)
                    else:
                        dve.wait_ge(S["wo_ready"], nth("wo_ready", s, i))
                        ins = dve.tensor_copy(y_sb[:, j, :], back[:, 272:272 + P])
                    ins.then_inc(S["x_done"], 1)

                def new_stats(I):
                    i = num(I)
                    if s < 4:
                        dve.wait_ge(S["x_done"], nth("x_done", s, i))
                        bn(i).then_inc(S["dve_step"], 1)

                def body(I, prev, nxt, nxt2):
                    t, j = I
                    if prev:
                        divide(item(I, -1))
                    if nxt:
                        keys_values(item(I, 1))
                    if nxt2:
                        norm_in(item(I, 2), True)
                    if nxt:
                        maxima(item(I, 1))
                    if prev:
                        p = item(I, -1)
                        if s == 4 and not (isinstance(p[0], int) and p[0] == 0):
                            dve.wait_ge(S[f"y_out{p[1]}"], 2 * nth_dma("y_out0", 4, p[0] - 1))
                        add_out(p)
                        new_stats(p)

                dve.wait_ge(S["stage_w_in"], W_IN[s])
                norm_in((0, 0), False)
                norm_in((0, 1), False)
                keys_values((0, 0))
                maxima((0, 0))
                steps(dve, body)
                end = (NB // 2 - 1, 1)
                divide(end)
                if s == 4:
                    dve.wait_ge(S["y_out1"], 2 * nth_dma("y_out0", 4, NB // 2 - 2))
                add_out(end)
                new_stats(end)
                if s < 4:
                    chain[0] += NB
                    dve.wait_ge(S["dve_step"], chain[0])

            def quantise(L, t, src, scs, lo, hi, dst, s, dequant=False):
                w = src(0).shape[1]
                tmp = lambda j: work[:, j, 0:w] if not dequant else xn[:, j, :]
                for j in range(4):
                    L.mark(dve.tensor_reduce(sc[:, j, 0:1], src(j), AX.X, ALU.max, apply_absolute_value=True))
                L.hold()
                for j in range(4):
                    L.mark(dve.tensor_scalar(sc[:, j, 1:2], sc[:, j, 0:1], 1e-5, 1.0 / hi, ALU.max, ALU.mult))
                L.hold()
                for j in range(4):
                    L.mark(dve.reciprocal(sc[:, j, 2:3], sc[:, j, 1:2]))
                L.hold()
                for j in range(4):
                    L.mark(dve.tensor_scalar(tmp(j), src(j), sc[:, j, 2:3], ROUND, ALU.mult, ALU.add))
                L.hold()
                for j in range(4):
                    L.mark(dve.tensor_scalar(tmp(j), tmp(j), -ROUND, lo, ALU.add, ALU.max))
                L.hold()
                for j in range(4):
                    if dequant:
                        dve.tensor_scalar(dst(j), tmp(j), hi, sc[:, j, 1:2], ALU.min, ALU.mult
                                          ).then_inc(S["f_xn"], 1)
                    else:
                        dve.tensor_scalar(dst(j), tmp(j), hi, None, ALU.min).then_inc(S["f_q"], 1)

            def hadamard_ffn():
                L = Loop(NB // 4, 4 * 5 + 4 + 4 + 4)
                with dve.Fori(0, NB // 4) as t:
                    L.turn(t)
                    for j in range(4):
                        normalise(xn[:, j, :], 4 * t + j).then_inc(S["f_xn"], 1)
                    dve.wait_ge(S["f_mm"], nth("f_mm", 10, 4 * t + 3))
                    quantise(L, t, lambda j: ps[:, j, P:2 * P], None, -8.0, 7.0,
                             lambda j: workb[:, j, 0:P], 10)
                    for j in range(4):
                        dve.wait_ge(S["f_out"], nth("f_out", 10, 4 * t + j))
                        L.mark(dve.scalar_tensor_tensor(work[:, j, P:2 * P], ps[:, j, 384:512], sc[:, j, 1:2],
                                                        wscale[:], ALU.mult, ALU.mult))
                    L.hold()
                    for j in range(4):
                        L.mark(dve.tensor_tensor(at(x, 4 * t + j), work[:, j, P:2 * P], at(x, 4 * t + j), ALU.add))
                    L.hold()
                    for j in range(4):
                        L.mark(bn(4 * t + j))
                    L.end()
                dve.wait_ge(S["dve_step"], chain[0])

            def conv_ffn():
                L = Loop(NB // 4, 4 + 2 * 4 * 5 + 4 + 4 + 4)
                with dve.Fori(0, NB // 4) as t:
                    L.turn(t)
                    for j in range(4):
                        L.mark(normalise(work[:, j, 0:P], 4 * t + j))
                    L.hold()
                    quantise(L, t, lambda j: work[:, j, 0:P], None, -128.0, 127.0,
                             lambda j: xn[:, j, :], 11, dequant=True)
                    dve.wait_ge(S["f_act"], nth("f_act", 11, 4 * t + 3))
                    quantise(L, t, lambda j: work[:, j, :], None, -128.0, 127.0,
                             lambda j: workb[:, j, :], 11)
                    for j in range(4):
                        L.mark(dve.tensor_scalar(sc[:, j, 3:4], sc[:, j, 1:2], sm[:, 5:6], None, ALU.mult))
                    L.hold()
                    for j in range(4):
                        dve.wait_ge(S["f_out"], nth("f_out", 11, 4 * t + j))
                        L.mark(dve.scalar_tensor_tensor(at(x, 4 * t + j), ps[:, j, 384:512], sc[:, j, 3:4],
                                                        at(x, 4 * t + j), ALU.mult, ALU.add))
                    L.hold()
                    for j in range(4):
                        L.mark(bn(4 * t + j))
                    L.end()
                dve.wait_ge(S["dve_step"], chain[0])

            def expert_ffn():
                with dve.Fori(0, NB // 4) as t:
                    for j in range(4):
                        dve.wait_ge(S["f_T"], nth("f_T", 12, 4 * t + j - 4))
                        normalise(xn[:, j, :], 4 * t + j).then_inc(S["f_xn"], 1)
                for u in range(2 * NE):
                    e, half = u // 2, u % 2
                    dve.wait_ge(S["f_down"], u + 1)
                    dve.tensor_scalar(h_all[:, half * 32:half * 32 + 32, e * 16:e * 16 + 16],
                                      ps[:, 4 + u % 2, :].rearrange("p (b n) -> p b n", n=16),
                                      b2c[:, e:e + 1], None, ALU.add).then_inc(S["f_acc"], 1)
                L = Loop(NB // 4, 8)
                with dve.Fori(0, NB // 4) as t:
                    L.turn(t)
                    for j in range(4):
                        dve.wait_ge(S["f_backT"], 4 * t + j + 1)
                        L.mark(dve.tensor_tensor(at(x, 4 * t + j), ps[:, j, 0:P], at(x, 4 * t + j), ALU.add))
                    L.hold()
                    dve.sem_inc(S["f_back"], 4)
                    for j in range(4):
                        L.mark(bn(4 * t + j))
                    L.end()
                dve.wait_ge(S["dve_step"], chain[0])

            def wide(fn):
                with dve.Fori(0, NB // 4) as t:
                    fn(t).then_inc(S["dve_step"], 1)
                chain[0] += NB // 4
                dve.wait_ge(S["dve_step"], chain[0])

            def hidden_in():
                with dve.Fori(0, NB) as t:
                    normalise(at(h_all, t), t).then_inc(S["dve_step"], 1)
                chain[0] += NB
                dve.wait_ge(S["dve_step"], chain[0])
                all_stats(h_all)
                finish_stats(9)
                with dve.Fori(0, NB) as t:
                    normalise(at(xT_all, t), t, h_all).then_inc(S["dve_step"], 1)
                chain[0] += NB
                dve.wait_ge(S["dve_step"], chain[0])
                dve.wait_ge(S["stage_w_in"], W_IN["ln1"])
                wide(lambda t: dve.tensor_tensor(at4(xT_all, t), at4(xT_all, t), bc(rows[:, 0, :], 4), ALU.mult))
                wide(lambda t: dve.tensor_tensor(at4(xT_all, t), at4(xT_all, t), bc(rows[:, 1, :], 4), ALU.add))
                ins = dve.memset(sm[:, 10:11], 0.0)
                ins.then_inc(S["u_made"], 1)
                dve.wait_ge(S["u_made"], 1)
                link_go(dve.memset(sm[:, 9:10], 0.0))

            def moe():
                dve.wait_ge(S["y_in"], 16)
                wide(lambda t: dve.tensor_tensor(at4(h_all, t), at4(h_all, t), at4(xT_all, t), ALU.add))
                wide(lambda t: dve.tensor_tensor(at4(x, t), at4(x, t), at4(h_all, t), ALU.add))
                all_stats(h_all)
                finish_stats(10)
                dve.wait_ge(S["stage_w_in"], W_IN["ln2"])
                L = Loop(NB // 4, 5)
                with dve.Fori(0, NB // 4) as t:
                    L.turn(t)
                    for j in range(4):
                        dve.wait_ge(S["f_T"], nth("f_T", 13, 4 * t + j - 4))
                        L.mark(normalise(xn[:, j, :], 4 * t + j, h_all))
                    L.hold()
                    L.mark(dve.tensor_tensor(xn[:], xn[:], bc(rows[:, 0, :], 4), ALU.mult))
                    L.hold()
                    dve.tensor_tensor(xn[:], xn[:], bc(rows[:, 1, :], 4), ALU.add).then_inc(S["f_xn"], 4)
                    L.end()
                dve.wait_ge(S["f_lg"], NB)
                dve.wait_ge(S["f_cp"], 2 * NB)
                lg = ps[:, 7, :].rearrange("p (s e) -> p s e", e=NE)
                m1, m2, top = t1[:], t2[:], nmr[:]

                def pick(logits, m, sel):
                    link(dve.tensor_reduce(m, logits, AX.X, ALU.max))
                    link(dve.tensor_tensor(sel, logits, bl(m, NE), ALU.is_ge))
                    link(dve.tensor_tensor(sel, sel, bc(descend, NB), ALU.mult))
                    link(dve.tensor_reduce(top, sel, AX.X, ALU.max))
                    link(dve.tensor_tensor(sel, sel, bl(top, NE), ALU.is_equal))

                pick(lg, m1, ra)
                link(dve.scalar_tensor_tensor(rb, ra, MASKED, lg, ALU.mult, ALU.add))
                pick(rb, m2, rc_)
                link(dve.tensor_tensor(selbf.rearrange("p (s e) -> p s e", e=NE), ra, rc_, ALU.add))
                dve.tensor_tensor(m2, m2, m1, ALU.subtract).then_inc(S["route_dve"], 1)
                dve.wait_ge(S["route_dve"], 1)
                dve.sem_inc(S["route_act"], 1)
                dve.wait_ge(S["route_act"], 2)
                link(dve.tensor_scalar(m1, m2, 1.0, None, ALU.add))
                link(dve.reciprocal(m1, m1))
                link(dve.tensor_tensor(m2, m2, m1, ALU.mult))
                link(dve.tensor_tensor(ra, ra, bl(m1, NE), ALU.mult))
                link(dve.tensor_tensor(rc_, rc_, bl(m2, NE), ALU.mult))
                link(dve.tensor_tensor(coef[:], ra, rc_, ALU.add))
                dve.wait_ge(S["route_pe"], 1)
                total = ps[:, 1, :].rearrange("p (s e) -> p s e", e=NE)
                link(dve.tensor_copy(ra, total))
                old, new = ra, rb
                k = 1
                while k < NB:
                    link(dve.tensor_tensor(new[:, k:, :], old[:, k:, :], old[:, :NB - k, :], ALU.add))
                    link(dve.tensor_copy(new[:, 0:k, :], old[:, 0:k, :]))
                    old, new = new, old
                    k *= 2
                link(dve.tensor_tensor(new, old, total, ALU.subtract))
                link(dve.tensor_tensor(new, new, ps[:, 0, :].rearrange("p (s e) -> p s e", e=NE), ALU.add))
                link(dve.scalar_tensor_tensor(coef[:], new, float(CAP), coef[:], ALU.is_lt, ALU.mult))
                dve.sem_inc(S["route_dve"], 1)
                L = Loop(NB // 4, 4 * NE)
                with dve.Fori(0, NB // 4) as t:
                    L.turn(t)
                    for e in range(NE):
                        dve.wait_ge(S["f_down"], G0 // FC + t * NE + e + 1)
                        for r in range(4):
                            i = 4 * t + r
                            L.mark(dve.scalar_tensor_tensor(
                                at(x, i), ps[:, 4 + e % 2, r * P:(r + 1) * P],
                                coef[:, bass.ds(i, 1), e:e + 1].rearrange("p a n -> p (a n)"), at(x, i),
                                ALU.mult, ALU.add))
                        L.hold()
                        dve.sem_inc(S["f_acc"], 1)
                    L.end()
                link_go(dve.memset(sm[:, 9:10], 0.0))

            if LAST >= 0:
                attention(0)
                finish_stats(2)
            if LAST >= 0.5:
                hadamard_ffn()
                finish_stats(3)
            if LAST >= 1:
                attention(1)
                finish_stats(4)
            if LAST >= 1.5:
                conv_ffn()
                finish_stats(5)
            if LAST >= 2:
                attention(2)
                finish_stats(6)
            if LAST >= 2.5:
                expert_ffn()
                finish_stats(7)
            if LAST >= 3:
                attention(3)
                finish_stats(8)
            if LAST >= 4:
                hidden_in()
                attention(4)
                moe()

        @block.gpsimd
        def _(pool):
            def settled():
                pool.sem_inc(S["pool_step"], 1)

            def attention(s):
                nk = nkeys(s)

                def casts(I):
                    t, j = I
                    i = num(I)
                    pool.wait_ge(S["q_ready"], nth("q_ready", s, i))
                    settled()
                    pool.tensor_copy(qb[:, j, :], qf[:, j, :]).then_inc(S["qb_ready"], 1)
                    pool.wait_ge(S["k_ready"], nth("k_ready", s, i))
                    settled()
                    pool.tensor_copy(kb[:, j, 0:HG * nk], kblk[:, j, 0:HG * nk]).then_inc(S["kb_ready"], 1)

                def bias(I, used):
                    t, j = I
                    i = num(I)
                    if s not in (0, 1, 3):
                        return
                    if used:
                        pool.wait_ge(S["b_ready"], nth("b_ready", s, i - 2, 2, 2))
                    if s == 0:
                        pool.wait_ge(S["bln_ready"], nth("bln_ready", s, i))
                        settled()
                        pool.tensor_scalar(biasf[:, j, :], bln[:, j, :], dscale[:, 0:1], None, ALU.mult
                                           ).then_inc(S["biasf_ready"], 1)
                        pool.wait_ge(S["biasf_ready"], nth("biasf_ready", s, i))
                        settled()
                        pool.tensor_copy(biasb[:, j, :], biasf[:, j, :]).then_inc(S["bias_ready"], 1)
                        return
                    pool.wait_ge(S[f"bias_in{j}"], nth_dma("bias_in0", s, t))
                    raw = braw[:, j, :].bitcast(I32) if s == 1 else braw_u[:, j, :]
                    settled()
                    pool.tensor_scalar(biasb[:, j, :], raw, 0.0, MASKED, ALU.is_equal, ALU.mult
                                       ).then_inc(S["bias_ready"], 1)

                def add_bo(I):
                    i = num(I)
                    if s < 3:
                        pool.wait_ge(S["xn_ready"], nth("xn_ready", s, i))
                        pool.tensor_tensor(at(x, i), at(x, i), rows[:, 1, :], ALU.add).then_inc(S["xbo_ready"], 1)
                    if s == 3:
                        pool.wait_ge(S["xn_ready"], nth("xn_ready", s, i))

                def body(I, prev, nxt, nxt2):
                    if nxt:
                        bias(item(I, 1), prev)
                        casts(item(I, 1))
                    add_bo(I)

                pool.wait_ge(S["stage_go"], GO[s])
                pool.wait_ge(S["stage_w_in"], W_IN[s])
                bias((0, 0), False)
                casts((0, 0))
                steps(pool, body)

            def expert_back():
                pool.wait_ge(S["f_acc"], 2 * NE)
                with pool.Fori(0, NB // 4) as t:
                    for j in range(4):
                        pool.wait_ge(S["f_back"], 4 * t + j + 1)
                        settled()
                        pool.tensor_copy(work[:, j, 0:P], at(h_all, 4 * t + j)).then_inc(S["f_cp"], 1)

            def keep_turned():
                with pool.Fori(0, NB // 4) as t:
                    for j in range(4):
                        pool.wait_ge(S["f_xT"], nth("f_xT", 13, 4 * t + j))
                        settled()
                        pool.tensor_copy(at(xT_all, 4 * t + j), work[:, j, 0:P]).then_inc(S["f_cp"], 1)
                    for j in range(4):
                        pool.wait_ge(S["f_cp"], NB + 4 * t + j + 1)
                        pool.wait_ge(S["f_lg"], 4 * t + j + 1)
                        pool.sem_inc(S["f_copied"], 1)

            pool.sem_inc(S["f_back"], 4)
            pool.sem_inc(S["f_copied"], 4)
            if LAST >= 0:
                attention(0)
            if LAST >= 1:
                attention(1)
            if LAST >= 2:
                attention(2)
            if LAST >= 2.5:
                expert_back()
                pool.wait_ge(S["stage_go"], GO[12] + 1)
                pool.sem_inc(S["ffn2_done"], 1)
            if LAST >= 3:
                attention(3)
            if LAST >= 4:
                attention(4)
                keep_turned()


def kernel(**inputs):
    import concourse.bacc as bacc
    from concourse.bass_utils import run_bass_kernel_spmd as run

    a = {n: np.ascontiguousarray(v) for n, v in inputs.items()}
    f = np.float32
    eye = np.eye(P, dtype=f)
    had = np.array([[1.0]])
    while had.shape[0] < P:
        had = np.block([[had, had], [had, -had]])
    had = (had / np.sqrt(P)).astype(f)
    p = np.arange(P)
    headmask = ((p[:, None] % 32) // DH == np.arange(HG)[None]).astype(f)
    descend = np.broadcast_to(np.arange(NE, 0, -1, dtype=f), (P, NE))
    cpack = np.concatenate([eye, had, np.ones((P, P), f), headmask, descend], axis=1)
    causal2 = np.where(p[None] <= p[:, None], 0.0, MASKED).astype(f)
    causal4 = np.where((p[None] // NB == p[:, None] // NB) & (p[None] <= p[:, None]), 0.0, MASKED).astype(f)
    tri = (p[:, None] < p[None]).astype(f)
    bpack = np.stack([causal2, causal4, tri, np.ones((P, P), f)], axis=1)
    sel = ((p[:, None] % 32 < 2 * HG) & (p[:, None] % HG == np.arange(HG)[None])).astype(f)
    selpack = np.ascontiguousarray(np.broadcast_to(sel[:, :, None], (P, HG, P)))
    h = np.arange(P) // DH
    r = (h // 2) * 4 * DH
    e = np.arange(P) % DH
    qkv = a["L3_ffn_qkv_weight"]
    moe_q, moe_k, moe_v = qkv[r + (h % 2) * DH + e], qkv[r + 2 * DH + e], qkv[r + 3 * DH + e]
    z = np.zeros((P, P), f)
    wm = np.stack([np.stack([w.T for w in ws]) for ws in (
        [a["L0_xattn_W" + c] for c in "qkvo"],
        [a["L1_xattn_W_" + c] for c in "qkvo"],
        [a["L2_xattn_W" + c] for c in "qkvo"],
        [a["L3_xattn_W" + c] for c in "qkv"] + [z],
        [moe_q, moe_k, moe_v, a["L3_ffn_proj_weight"]])])
    zr = np.zeros(P, f)
    cols = np.stack([a["L0_xattn_bq"], a["L0_xattn_bk"], a["L1_xattn_b_q"], a["L1_xattn_b_k"], zr, zr,
                     a["L3_xattn_bq"], a["L3_xattn_bk"], zr, zr], axis=1)
    rows = np.stack([np.stack(v) for v in (
        [a["L0_xattn_bv"], a["L0_xattn_bo"]], [a["L1_xattn_b_v"], a["L1_xattn_b_o"]],
        [zr, a["L2_xattn_bo"]], [a["L3_xattn_bv"], zr], [zr, zr],
        [a["L3_ffn_ln1_weight"], a["L3_ffn_ln1_bias"]], [a["L3_ffn_ln2_weight"], a["L3_ffn_ln2_bias"]])])
    arrays = {
        "x": a["x"], "ctx": a["ctx_1024"], "dist": a["fside_BxSxS2_0"],
        "mask1": a["mask_Bx1xSxS2_ik1"].reshape(NB, P, NC), "mask3": a["mask_BxSxS2_bk1"],
        "cpack": cpack, "bpack": bpack, "selpack": selpack, "wm": wm, "cols": cols, "rows": rows,
        "dscale": a["L0_xattn_distance_scaling"].reshape(1, 1), "router": a["L3_ffn_router_weight"],
        "L0_w": a["L0_ffn_weight"], "w1T": a["L1_ffn_w1"].T,
        "w2T": a["L1_ffn_w2"].T.reshape(FC, P, P).transpose(1, 0, 2),
        "convT": a["L1_ffn_conv_w"][:, 0, :].T, "convb": a["L1_ffn_conv_b"].reshape(1, FF),
        "b1c": a["L2_ffn_b1"].reshape(NE, FC, P).transpose(2, 0, 1), "b2c": a["L2_ffn_b2"].T,
        "L2_W1": a["L2_ffn_W1"], "L2_W2": a["L2_ffn_W2"],
        "L3_W1": a["L3_ffn_moe_w1"], "L3_W2": a["L3_ffn_moe_w2"],
    }
    arrays = {n: np.ascontiguousarray(v) for n, v in arrays.items()}
    nc = bacc.Bacc("TRN2", target_bir_lowering=False, num_devices=1)
    d = {n: nc.dram_tensor("in_" + n, v.shape, mybir.dt.from_np(v.dtype), kind="ExternalInput").ap()
         for n, v in arrays.items()}
    out = nc.dram_tensor("out", (NB, P, P), F32, kind="ExternalOutput").ap()
    build(nc, d, out)
    r = run(nc, [{"in_" + n: v for n, v in arrays.items()}], core_ids=[0])
    return r.results[0]["out"]
```

```python
from contextlib import ExitStack

import numpy as np

import concourse.bass as bass
from concourse import mybir

F32 = mybir.dt.float32
BF16 = mybir.dt.bfloat16
F16 = mybir.dt.float16
I32 = mybir.dt.int32
U8 = mybir.dt.uint8
ALU = mybir.AluOpType
ACT = mybir.ActivationFunctionType
AX = mybir.AxisListType

P = 128
NB = 64
NC = 120
NH = 16
DH = P // NH
HG = 4
NG = NH // HG
NE = 8
FF = 512
FC = FF // P
CAP = 2560
EPS = 1e-5
QSCALE = [float(1.0 / np.sqrt(np.float32(w))) for w in (DH, DH, DH, P, DH)]
MASKED = -(2.0 ** 100)
ROUND = 1.5 * 2.0 ** 23

LAST = 4

_ORDER = [0, 10, 1, 11, 2, 12, 3, "ln1", "ln1b", 4, 13, "end"]
GO = {s: k + 1 for k, s in enumerate(_ORDER)}
if LAST < 4:
    GO["end"] = int(2 * LAST) + 2
W_IN = {0: 32, 1: 64, 2: 96, 3: 128, "ln1": 144, 4: 176, "ln2": 192}
G0 = 2 * NE * FC


def build(nc, d, out, last_stage=99):
    with ExitStack() as ctx:
        def sb(name, shape, dt=F32):
            return ctx.enter_context(nc.sbuf_tensor(name, shape, dt))

        x = sb("x", [P, NB, P])
        h_all = sb("h_all", [P, NB, P])
        xT_all = sb("xT_all", [P, NB, P])
        w1_sb = sb("w1_sb", [P, NE, FF])
        w2_sb = sb("w2_sb", [P, NE, FC, P])
        cpack = sb("cpack", [P, 3 * P + NH + NE])
        ident, hada, onesf = cpack[:, 0:P], cpack[:, P:2 * P], cpack[:, 2 * P:3 * P]
        headmask = cpack[:, 3 * P:3 * P + NH]
        descend = cpack[:, 3 * P + NH:3 * P + NH + NE]
        identb = sb("identb", [P, P], BF16)
        causalb = sb("causalb", [P, 2, P], BF16)
        trib = sb("trib", [P, P], BF16)
        onesb = sb("onesb", [P, P], BF16)
        selb = sb("selb", [P, NH, P], BF16)
        wm = sb("wm", [P, 4, P])
        cols = sb("cols", [P, 10])
        rows = sb("rows", [P, 2, P])
        stats = sb("stats", [P, NB, 6])
        rstd = sb("rstd", [P, NB])
        nmr = sb("nmr", [P, NB])
        t1 = sb("t1", [P, NB])
        t2 = sb("t2", [P, NB])
        dscale = sb("dscale", [P, 1])
        xn = sb("xn", [P, 4, P])
        ctx_sb = sb("ctx_sb", [NC, 2, P])
        braw = sb("braw", [P, 2, NC])
        bln = sb("bln", [P, 2, NC])
        braw_u = sb("braw_u", [P, 2, NC], U8)
        biasf = sb("biasf", [P, 2, NC])
        biasb = sb("biasb", [P, 2, NC], BF16)
        xcT = sb("xcT", [P, 2, 2 * P])
        qf = sb("qf", [P, 2, P])
        kblk = sb("kblk", [P, 2, NH * P])
        vf = sb("vf", [P, 2, P])
        vh = sb("vh", [P, 2, NH, DH + 1], BF16)
        vl = sb("vl", [P, 2, NH, DH + 1], F16)
        negmax = sb("negmax", [P, 2, NH])
        mparts = sb("mparts", [P, 2, P], BF16)
        mT = sb("mT", [P, 2, P], BF16)
        ex = sb("ex", [P, 2, NH * P])
        exl = sb("exl", [P, 2, NH * P], F16)
        rec = sb("rec", [P, 2, NH])
        o_sb = sb("o_sb", [P, 2, P])
        oT = sb("oT", [P, 2, P])
        y_sb = sb("y_sb", [P, 2, P])
        work = kblk[:, 0, :].rearrange("p (a n) -> p a n", a=4)
        workb = exl[:, 0, :].bitcast(BF16).rearrange("p (a n) -> p a n", a=4)
        qT = exl[:, 1, :].bitcast(BF16).rearrange("p (a n) -> p a n", a=4)
        xqT = sb("xqT", [P, 4, P + 2])
        sc = sb("sc", [P, 4, 4])
        wconv = h_all[:, 0:12, :].rearrange("p a n -> p (a n)").rearrange("p (k n) -> p k n", k=3)
        convb = h_all[0:1, 12:16, :].rearrange("p a n -> p (a n)")
        wscale = h_all[:, 16, :]
        w2q = h_all[:, 17:19, :].rearrange("p a n -> p (a n)").bitcast(BF16).rearrange("p (c n) -> p c n", c=FC)
        ternT = h_all[:, 19, 0:P // 2].bitcast(BF16)
        sm = sb("sm", [P, 12])
        b1c = sb("b1c", [P, NE, FC])
        b2c = sb("b2c", [P, NE])
        router = sb("router", [P, NE])
        coef = xcT[:, :, :].rearrange("p a n -> p (a n)").rearrange("p (b e) -> p b e", e=NE)
        hid = ex[:, :, :].rearrange("p a (c n) -> p a c n", c=FC)
        ra, rb, rc_, rd = (work[:, k, :].rearrange("p (s e) -> p s e", e=NE) for k in range(4))
        selbf = workb[:, 0, :]

        ps = ctx.enter_context(nc.psum_tensor("ps", [P, 8, 512], F32))
        a_ps = [ps[:, 0, :], ps[:, 1, :]]
        b_ps = [ps[:, 2:4, :].rearrange("p a n -> p (a n)"), ps[:, 4:6, :].rearrange("p a n -> p (a n)")]
        front, back = ps[:, 6, :], ps[:, 7, :]
        mT_ps = ps[:, 0, 0:64].bitcast(BF16)

        u_dram = nc.dram_tensor("u_dram", [NB, P, P], F32, kind="Internal").ap()
        y_dram = nc.dram_tensor("y_dram", [NB, P, P], F32, kind="Internal").ap()

        names = """consts_in weights_in stage_w_in u_out ctx_in0 ctx_in1 bias_in0 bias_in1 u_in0 u_in1
            y_out0 y_out1 y_in moe_w_in out_done stage_go sq_in sq_out dve_step setup_dve setup_pe
            xn_ready T_ready xcT_ready proj_ready vproj_ready vf_ready vh_ready vl_ready el_ready q_ready k_ready bln_ready
            biasf_ready bias_ready a_ready max_ready mparts_ready mT_out mT_ready b_ready e_ready pv_ready rec_ready eps_ready
            o_ready oT_out oT_ready wo_ready xbo_ready x_done
            f_xn f_T f_xT f_mm f_q f_qT f_qTs f_out f_act f_up f_gelu f_down f_acc f_cp f_back f_backT
            f_lg f_copied u_made y_added x_init pool_step route_dve route_pe route_act ffn2_done sp_step""".split()
        S = {n: ctx.enter_context(nc.semaphore(n)) for n in names}

        ATT = [0, 1, 2, 3, 4]
        USES = {n: ATT for n in names}
        USES.update({n: [0, 1, 2, 3] for n in ("xn_ready", "xbo_ready", "ctx_in0", "ctx_in1")})
        USES.update({n: [0, 1, 3] for n in ("bias_ready", "bias_in0", "bias_in1")})
        USES.update({n: [0] for n in ("bln_ready", "biasf_ready")})
        USES.update({n: [0, 1, 2, 4] for n in ("oT_out", "oT_ready", "wo_ready", "rec_ready")})
        USES.update({n: [4] for n in ("u_in0", "u_in1", "y_out0", "y_out1")})
        USES.update({n: [10, 11, 12, 13] for n in ("f_xn", "f_T", "f_xT")})
        USES.update({n: [10, 11] for n in ("f_mm", "f_q", "f_qT", "f_qTs", "f_out")})
        USES.update({n: [11] for n in ("f_act",)})

        def nth(name, s, i, k=1, n=1):
            return (USES[name].index(s) * NB + i) * n + k

        def nth_dma(name, s, t):
            return 16 * (USES[name].index(s) * (NB // 2) + t + 1)

        def bc(ap, n):
            return ap.unsqueeze(1).to_broadcast([ap.shape[0], n, ap.shape[1]])

        def bl(ap, n):
            return ap.unsqueeze(2).to_broadcast([ap.shape[0], ap.shape[1], n])

        def high(ap):
            return ap.bitcast(BF16).rearrange("p (n two) -> p n two", two=2)[:, :, 1]

        def item(I, k):
            t, j = I
            return t + (j + k) // 2, (j + k) % 2

        def num(I):
            return 2 * I[0] + I[1]

        def at(tensor, i):
            if isinstance(i, int):
                return tensor[:, i, :]
            return tensor[:, bass.ds(i, 1), :].rearrange("p a n -> p (a n)")

        def at4(tensor, t):
            return tensor[:, bass.ds(4 * t, 4), :]

        def col(tensor, i):
            return tensor[:, bass.ds(i, 1)]

        def steps(eng, body):
            def peeled(i):
                body((i // 2, i % 2), lambda k: 0 <= i + k < NB)

            peeled(0)
            peeled(1)
            with eng.Fori(1, NB // 2 - 2) as t:
                for j in range(2):
                    body((t, j), lambda k: True)
            for i in range(NB - 4, NB):
                peeled(i)

        def nkeys(s):
            return P if s == 4 else NC

        block = ctx.enter_context(nc.Block())

        N_CONSTS, N_WEIGHTS = 6, 10

        @block.sync
        def _(sp):
            sp.dma_start(x[:], d["x"].rearrange("b s n -> s b n")).then_inc(S["x_init"], 16)
            sp.dma_start(cpack[:], d["cpack"]).then_inc(S["consts_in"], 16)
            sp.dma_start(xT_all[:, 0:4, :], d["bpack"]).then_inc(S["consts_in"], 16)
            sp.dma_start(xT_all[:, 4:4 + NH, :], d["selpack"]).then_inc(S["consts_in"], 16)
            sp.dma_start(cols[:], d["cols"]).then_inc(S["consts_in"], 16)
            sp.dma_start(dscale[:], d["dscale"].to_broadcast([P, 1])).then_inc(S["consts_in"], 16)
            sp.dma_start(router[:], d["router"]).then_inc(S["consts_in"], 16)
            sp.dma_start(work[:, 0, 0:P], d["L0_w"]).then_inc(S["weights_in"], 16)
            sp.dma_start(work[:, 1, :], d["w1T"]).then_inc(S["weights_in"], 16)
            sp.dma_start(work[:, 2, :].rearrange("p (c n) -> p c n", c=FC), d["w2T"]).then_inc(S["weights_in"], 16)
            for k in range(3):
                sp.dma_start(ex[:, 0, k * FF:(k + 1) * FF],
                             d["convT"][k:k + 1, :].to_broadcast([P, FF])).then_inc(S["weights_in"], 16)
            sp.dma_start(convb, d["convb"]).then_inc(S["weights_in"], 16)
            sp.dma_start(b1c[:], d["b1c"]).then_inc(S["weights_in"], 16)
            sp.dma_start(b2c[:], d["b2c"]).then_inc(S["weights_in"], 16)
            sp.dma_start(w1_sb[:], d["L2_W1"].rearrange("e p f -> p e f")).then_inc(S["weights_in"], 16)
            for e in range(NE):
                sp.dma_start(w2_sb[:, e, :, :],
                             d["L2_W2"][e].rearrange("(c p) n -> p c n", p=P)).then_inc(S["moe_w_in"], 16)

            def att_loads(s, I):
                t, j = I
                if s < 4:
                    sp.dma_start(ctx_sb[:, j, :], d["ctx"][bass.ds(num(I), 1)].rearrange("a k n -> (a k) n")
                                 ).then_inc(S[f"ctx_in{j}"], 16)
                if s == 0:
                    sp.dma_start(braw[:, j, :], d["dist"][bass.ds(num(I), 1)].rearrange("a q k -> (a q) k")
                                 ).then_inc(S[f"bias_in{j}"], 16)
                if s == 1:
                    sp.dma_start(braw[:, j, :].bitcast(I32), d["mask1"][bass.ds(num(I), 1)].rearrange("a q k -> (a q) k")
                                 ).then_inc(S[f"bias_in{j}"], 16)
                if s == 3:
                    sp.dma_start(braw_u[:, j, :], d["mask3"][bass.ds(num(I), 1)].rearrange("a q k -> (a q) k")
                                 ).then_inc(S[f"bias_in{j}"], 16)
                if s == 4:
                    for c in range(2):
                        sp.dma_start(xn[c * NB:(c + 1) * NB, j, :],
                                     u_dram[:, bass.ds(2 * num(I) + c, 1), :].rearrange("s a n -> s (a n)")
                                     ).then_inc(S[f"u_in{j}"], 16)

            def attention(s):
                if s:
                    sp.wait_ge(S["stage_go"], GO[s])
                sp.dma_start(wm[:], d["wm"][s].rearrange("m p n -> p m n")).then_inc(S["stage_w_in"], 16)
                sp.dma_start(rows[:], d["rows"][s].unsqueeze(0).to_broadcast([P, 2, P])).then_inc(S["stage_w_in"], 16)
                if s == 4:
                    sp.wait_ge(S["u_out"], 16)
                att_loads(s, (0, 0))
                att_loads(s, (0, 1))

                def reload(I):
                    i = num(I)
                    sp.wait_ge(S["T_ready"], nth("T_ready", s, i))
                    sp.sem_inc(S["sp_step"], 1)
                    if s in (0, 1, 3):
                        sp.wait_ge(S["bias_ready"], nth("bias_ready", s, i))
                    sp.sem_inc(S["sp_step"], 1)
                    att_loads(s, item(I, 2))

                reload((0, 0))

                def body(I, has):
                    if has(3):
                        reload(item(I, 1))
                    if has(-1) and s == 4:
                        store_y(item(I, -1))

                def store_y(I):
                    sp.wait_ge(S["x_done"], nth("x_done", s, num(I)))
                    sp.sem_inc(S["sp_step"], 1)
                    for c in range(2):
                        sp.dma_start(y_dram[:, bass.ds(2 * num(I) + c, 1), :].rearrange("s a n -> s (a n)"),
                                     y_sb[c * NB:(c + 1) * NB, I[1], :]).then_inc(S[f"y_out{I[1]}"], 16)

                steps(sp, body)
                if s == 4:
                    store_y((NB // 2 - 1, 1))

            for s in range(4):
                if s <= LAST:
                    attention(s)
            if LAST >= 4:
                sp.wait_ge(S["ffn2_done"], 1)
                sp.dma_start(w1_sb[:], d["L3_W1"].rearrange("e p f -> p e f")).then_inc(S["moe_w_in"], 16)
                for e in range(NE):
                    sp.dma_start(w2_sb[:, e, :, :],
                                 d["L3_W2"][e].rearrange("(c p) n -> p c n", p=P)).then_inc(S["moe_w_in"], 16)
                sp.wait_ge(S["stage_go"], GO["ln1"])
                sp.dma_start(rows[:], d["rows"][5].unsqueeze(0).to_broadcast([P, 2, P])).then_inc(S["stage_w_in"], 16)
                sp.wait_ge(S["u_made"], 1)
                sp.dma_start(u_dram.rearrange("s b n -> b s n"), xT_all[:]).then_inc(S["u_out"], 16)
                attention(4)
                for j in range(2):
                    sp.wait_ge(S[f"y_out{j}"], 2 * nth_dma("y_out0", 4, NB // 2 - 1))
                sp.dma_start(rows[:], d["rows"][6].unsqueeze(0).to_broadcast([P, 2, P])).then_inc(S["stage_w_in"], 16)
                sp.dma_start(xT_all[:], y_dram.rearrange("s b n -> b s n")).then_inc(S["y_in"], 16)
            sp.wait_ge(S["stage_go"], GO["end"])
            sp.dma_start(out.rearrange("b s n -> s b n"), x[:]).then_inc(S["out_done"], 16)
            sp.wait_ge(S["out_done"], 16)

        @block.tensor
        def _(pe):
            pe.wait_ge(S["setup_dve"], 1)
            pe.transpose(ps[:, 0, 0:64].bitcast(BF16), workb[:, 0, 0:P], identb[:]).then_inc(S["setup_pe"], 1)
            pe.matmul(ps[:, 1, 0:P], onesf, work[:, 3, 0:P], start=True, stop=True)
            pe.matmul(ps[:, 2, 0:2], onesf, sm[:, 0:2], start=True, stop=True).then_inc(S["setup_pe"], 1)

            def attention(s):
                nk = nkeys(s)
                bias = {0: biasb, 1: biasb, 3: biasb}.get(s)

                def turn(I, first=False):
                    t, j = I
                    i = num(I)
                    if not first:
                        pe.wait_ge(S["vf_ready"], nth("vf_ready", s, i - 1))
                    if s < 4:
                        pe.wait_ge(S["xn_ready"], nth("xn_ready", s, i))
                        pe.wait_ge(S[f"ctx_in{j}"], nth_dma("ctx_in0", s, t))
                    else:
                        pe.wait_ge(S[f"u_in{j}"], 2 * nth_dma("u_in0", s, t))
                    mm = pe.transpose(front[:, 0:P], xn[:, j, :], ident)
                    if s < 4:
                        mm = pe.transpose(front[:, P:P + NC], ctx_sb[:, j, :], ident[0:NC, 0:NC])
                    mm.then_inc(S["T_ready"], 1)

                def kv_src(j):
                    return xcT[:, j, 0:P] if s == 4 else xcT[:, j, P:P + NC]

                def project(I):
                    t, j = I
                    pe.wait_ge(S["xcT_ready"], nth("xcT_ready", s, num(I)))
                    pe.matmul(front[:, 0:P], wm[:, 0, :], xcT[:, j, 0:P], start=True, stop=True)
                    pe.matmul(front[:, P:P + nk], wm[:, 1, :], kv_src(j), start=True, stop=True
                              ).then_inc(S["proj_ready"], 1)

                def project_v(I):
                    t, j = I
                    pe.wait_ge(S["q_ready"], nth("q_ready", s, num(I)))
                    pe.wait_ge(S["k_ready"], nth("k_ready", s, num(I)))
                    pe.matmul(front[0:nk, 2 * P:3 * P], kv_src(j), wm[:, 2, :], start=True, stop=True
                              ).then_inc(S["vproj_ready"], 1)

                def scores_by_query(I, first):
                    t, j = I
                    i = num(I)
                    pe.wait_ge(S["q_ready"], nth("q_ready", s, i))
                    pe.wait_ge(S["k_ready"], nth("k_ready", s, i))
                    if bias is not None:
                        pe.wait_ge(S["bias_ready"], nth("bias_ready", s, i))
                    b = biasb[:, j, 0:nk] if bias is not None else causalb[:, (0 if s == 2 else 1), 0:nk]
                    for g in range(NG):
                        if not (first and g < 2):
                            pe.wait_ge(S["max_ready"], nth("max_ready", s, i, g - 1, NG))
                        pe.matmul(a_ps[g % 2][:, 0:HG * nk], identb[:], bc(b, HG), start=True, stop=False)
                        pe.matmul(a_ps[g % 2][:, 0:HG * nk], high(qf[:, j, :]),
                                  high(kblk[:, j, g * HG * nk:(g + 1) * HG * nk]), start=False, stop=True
                                  ).then_inc(S["a_ready"], 1)

                def turn_max(I):
                    t, j = I
                    pe.wait_ge(S["mparts_ready"], nth("mparts_ready", s, num(I), 2, 2))
                    pe.transpose(mT_ps, mparts[:, j, :], identb[:]).then_inc(S["mT_out"], 1)

                def scores_by_key(I, first, chunks):
                    t, j = I
                    i = num(I)
                    if s == 0:
                        pe.wait_ge(S["biasf_ready"], nth("biasf_ready", s, i))
                    for c in chunks:
                        if not first:
                            pe.wait_ge(S["e_ready"], nth("e_ready", s, i - 1, c + 1, 2))
                        for g in range(2 * c, 2 * c + 2):
                            o = b_ps[c][0:nk, (g % 2) * 512:(g % 2) * 512 + 512]
                            if s == 0:
                                pe.matmul(o, biasf[:, j, 0:nk], bc(ident, HG), start=True, stop=False,
                                          skip_group_check=True)
                            else:
                                b = biasb[:, j, 0:nk] if bias is not None else causalb[:, (0 if s == 2 else 1), 0:nk]
                                pe.matmul(o, b, bc(identb[:], HG), start=True, stop=False,
                                          skip_group_check=True)
                            for k in range(HG):
                                h = HG * g + k
                                pe.matmul(o[:, k * P:(k + 1) * P], kblk[:, j, h * nk:(h + 1) * nk], qf[:, j, :],
                                          start=False, stop=False, skip_group_check=True)
                            if g == 0:
                                pe.wait_ge(S["mT_ready"], nth("mT_ready", s, i))
                            for k in range(HG):
                                mm = pe.matmul(o[:, k * P:(k + 1) * P], selb[:, HG * g + k, 0:nk], mT[:, j, :],
                                               start=False, stop=True, skip_group_check=True)
                        mm.then_inc(S["b_ready"], 1)

                def values(I, first, half):
                    t, j = I
                    i = num(I)
                    if half == 0:
                        pe.wait_ge(S["vl_ready"], nth("vl_ready", s, i))
                        if not first:
                            pe.wait_ge(S["x_done"], nth("x_done", s, i - 1))
                    pe.wait_ge(S["el_ready"], nth("el_ready", s, i, half + 1, 2))
                    for h in range(8 * half, 8 * half + 8):
                        o, q = back[:, h * 9:h * 9 + 9], slice(h * P, (h + 1) * P)
                        pe.matmul(o, high(ex[0:nk, j, q]), vh[0:nk, j, h, :], start=True, stop=False)
                        pe.matmul(o, high(ex[0:nk, j, q]), vl[0:nk, j, h, :], start=False, stop=False)
                        pe.matmul(o, exl[0:nk, j, q], vh[0:nk, j, h, :], start=False, stop=False)
                        mm = pe.matmul(o, exl[0:nk, j, q], vl[0:nk, j, h, :], start=False, stop=True)
                    if half:
                        mm.then_inc(S["pv_ready"], 1)

                def turn_out(I):
                    if s == 3:
                        return
                    t, j = I
                    pe.wait_ge(S["o_ready"], nth("o_ready", s, num(I)))
                    pe.transpose(back[:, 144:144 + P], o_sb[:, j, :], ident).then_inc(S["oT_out"], 1)

                def project_out(I):
                    if s == 3:
                        return
                    t, j = I
                    pe.wait_ge(S["oT_ready"], nth("oT_ready", s, num(I)))
                    pe.matmul(back[:, 272:272 + P], oT[:, j, :], wm[:, 3, :], start=True, stop=True
                              ).then_inc(S["wo_ready"], 1)

                def body(I, has):
                    turn_max(I)
                    for half in range(2):
                        scores_by_key(I, not has(-1), (half,))
                        if has(-1):
                            values(item(I, -1), not has(-2), half)
                    if has(1):
                        project_v(item(I, 1))
                        scores_by_query(item(I, 1), False)
                    if has(-1):
                        turn_out(item(I, -1))
                    if has(2):
                        turn(item(I, 2))
                    if has(-1):
                        project_out(item(I, -1))
                    if has(2):
                        project(item(I, 2))

                pe.wait_ge(S["stage_go"], GO[s])
                pe.wait_ge(S["stage_w_in"], W_IN[s])
                turn((0, 0), True)
                project((0, 0))
                project_v((0, 0))
                scores_by_query((0, 0), True)
                turn((0, 1))
                project((0, 1))
                steps(pe, body)
                end = (NB // 2 - 1, 1)
                values(end, False, 0)
                values(end, False, 1)
                turn_out(end)
                project_out(end)

            def wait4(name, s, t, j, back_by=0):
                pe.wait_ge(S[name], nth(name, s, 4 * t + j - back_by))

            def hadamard_ffn():
                pe.wait_ge(S["stage_go"], GO[10])
                with pe.Fori(0, NB // 4) as t:
                    for j in range(4):
                        wait4("f_xn", 10, t, j)
                        pe.transpose(ps[:, j, 0:P], xn[:, j, :], ident).then_inc(S["f_T"], 1)
                    for j in range(4):
                        wait4("f_xT", 10, t, j)
                        pe.matmul(ps[:, j, P:2 * P], work[:, j, 0:P], hada, start=True, stop=True
                                  ).then_inc(S["f_mm"], 1)
                    for j in range(4):
                        wait4("f_q", 10, t, j)
                        pe.transpose(ps[:, j, 256:320].bitcast(BF16), workb[:, j, 0:P], identb[:]
                                     ).then_inc(S["f_qT"], 1)
                    for j in range(4):
                        wait4("f_qTs", 10, t, j)
                        pe.matmul(ps[:, j, 384:512], qT[:, j, 0:P], ternT, start=True, stop=True
                                  ).then_inc(S["f_out"], 1)

            def conv_ffn():
                pe.wait_ge(S["stage_go"], GO[11])
                with pe.Fori(0, NB // 4) as t:
                    for j in range(4):
                        wait4("f_xn", 11, t, j)
                        pe.transpose(ps[:, j, 0:P], xn[:, j, :], ident).then_inc(S["f_T"], 1)
                    for j in range(4):
                        wait4("f_xT", 11, t, j)
                        pe.matmul(ps[:, j, :], onesf[0:1, :], convb, start=True, stop=False)
                        for k in range(3):
                            mm = pe.matmul(ps[:, j, :], xqT[:, j, k:k + P], wconv[:, k, :],
                                           start=False, stop=k == 2)
                        mm.then_inc(S["f_mm"], 1)
                    for j in range(4):
                        wait4("f_q", 11, t, j)
                        for c in range(FC):
                            mm = pe.transpose(ps[:, j, 64 * c:64 * c + 64].bitcast(BF16),
                                              workb[:, j, c * P:(c + 1) * P], identb[:])
                        mm.then_inc(S["f_qT"], 1)
                    for j in range(4):
                        wait4("f_qTs", 11, t, j)
                        for c in range(FC):
                            mm = pe.matmul(ps[:, j, 384:512], qT[:, j, c * P:(c + 1) * P], w2q[:, c, :],
                                           start=c == 0, stop=c == FC - 1)
                        mm.then_inc(S["f_out"], 1)

            def turn_all(s):
                with pe.Fori(0, NB // 4) as t:
                    for j in range(4):
                        wait4("f_xn", s, t, j)
                        wait4("f_xT", s, t, j, 4)
                        pe.transpose(ps[:, j, 0:P], xn[:, j, :], ident).then_inc(S["f_T"], 1)

            def expert_ffn():
                pe.wait_ge(S["stage_go"], GO[12])
                turn_all(12)
                pe.wait_ge(S["f_xT"], nth("f_xT", 12, NB - 1))
                pe.wait_ge(S["moe_w_in"], 16 * NE)
                units = [(e, half) for e in range(NE) for half in range(2)]

                def up(u):
                    e, half = units[u]
                    rhs = xT_all[:, half * 32:half * 32 + 32, e * 16:e * 16 + 16]
                    for c in range(FC):
                        if u:
                            pe.wait_ge(S["f_gelu"], (u - 1) * FC + c + 1)
                        pe.matmul(ps[:, c, :], w1_sb[:, e, c * P:(c + 1) * P], rhs, start=True, stop=True
                                  ).then_inc(S["f_up"], 1)

                def down(u):
                    e, half = units[u]
                    if u >= 2:
                        pe.wait_ge(S["f_acc"], u - 1)
                    for c in range(FC):
                        pe.wait_ge(S["f_gelu"], u * FC + c + 1)
                        mm = pe.matmul(ps[:, 4 + u % 2, :], w2_sb[:, e, c, :], hid[:, u % 2, c, :],
                                       start=c == 0, stop=c == FC - 1)
                    mm.then_inc(S["f_down"], 1)

                up(0)
                for u in range(len(units)):
                    if u + 1 < len(units):
                        up(u + 1)
                    down(u)
                with pe.Fori(0, NB // 4) as t:
                    for j in range(4):
                        pe.wait_ge(S["f_cp"], 4 * t + j + 1)
                        pe.transpose(ps[:, j, 0:P], work[:, j, 0:P], ident).then_inc(S["f_backT"], 1)

            def moe():
                turn_all_moe()
                pe.wait_ge(S["route_dve"], 1)
                pe.matmul(ps[:, 0, :], trib[:], selbf, start=True, stop=True)
                pe.matmul(ps[:, 1, :], onesb[:], selbf, start=True, stop=True).then_inc(S["route_pe"], 1)
                pe.wait_ge(S["route_dve"], 2)
                pe.wait_ge(S["moe_w_in"], 16 * (2 * NE + 1))

                def up(t, e):
                    rhs = at4(xT_all, t).rearrange("p a n -> p (a n)")
                    n = t * (NE * FC) + e * FC
                    for c in range(FC):
                        pe.wait_ge(S["f_gelu"], G0 + n + c + 1 - FC)
                        pe.matmul(ps[:, c, :], w1_sb[:, e, c * P:(c + 1) * P], rhs, start=True, stop=True
                                  ).then_inc(S["f_up"], 1)

                def down(t, e):
                    n = t * NE + e
                    pe.wait_ge(S["f_acc"], G0 // FC + n - 1)
                    pe.wait_ge(S["f_gelu"], G0 + (n + 1) * FC)
                    for r in range(4):
                        for c in range(FC):
                            mm = pe.matmul(ps[:, 4 + e % 2, r * P:(r + 1) * P], hid[:, e % 2, c, r * P:(r + 1) * P],
                                           w2_sb[:, e, c, :], start=c == 0, stop=c == FC - 1)
                    mm.then_inc(S["f_down"], 1)

                with pe.Fori(0, NB // 4) as t:
                    up(t, 0)
                    for e in range(NE):
                        if e + 1 < NE:
                            up(t, e + 1)
                        down(t, e)

            def turn_all_moe():
                with pe.Fori(0, NB // 4) as t:
                    for j in range(4):
                        wait4("f_xn", 13, t, j)
                        wait4("f_xT", 13, t, j, 4)
                        pe.transpose(ps[:, j, 0:P], xn[:, j, :], ident).then_inc(S["f_T"], 1)
                    for j in range(4):
                        wait4("f_xT", 13, t, j)
                        pe.matmul(ps[:, 7, bass.ds((4 * t + j) * NE, NE)], work[:, j, 0:P], router[:],
                                  start=True, stop=True).then_inc(S["f_lg"], 1)

            if LAST >= 0:
                attention(0)
            if LAST >= 0.5:
                hadamard_ffn()
            if LAST >= 1:
                attention(1)
            if LAST >= 1.5:
                conv_ffn()
            if LAST >= 2:
                attention(2)
            if LAST >= 2.5:
                expert_ffn()
            if LAST >= 3:
                attention(3)
            if LAST >= 4:
                attention(4)
                moe()

        @block.scalar
        def _(act):
            def sqrt_stats(n):
                act.wait_ge(S["sq_in"], n)
                act.activation(t1[:], t1[:], ACT.Sqrt).then_inc(S["sq_out"], 1)

            def attention(s):
                nk = nkeys(s)

                def copy_turned(I):
                    t, j = I
                    act.wait_ge(S["T_ready"], nth("T_ready", s, num(I)))
                    w = P if s == 4 else P + NC
                    act.copy(xcT[:, j, 0:w], front[:, 0:w]).then_inc(S["xcT_ready"], 1)

                def scale_q(I):
                    t, j = I
                    act.wait_ge(S["proj_ready"], nth("proj_ready", s, num(I)))
                    act.activation(qf[:, j, :], front[:, 0:P], ACT.Identity, bias=cols[:, 2 * s:2 * s + 1],
                                   scale=QSCALE[s]).then_inc(S["q_ready"], 1)

                def log_dist(I):
                    t, j = I
                    if s == 0:
                        act.wait_ge(S[f"bias_in{j}"], nth_dma("bias_in0", s, t))
                        act.activation(bln[:, j, :], braw[:, j, :], ACT.Ln, bias=sm[:, 11:12]
                                       ).then_inc(S["bln_ready"], 1)

                def copy_max(I):
                    t, j = I
                    act.wait_ge(S["mT_out"], nth("mT_out", s, num(I)))
                    act.copy(mT[:, j, :], mT_ps).then_inc(S["mT_ready"], 1)

                def exps(I):
                    t, j = I
                    for c in range(2):
                        act.wait_ge(S["b_ready"], nth("b_ready", s, num(I), c + 1, 2))
                        act.activation(ex[0:nk, j, c * 1024:(c + 1) * 1024], b_ps[c][0:nk, :], ACT.Exp
                                       ).then_inc(S["e_ready"], 1)

                def copy_out(I):
                    t, j = I
                    if s == 3:
                        return
                    act.wait_ge(S["oT_out"], nth("oT_out", s, num(I)))
                    act.copy(oT[:, j, :], back[:, 144:144 + P]).then_inc(S["oT_ready"], 1)

                def norm_in(I, wait=True):
                    t, j = I
                    if s == 4:
                        return
                    if wait:
                        act.wait_ge(S["T_ready"], nth("T_ready", s, num(I) - 2))
                    act.activation(xn[:, j, :], at(x, num(I)), ACT.Identity, bias=col(nmr, num(I)),
                                   scale=col(rstd, num(I))).then_inc(S["xn_ready"], 1)

                def body(I, has):
                    copy_max(I)
                    if has(1) and s == 0:
                        if has(-1):
                            act.wait_ge(S["biasf_ready"], nth("biasf_ready", s, num(I) - 1))
                        log_dist(item(I, 1))
                    exps(I)
                    if has(-1):
                        copy_out(item(I, -1))
                    if has(2):
                        copy_turned(item(I, 2))
                    if has(3):
                        norm_in(item(I, 3))
                    if has(2):
                        scale_q(item(I, 2))

                act.wait_ge(S["stage_go"], GO[s])
                log_dist((0, 0))
                norm_in((0, 0), False)
                norm_in((0, 1), False)
                copy_turned((0, 0))
                norm_in((1, 0))
                scale_q((0, 0))
                copy_turned((0, 1))
                scale_q((0, 1))
                steps(act, body)
                copy_out((NB // 2 - 1, 1))

            def turned(s, dst, pad=0):
                def f(t):
                    for j in range(4):
                        act.wait_ge(S["f_T"], nth("f_T", s, 4 * t + j))
                        act.copy(dst(t, j), ps[:, j, 0:P]).then_inc(S["f_xT"], 1)
                return f

            def quant_turned(s, t, w):
                for j in range(4):
                    act.wait_ge(S["f_qT"], nth("f_qT", s, 4 * t + j))
                    act.copy(qT[:, j, 0:w], ps[:, j, 0 if w == FF else 256:][:, 0:w // 2].bitcast(BF16)
                             ).then_inc(S["f_qTs"], 1)

            def hadamard_ffn():
                act.wait_ge(S["stage_go"], GO[10])
                copy = turned(10, lambda t, j: work[:, j, 0:P])
                with act.Fori(0, NB // 4) as t:
                    copy(t)
                    quant_turned(10, t, P)

            def conv_ffn():
                act.wait_ge(S["stage_go"], GO[11])
                copy = turned(11, lambda t, j: xqT[:, j, 1:1 + P])
                with act.Fori(0, NB // 4) as t:
                    copy(t)
                    for j in range(4):
                        act.wait_ge(S["f_mm"], nth("f_mm", 11, 4 * t + j))
                        act.activation(work[:, j, :], ps[:, j, :], ACT.Silu).then_inc(S["f_act"], 1)
                    quant_turned(11, t, FF)

            def expert_ffn():
                act.wait_ge(S["stage_go"], GO[12])
                copy = turned(12, lambda t, j: at(xT_all, 4 * t + j))
                with act.Fori(0, NB // 4) as t:
                    copy(t)
                for u in range(2 * NE):
                    if u >= 2:
                        act.wait_ge(S["f_down"], u - 1)
                    for c in range(FC):
                        act.wait_ge(S["f_up"], u * FC + c + 1)
                        act.activation(hid[:, u % 2, c, :], ps[:, c, :], ACT.Gelu_apprx_tanh,
                                       bias=b1c[:, u // 2, c:c + 1]).then_inc(S["f_gelu"], 1)

            def moe():
                copy = turned(13, lambda t, j: work[:, j, 0:P])
                with act.Fori(0, NB // 4) as t:
                    act.wait_ge(S["f_copied"], 4 * t + 4)
                    copy(t)
                act.wait_ge(S["route_act"], 1)
                act.activation(t2[:], t2[:], ACT.Exp).then_inc(S["route_act"], 1)
                with act.Fori(0, NB // 4) as t:
                    for e in range(NE):
                        n = t * NE + e
                        act.wait_ge(S["f_down"], G0 // FC + n - 1)
                        for c in range(FC):
                            act.wait_ge(S["f_up"], G0 + n * FC + c + 1)
                            act.activation(hid[:, e % 2, c, :], ps[:, c, :], ACT.Gelu).then_inc(S["f_gelu"], 1)

            sqrt_stats(1)
            if LAST >= 0:
                attention(0)
                sqrt_stats(2)
            if LAST >= 0.5:
                hadamard_ffn()
                sqrt_stats(3)
            if LAST >= 1:
                attention(1)
                sqrt_stats(4)
            if LAST >= 1.5:
                conv_ffn()
                sqrt_stats(5)
            if LAST >= 2:
                attention(2)
                sqrt_stats(6)
            if LAST >= 2.5:
                expert_ffn()
                sqrt_stats(7)
            if LAST >= 3:
                attention(3)
                sqrt_stats(8)
            if LAST >= 4:
                sqrt_stats(9)
                attention(4)
                sqrt_stats(10)
                moe()

        @block.vector
        def _(dve):
            chain = [0]

            def link(ins):
                chain[0] += 1
                ins.then_inc(S["dve_step"], 1)
                dve.wait_ge(S["dve_step"], chain[0])

            class Loop:
                def __init__(self, times, per):
                    self.times, self.per, self.base = times, per, chain[0]
                    chain[0] += times * per

                def turn(self, t):
                    self.t, self.k = t, 0

                def mark(self, ins):
                    self.k += 1
                    ins.then_inc(S["dve_step"], 1)

                def hold(self):
                    dve.wait_ge(S["dve_step"], self.base + self.t * self.per + self.k)

                def end(self):
                    assert self.k == self.per, (self.k, self.per)

            go = [0]

            def let_go(ins):
                go[0] += 1
                ins.then_inc(S["stage_go"], 1)

            def finish_stats(n):
                me, mo, ve, vo = stats[:, :, 1], stats[:, :, 4], stats[:, :, 2], stats[:, :, 5]
                link(dve.tensor_tensor(t1[:], ve, vo, ALU.add))
                link(dve.tensor_tensor(t2[:], me, mo, ALU.subtract))
                link(dve.tensor_tensor(t2[:], t2[:], t2[:], ALU.mult))
                link(dve.tensor_scalar(t1[:], t1[:], 1.0 / P, EPS, ALU.mult, ALU.add))
                link(dve.scalar_tensor_tensor(t1[:], t2[:], 0.25, t1[:], ALU.mult, ALU.add))
                dve.tensor_tensor(t2[:], me, mo, ALU.add).then_inc(S["sq_in"], 1)
                dve.wait_ge(S["sq_in"], n)
                dve.wait_ge(S["sq_out"], n)
                link(dve.reciprocal(rstd[:], t1[:]))
                ins = dve.scalar_tensor_tensor(nmr[:], t2[:], -0.5, rstd[:], ALU.mult, ALU.mult)
                link_go(ins)

            def link_go(ins):
                go[0] += 1
                ins.then_inc(S["stage_go"], 1)
                dve.wait_ge(S["stage_go"], go[0])

            def normalise(dst, i, src=x):
                return dve.tensor_scalar(dst, at(src, i), col(rstd, i), col(nmr, i), ALU.mult, ALU.add)

            def bn(i, src=x):
                o = stats[:, i, :] if isinstance(i, int) else stats[:, bass.ds(i, 1), :].rearrange("p a n -> p (a n)")
                return dve.bn_stats(o, at(src, i))

            def all_stats(src):
                with dve.Fori(0, NB) as t:
                    bn(t, src).then_inc(S["dve_step"], 1)
                chain[0] += NB
                dve.wait_ge(S["dve_step"], chain[0])

            dve.wait_ge(S["consts_in"], 16 * N_CONSTS)
            link(dve.tensor_copy(identb[:], cpack[:, 0:P]))
            dve.tensor_copy(causalb[:], xT_all[:, 0:2, :])
            dve.tensor_copy(trib[:], xT_all[:, 2, :])
            dve.tensor_copy(onesb[:], xT_all[:, 3, :])
            dve.tensor_copy(selb[:], xT_all[:, 4:4 + NH, :])
            dve.memset(mparts[:], 0.0)
            dve.memset(vh[:], 1.0)
            dve.memset(vl[:], 0.0)
            dve.memset(xqT[:], 0.0)
            dve.memset(sm[:, 11:12], 1e-9)
            for s in range(5):
                dve.tensor_scalar(cols[:, 2 * s:2 * s + 1], cols[:, 2 * s:2 * s + 1], QSCALE[s], None, ALU.mult)
            link(dve.scalar_tensor_tensor(dscale[:], dscale[:], -1.0, dscale[:], ALU.mult, ALU.min))
            dve.wait_ge(S["weights_in"], 16 * N_WEIGHTS)
            w0, w1, w2 = work[:, 0, 0:P], work[:, 1, :], work[:, 2, :]
            dve.tensor_reduce(sm[:, 0:1], w1, AX.X, ALU.add, apply_absolute_value=True)
            dve.tensor_reduce(sm[:, 1:2], w2, AX.X, ALU.add, apply_absolute_value=True)
            link(dve.tensor_reduce(sm[:, 2:3], w0, AX.X, ALU.add, apply_absolute_value=True))
            link(dve.tensor_scalar(sm[:, 2:3], sm[:, 2:3], 1.0 / P, 1e-5, ALU.mult, ALU.max))
            link(dve.reciprocal(sm[:, 3:4], sm[:, 2:3]))
            dve.tensor_scalar(work[:, 3, 0:P], ident, sm[:, 2:3], None, ALU.mult)
            link(dve.tensor_scalar(work[:, 3, P:2 * P], w0, sm[:, 3:4], 0.5, ALU.mult, ALU.is_gt))
            link(dve.tensor_scalar(work[:, 3, 2 * P:3 * P], w0, sm[:, 3:4], -0.5, ALU.mult, ALU.is_lt))
            dve.tensor_tensor(workb[:, 0, 0:P], work[:, 3, P:2 * P], work[:, 3, 2 * P:3 * P], ALU.subtract
                              ).then_inc(S["setup_dve"], 1)
            dve.wait_ge(S["setup_pe"], 2)
            dve.tensor_copy(ternT, ps[:, 0, 0:64].bitcast(BF16))
            dve.tensor_copy(wscale, ps[:, 1, 0:P])
            link(dve.tensor_scalar(sm[:, 4:6], ps[:, 2, 0:2], 1.0 / (P * FF), 1e-5, ALU.mult, ALU.max))
            link(dve.reciprocal(sm[:, 6:8], sm[:, 4:6]))
            for k, w in ((0, w1), (1, w2)):
                link(dve.tensor_scalar(w, w, sm[:, 6 + k:7 + k], ROUND, ALU.mult, ALU.add))
                link(dve.tensor_scalar(w, w, -ROUND, -1.0, ALU.add, ALU.max))
            link(dve.tensor_scalar(w1, w1, 1.0, sm[:, 4:5], ALU.min, ALU.mult))
            link(dve.tensor_scalar(w2q.rearrange("p c n -> p (c n)"), w2, 1.0, None, ALU.min))
            for k in range(3):
                link(dve.tensor_tensor(wconv[:, k, :], w1, ex[:, 0, k * FF:(k + 1) * FF], ALU.mult))
            dve.wait_ge(S["x_init"], 16)
            all_stats(x)
            finish_stats(1)

            def attention(s):
                nk = nkeys(s)

                def keys(I):
                    t, j = I
                    dve.wait_ge(S["q_ready"], nth("q_ready", s, num(I)))
                    dve.wait_ge(S["proj_ready"], nth("proj_ready", s, num(I)))
                    dve.scalar_tensor_tensor(
                        kblk[:, j, 0:NH * nk].rearrange("p (a n) -> p a n", a=NH), bc(front[:, P:P + nk], NH),
                        cols[:, 2 * s + 1:2 * s + 2], bl(headmask, nk), ALU.add, ALU.mult
                    ).then_inc(S["k_ready"], 1)

                def values_in(I):
                    t, j = I
                    dve.wait_ge(S["vproj_ready"], nth("vproj_ready", s, num(I)))
                    dve.tensor_tensor(vf[0:nk, j, :], front[0:nk, 2 * P:3 * P], rows[0:nk, 0, :], ALU.add
                                      ).then_inc(S["vf_ready"], 1)

                def low_parts(I):
                    t, j = I
                    for c in range(2):
                        dve.wait_ge(S["e_ready"], nth("e_ready", s, num(I), c + 1, 2))
                        e = ex[0:nk, j, c * 1024:(c + 1) * 1024]
                        dve.tensor_tensor(exl[0:nk, j, c * 1024:(c + 1) * 1024], e, high(e), ALU.subtract
                                          ).then_inc(S["el_ready"], 1)

                def maxima(I):
                    t, j = I
                    i = num(I)
                    for g in range(NG):
                        dve.wait_ge(S["a_ready"], nth("a_ready", s, i, g + 1, NG))
                        dve.tensor_reduce(negmax[:, j, HG * g:HG * g + HG],
                                          a_ps[g % 2][:, 0:HG * nk].rearrange("p (a n) -> p a n", a=HG),
                                          AX.X, ALU.max, negate=True).then_inc(S["max_ready"], 1)
                    dve.wait_ge(S["max_ready"], nth("max_ready", s, i, NG, NG))
                    hi, low, whole = mparts[:, j, 0:NH], mparts[:, j, NH:2 * NH], negmax[:, j, :]
                    dve.tensor_copy(hi, whole).then_inc(S["mparts_ready"], 1)
                    dve.wait_ge(S["mparts_ready"], nth("mparts_ready", s, i, 1, 2))
                    dve.tensor_tensor(low, whole, hi, ALU.subtract
                                      ).then_inc(S["mparts_ready"], 1)

                def divide(I):
                    t, j = I
                    i = num(I)
                    pv = back[:, 0:NH * 9].rearrange("p (h e) -> p h e", e=9)
                    dve.wait_ge(S["pv_ready"], nth("pv_ready", s, i))
                    if s == 3:
                        dve.tensor_scalar(rec[:, j, :], pv[:, :, 8], 1e-6, None, ALU.add).then_inc(S["eps_ready"], 1)
                        dve.wait_ge(S["eps_ready"], nth_o(i, 1))
                        dve.reciprocal(rec[:, j, :], rec[:, j, :]).then_inc(S["eps_ready"], 1)
                        dve.wait_ge(S["eps_ready"], nth_o(i, 2))
                        dve.scalar_tensor_tensor(rec[:, j, :], negmax[:, j, :], -MASKED / 2, rec[:, j, :],
                                                 ALU.is_lt, ALU.mult).then_inc(S["eps_ready"], 1)
                        dve.wait_ge(S["eps_ready"], nth_o(i, 3))
                    else:
                        dve.reciprocal(rec[:, j, :], pv[:, :, 8]).then_inc(S["rec_ready"], 1)
                        dve.wait_ge(S["rec_ready"], nth("rec_ready", s, i))
                    dve.tensor_tensor(o_sb[:, j, :].rearrange("p (h e) -> p h e", e=DH), pv[:, :, 0:DH],
                                      bl(rec[:, j, :], DH), ALU.mult).then_inc(S["o_ready"], 1)

                def nth_o(i, k):
                    return i * 3 + k

                def add_out(I):
                    t, j = I
                    i = num(I)
                    if s == 3:
                        dve.wait_ge(S["o_ready"], nth("o_ready", s, i))
                        ins = dve.tensor_tensor(at(x, i), o_sb[:, j, :], at(x, i), ALU.add)
                    elif s < 3:
                        dve.wait_ge(S["wo_ready"], nth("wo_ready", s, i))
                        dve.wait_ge(S["xbo_ready"], nth("xbo_ready", s, i))
                        ins = dve.tensor_tensor(at(x, i), back[:, 272:272 + P], at(x, i), ALU.add)
                    else:
                        dve.wait_ge(S["wo_ready"], nth("wo_ready", s, i))
                        ins = dve.tensor_copy(y_sb[:, j, :], back[:, 272:272 + P])
                    ins.then_inc(S["x_done"], 1)

                def new_stats(I):
                    i = num(I)
                    if s < 4:
                        dve.wait_ge(S["x_done"], nth("x_done", s, i))
                        bn(i).then_inc(S["dve_step"], 1)

                def finish(I, first=False):
                    p = item(I, 0)
                    if s == 4 and not first:
                        dve.wait_ge(S[f"y_out{p[1]}"], 2 * nth_dma("y_out0", 4, p[0] - 1))
                    add_out(p)
                    new_stats(p)

                def body(I, has):
                    if has(-1):
                        low_parts(item(I, -1))
                        divide(item(I, -1))
                    if has(1):
                        values_in(item(I, 1))
                        maxima(item(I, 1))
                    if has(-1):
                        finish(item(I, -1), not has(-3))
                    if has(2):
                        keys(item(I, 2))

                dve.wait_ge(S["stage_w_in"], W_IN[s])
                keys((0, 0))
                values_in((0, 0))
                maxima((0, 0))
                keys((0, 1))
                steps(dve, body)
                end = (NB // 2 - 1, 1)
                low_parts(end)
                divide(end)
                finish(end)
                if s < 4:
                    chain[0] += NB
                    dve.wait_ge(S["dve_step"], chain[0])

            def quantise(L, t, src, scs, lo, hi, dst, s, dequant=False):
                w = src(0).shape[1]
                tmp = lambda j: work[:, j, 0:w] if not dequant else xn[:, j, :]
                for j in range(4):
                    L.mark(dve.tensor_reduce(sc[:, j, 0:1], src(j), AX.X, ALU.max, apply_absolute_value=True))
                L.hold()
                for j in range(4):
                    L.mark(dve.tensor_scalar(sc[:, j, 1:2], sc[:, j, 0:1], 1e-5, 1.0 / hi, ALU.max, ALU.mult))
                L.hold()
                for j in range(4):
                    L.mark(dve.reciprocal(sc[:, j, 2:3], sc[:, j, 1:2]))
                L.hold()
                for j in range(4):
                    L.mark(dve.tensor_scalar(tmp(j), src(j), sc[:, j, 2:3], ROUND, ALU.mult, ALU.add))
                L.hold()
                for j in range(4):
                    L.mark(dve.tensor_scalar(tmp(j), tmp(j), -ROUND, lo, ALU.add, ALU.max))
                L.hold()
                for j in range(4):
                    if dequant:
                        dve.tensor_scalar(dst(j), tmp(j), hi, sc[:, j, 1:2], ALU.min, ALU.mult
                                          ).then_inc(S["f_xn"], 1)
                    else:
                        dve.tensor_scalar(dst(j), tmp(j), hi, None, ALU.min).then_inc(S["f_q"], 1)

            def hadamard_ffn():
                L = Loop(NB // 4, 4 * 5 + 4 + 4 + 4)
                with dve.Fori(0, NB // 4) as t:
                    L.turn(t)
                    for j in range(4):
                        normalise(xn[:, j, :], 4 * t + j).then_inc(S["f_xn"], 1)
                    dve.wait_ge(S["f_mm"], nth("f_mm", 10, 4 * t + 3))
                    quantise(L, t, lambda j: ps[:, j, P:2 * P], None, -8.0, 7.0,
                             lambda j: workb[:, j, 0:P], 10)
                    for j in range(4):
                        dve.wait_ge(S["f_out"], nth("f_out", 10, 4 * t + j))
                        L.mark(dve.scalar_tensor_tensor(work[:, j, P:2 * P], ps[:, j, 384:512], sc[:, j, 1:2],
                                                        wscale, ALU.mult, ALU.mult))
                    L.hold()
                    for j in range(4):
                        L.mark(dve.tensor_tensor(at(x, 4 * t + j), work[:, j, P:2 * P], at(x, 4 * t + j), ALU.add))
                    L.hold()
                    for j in range(4):
                        L.mark(bn(4 * t + j))
                    L.end()
                dve.wait_ge(S["dve_step"], chain[0])

            def conv_ffn():
                L = Loop(NB // 4, 4 + 2 * 4 * 5 + 4 + 4 + 4)
                with dve.Fori(0, NB // 4) as t:
                    L.turn(t)
                    for j in range(4):
                        L.mark(normalise(work[:, j, 0:P], 4 * t + j))
                    L.hold()
                    quantise(L, t, lambda j: work[:, j, 0:P], None, -128.0, 127.0,
                             lambda j: xn[:, j, :], 11, dequant=True)
                    dve.wait_ge(S["f_act"], nth("f_act", 11, 4 * t + 3))
                    quantise(L, t, lambda j: work[:, j, :], None, -128.0, 127.0,
                             lambda j: workb[:, j, :], 11)
                    for j in range(4):
                        L.mark(dve.tensor_scalar(sc[:, j, 3:4], sc[:, j, 1:2], sm[:, 5:6], None, ALU.mult))
                    L.hold()
                    for j in range(4):
                        dve.wait_ge(S["f_out"], nth("f_out", 11, 4 * t + j))
                        L.mark(dve.scalar_tensor_tensor(at(x, 4 * t + j), ps[:, j, 384:512], sc[:, j, 3:4],
                                                        at(x, 4 * t + j), ALU.mult, ALU.add))
                    L.hold()
                    for j in range(4):
                        L.mark(bn(4 * t + j))
                    L.end()
                dve.wait_ge(S["dve_step"], chain[0])

            def expert_ffn():
                with dve.Fori(0, NB // 4) as t:
                    for j in range(4):
                        dve.wait_ge(S["f_T"], nth("f_T", 12, 4 * t + j - 4))
                        normalise(xn[:, j, :], 4 * t + j).then_inc(S["f_xn"], 1)
                for u in range(2 * NE):
                    e, half = u // 2, u % 2
                    dve.wait_ge(S["f_down"], u + 1)
                    dve.tensor_scalar(h_all[:, half * 32:half * 32 + 32, e * 16:e * 16 + 16],
                                      ps[:, 4 + u % 2, :].rearrange("p (b n) -> p b n", n=16),
                                      b2c[:, e:e + 1], None, ALU.add).then_inc(S["f_acc"], 1)
                L = Loop(NB // 4, 8)
                with dve.Fori(0, NB // 4) as t:
                    L.turn(t)
                    for j in range(4):
                        dve.wait_ge(S["f_backT"], 4 * t + j + 1)
                        L.mark(dve.tensor_tensor(at(x, 4 * t + j), ps[:, j, 0:P], at(x, 4 * t + j), ALU.add))
                    L.hold()
                    dve.sem_inc(S["f_back"], 4)
                    for j in range(4):
                        L.mark(bn(4 * t + j))
                    L.end()
                dve.wait_ge(S["dve_step"], chain[0])

            def wide(fn):
                with dve.Fori(0, NB // 4) as t:
                    fn(t).then_inc(S["dve_step"], 1)
                chain[0] += NB // 4
                dve.wait_ge(S["dve_step"], chain[0])

            def hidden_in():
                with dve.Fori(0, NB) as t:
                    normalise(at(h_all, t), t).then_inc(S["dve_step"], 1)
                chain[0] += NB
                dve.wait_ge(S["dve_step"], chain[0])
                all_stats(h_all)
                finish_stats(9)
                with dve.Fori(0, NB) as t:
                    normalise(at(xT_all, t), t, h_all).then_inc(S["dve_step"], 1)
                chain[0] += NB
                dve.wait_ge(S["dve_step"], chain[0])
                dve.wait_ge(S["stage_w_in"], W_IN["ln1"])
                wide(lambda t: dve.tensor_tensor(at4(xT_all, t), at4(xT_all, t), bc(rows[:, 0, :], 4), ALU.mult))
                wide(lambda t: dve.tensor_tensor(at4(xT_all, t), at4(xT_all, t), bc(rows[:, 1, :], 4), ALU.add))
                ins = dve.memset(sm[:, 10:11], 0.0)
                ins.then_inc(S["u_made"], 1)
                dve.wait_ge(S["u_made"], 1)
                link_go(dve.memset(sm[:, 9:10], 0.0))

            def moe():
                dve.wait_ge(S["y_in"], 16)
                wide(lambda t: dve.tensor_tensor(at4(h_all, t), at4(h_all, t), at4(xT_all, t), ALU.add))
                wide(lambda t: dve.tensor_tensor(at4(x, t), at4(x, t), at4(h_all, t), ALU.add))
                all_stats(h_all)
                finish_stats(10)
                dve.wait_ge(S["stage_w_in"], W_IN["ln2"])
                L = Loop(NB // 4, 5)
                with dve.Fori(0, NB // 4) as t:
                    L.turn(t)
                    for j in range(4):
                        dve.wait_ge(S["f_T"], nth("f_T", 13, 4 * t + j - 4))
                        L.mark(normalise(xn[:, j, :], 4 * t + j, h_all))
                    L.hold()
                    L.mark(dve.tensor_tensor(xn[:], xn[:], bc(rows[:, 0, :], 4), ALU.mult))
                    L.hold()
                    dve.tensor_tensor(xn[:], xn[:], bc(rows[:, 1, :], 4), ALU.add).then_inc(S["f_xn"], 4)
                    L.end()
                dve.wait_ge(S["f_lg"], NB)
                dve.wait_ge(S["f_cp"], 2 * NB)
                lg = ps[:, 7, :].rearrange("p (s e) -> p s e", e=NE)
                m1, m2, top = t1[:], t2[:], nmr[:]

                def pick(logits, m, sel):
                    link(dve.tensor_reduce(m, logits, AX.X, ALU.max))
                    link(dve.tensor_tensor(sel, logits, bl(m, NE), ALU.is_ge))
                    link(dve.tensor_tensor(sel, sel, bc(descend, NB), ALU.mult))
                    link(dve.tensor_reduce(top, sel, AX.X, ALU.max))
                    link(dve.tensor_tensor(sel, sel, bl(top, NE), ALU.is_equal))

                pick(lg, m1, ra)
                link(dve.scalar_tensor_tensor(rb, ra, MASKED, lg, ALU.mult, ALU.add))
                pick(rb, m2, rc_)
                link(dve.tensor_tensor(selbf.rearrange("p (s e) -> p s e", e=NE), ra, rc_, ALU.add))
                dve.tensor_tensor(m2, m2, m1, ALU.subtract).then_inc(S["route_dve"], 1)
                dve.wait_ge(S["route_dve"], 1)
                dve.sem_inc(S["route_act"], 1)
                dve.wait_ge(S["route_act"], 2)
                link(dve.tensor_scalar(m1, m2, 1.0, None, ALU.add))
                link(dve.reciprocal(m1, m1))
                link(dve.tensor_tensor(m2, m2, m1, ALU.mult))
                link(dve.tensor_tensor(ra, ra, bl(m1, NE), ALU.mult))
                link(dve.tensor_tensor(rc_, rc_, bl(m2, NE), ALU.mult))
                link(dve.tensor_tensor(coef, ra, rc_, ALU.add))
                dve.wait_ge(S["route_pe"], 1)
                total = ps[:, 1, :].rearrange("p (s e) -> p s e", e=NE)
                link(dve.tensor_copy(ra, total))
                old, new = ra, rb
                k = 1
                while k < NB:
                    link(dve.tensor_tensor(new[:, k:, :], old[:, k:, :], old[:, :NB - k, :], ALU.add))
                    link(dve.tensor_copy(new[:, 0:k, :], old[:, 0:k, :]))
                    old, new = new, old
                    k *= 2
                link(dve.tensor_tensor(new, old, total, ALU.subtract))
                link(dve.tensor_tensor(new, new, ps[:, 0, :].rearrange("p (s e) -> p s e", e=NE), ALU.add))
                link(dve.scalar_tensor_tensor(coef, new, float(CAP), coef, ALU.is_lt, ALU.mult))
                dve.sem_inc(S["route_dve"], 1)
                L = Loop(NB // 4, 4 * NE)
                with dve.Fori(0, NB // 4) as t:
                    L.turn(t)
                    for e in range(NE):
                        dve.wait_ge(S["f_down"], G0 // FC + t * NE + e + 1)
                        for r in range(4):
                            i = 4 * t + r
                            L.mark(dve.scalar_tensor_tensor(
                                at(x, i), ps[:, 4 + e % 2, r * P:(r + 1) * P],
                                coef[:, bass.ds(i, 1), e:e + 1].rearrange("p a n -> p (a n)"), at(x, i),
                                ALU.mult, ALU.add))
                        L.hold()
                        dve.sem_inc(S["f_acc"], 1)
                    L.end()
                link_go(dve.memset(sm[:, 9:10], 0.0))

            if LAST >= 0:
                attention(0)
                finish_stats(2)
            if LAST >= 0.5:
                hadamard_ffn()
                finish_stats(3)
            if LAST >= 1:
                attention(1)
                finish_stats(4)
            if LAST >= 1.5:
                conv_ffn()
                finish_stats(5)
            if LAST >= 2:
                attention(2)
                finish_stats(6)
            if LAST >= 2.5:
                expert_ffn()
                finish_stats(7)
            if LAST >= 3:
                attention(3)
                finish_stats(8)
            if LAST >= 4:
                hidden_in()
                attention(4)
                moe()

        @block.gpsimd
        def _(pool):
            def settled():
                pool.sem_inc(S["pool_step"], 1)

            def attention(s):
                nk = nkeys(s)

                def bias(I, used):
                    t, j = I
                    i = num(I)
                    if s not in (0, 1, 3):
                        return
                    if used:
                        pool.wait_ge(S["b_ready"], nth("b_ready", s, i - 2, 2, 2))
                    if s == 0:
                        pool.wait_ge(S["bln_ready"], nth("bln_ready", s, i))
                        settled()
                        pool.tensor_scalar(biasf[:, j, :], bln[:, j, :], dscale[:, 0:1], None, ALU.mult
                                           ).then_inc(S["biasf_ready"], 1)
                        pool.wait_ge(S["biasf_ready"], nth("biasf_ready", s, i))
                        settled()
                        pool.tensor_copy(biasb[:, j, :], biasf[:, j, :]).then_inc(S["bias_ready"], 1)
                        return
                    pool.wait_ge(S[f"bias_in{j}"], nth_dma("bias_in0", s, t))
                    raw = braw[:, j, :].bitcast(I32) if s == 1 else braw_u[:, j, :]
                    settled()
                    pool.tensor_scalar(biasb[:, j, :], raw, 0.0, MASKED, ALU.is_equal, ALU.mult
                                       ).then_inc(S["bias_ready"], 1)

                def split_v(I):
                    t, j = I
                    v = vf[0:nk, j, :].rearrange("p (h e) -> p h e", e=DH)
                    pool.wait_ge(S["vf_ready"], nth("vf_ready", s, num(I)))
                    settled()
                    pool.tensor_copy(vh[0:nk, j, :, 0:DH], v).then_inc(S["vh_ready"], 1)
                    pool.wait_ge(S["vh_ready"], nth("vh_ready", s, num(I)))
                    pool.tensor_tensor(vl[0:nk, j, :, 0:DH], v, vh[0:nk, j, :, 0:DH], ALU.subtract
                                       ).then_inc(S["vl_ready"], 1)

                def add_bo(I):
                    i = num(I)
                    if s < 3:
                        pool.wait_ge(S["xn_ready"], nth("xn_ready", s, i))
                        pool.tensor_tensor(at(x, i), at(x, i), rows[:, 1, :], ALU.add).then_inc(S["xbo_ready"], 1)
                    if s == 3:
                        pool.wait_ge(S["xn_ready"], nth("xn_ready", s, i))

                def body(I, has):
                    if has(1):
                        bias(item(I, 1), has(-1))
                        split_v(item(I, 1))
                    add_bo(I)

                pool.wait_ge(S["stage_go"], GO[s])
                pool.wait_ge(S["stage_w_in"], W_IN[s])
                bias((0, 0), False)
                split_v((0, 0))
                steps(pool, body)

            def expert_back():
                pool.wait_ge(S["f_acc"], 2 * NE)
                with pool.Fori(0, NB // 4) as t:
                    for j in range(4):
                        pool.wait_ge(S["f_back"], 4 * t + j + 1)
                        settled()
                        pool.tensor_copy(work[:, j, 0:P], at(h_all, 4 * t + j)).then_inc(S["f_cp"], 1)

            def keep_turned():
                with pool.Fori(0, NB // 4) as t:
                    for j in range(4):
                        pool.wait_ge(S["f_xT"], nth("f_xT", 13, 4 * t + j))
                        settled()
                        pool.tensor_copy(at(xT_all, 4 * t + j), work[:, j, 0:P]).then_inc(S["f_cp"], 1)
                    for j in range(4):
                        pool.wait_ge(S["f_cp"], NB + 4 * t + j + 1)
                        pool.wait_ge(S["f_lg"], 4 * t + j + 1)
                        pool.sem_inc(S["f_copied"], 1)

            pool.sem_inc(S["f_back"], 4)
            pool.sem_inc(S["f_copied"], 4)
            if LAST >= 0:
                attention(0)
            if LAST >= 1:
                attention(1)
            if LAST >= 2:
                attention(2)
            if LAST >= 2.5:
                expert_back()
                pool.wait_ge(S["stage_go"], GO[12] + 1)
                pool.sem_inc(S["ffn2_done"], 1)
            if LAST >= 3:
                attention(3)
            if LAST >= 4:
                attention(4)
                keep_turned()


def kernel(**inputs):
    import concourse.bacc as bacc
    from concourse.bass_utils import run_bass_kernel_spmd as run

    a = {n: np.ascontiguousarray(v) for n, v in inputs.items()}
    f = np.float32
    eye = np.eye(P, dtype=f)
    had = np.array([[1.0]])
    while had.shape[0] < P:
        had = np.block([[had, had], [had, -had]])
    had = (had / np.sqrt(P)).astype(f)
    p = np.arange(P)
    headmask = (p[:, None] // DH == np.arange(NH)[None]).astype(f)
    descend = np.broadcast_to(np.arange(NE, 0, -1, dtype=f), (P, NE))
    cpack = np.concatenate([eye, had, np.ones((P, P), f), headmask, descend], axis=1)
    causal2 = np.where(p[None] <= p[:, None], 0.0, MASKED).astype(f)
    causal4 = np.where((p[None] // NB == p[:, None] // NB) & (p[None] <= p[:, None]), 0.0, MASKED).astype(f)
    tri = (p[:, None] < p[None]).astype(f)
    bpack = np.stack([causal2, causal4, tri, np.ones((P, P), f)], axis=1)
    sel = ((p[:, None] < 2 * NH) & (p[:, None] % NH == np.arange(NH)[None])).astype(f)
    selpack = np.ascontiguousarray(np.broadcast_to(sel[:, :, None], (P, NH, P)))
    h = np.arange(P) // DH
    r = (h // 2) * 4 * DH
    e = np.arange(P) % DH
    qkv = a["L3_ffn_qkv_weight"]
    moe_q, moe_k, moe_v = qkv[r + (h % 2) * DH + e], qkv[r + 2 * DH + e], qkv[r + 3 * DH + e]
    z = np.zeros((P, P), f)
    wm = np.stack([np.stack([w.T for w in ws]) for ws in (
        [a["L0_xattn_W" + c] for c in "qkvo"],
        [a["L1_xattn_W_" + c] for c in "qkvo"],
        [a["L2_xattn_W" + c] for c in "qkvo"],
        [a["L3_xattn_W" + c] for c in "qkv"] + [z],
        [moe_q, moe_k, moe_v, a["L3_ffn_proj_weight"]])])
    zr = np.zeros(P, f)
    cols = np.stack([a["L0_xattn_bq"], a["L0_xattn_bk"], a["L1_xattn_b_q"], a["L1_xattn_b_k"], zr, zr,
                     a["L3_xattn_bq"], a["L3_xattn_bk"], zr, zr], axis=1)
    rows = np.stack([np.stack(v) for v in (
        [a["L0_xattn_bv"], a["L0_xattn_bo"]], [a["L1_xattn_b_v"], a["L1_xattn_b_o"]],
        [zr, a["L2_xattn_bo"]], [a["L3_xattn_bv"], zr], [zr, zr],
        [a["L3_ffn_ln1_weight"], a["L3_ffn_ln1_bias"]], [a["L3_ffn_ln2_weight"], a["L3_ffn_ln2_bias"]])])
    arrays = {
        "x": a["x"], "ctx": a["ctx_1024"], "dist": a["fside_BxSxS2_0"],
        "mask1": a["mask_Bx1xSxS2_ik1"].reshape(NB, P, NC), "mask3": a["mask_BxSxS2_bk1"],
        "cpack": cpack, "bpack": bpack, "selpack": selpack, "wm": wm, "cols": cols, "rows": rows,
        "dscale": a["L0_xattn_distance_scaling"].reshape(1, 1), "router": a["L3_ffn_router_weight"],
        "L0_w": a["L0_ffn_weight"], "w1T": a["L1_ffn_w1"].T,
        "w2T": a["L1_ffn_w2"].T.reshape(FC, P, P).transpose(1, 0, 2),
        "convT": a["L1_ffn_conv_w"][:, 0, :].T, "convb": a["L1_ffn_conv_b"].reshape(1, FF),
        "b1c": a["L2_ffn_b1"].reshape(NE, FC, P).transpose(2, 0, 1), "b2c": a["L2_ffn_b2"].T,
        "L2_W1": a["L2_ffn_W1"], "L2_W2": a["L2_ffn_W2"],
        "L3_W1": a["L3_ffn_moe_w1"], "L3_W2": a["L3_ffn_moe_w2"],
    }
    arrays = {n: np.ascontiguousarray(v) for n, v in arrays.items()}
    nc = bacc.Bacc("TRN2", target_bir_lowering=False, num_devices=1)
    d = {n: nc.dram_tensor("in_" + n, v.shape, mybir.dt.from_np(v.dtype), kind="ExternalInput").ap()
         for n, v in arrays.items()}
    out = nc.dram_tensor("out", (NB, P, P), F32, kind="ExternalOutput").ap()
    build(nc, d, out)
    r = run(nc, [{"in_" + n: v for n, v in arrays.items()}], core_ids=[0])
    return r.results[0]["out"]
```

```python
from contextlib import ExitStack

import numpy as np

import concourse.bass as bass
from concourse import mybir

F32 = mybir.dt.float32
BF16 = mybir.dt.bfloat16
F16 = mybir.dt.float16
I32 = mybir.dt.int32
U8 = mybir.dt.uint8
ALU = mybir.AluOpType
ACT = mybir.ActivationFunctionType
AX = mybir.AxisListType

P = 128
NB = 64
NC = 120
NH = 16
DH = P // NH
HG = 4
NG = NH // HG
NE = 8
FF = 512
FC = FF // P
CAP = 2560
EPS = 1e-5
QSCALE = [float(1.0 / np.sqrt(np.float32(w))) for w in (DH, DH, DH, P, DH)]
MASKED = -(2.0 ** 100)
ROUND = 1.5 * 2.0 ** 23

_ORDER = [0, 10, 1, 11, 2, 12, 3, "ln1", "ln1b", 4, 13, "end"]
GO = {s: k + 1 for k, s in enumerate(_ORDER)}
W_IN = {0: 32, 1: 64, 2: 96, 3: 128, "ln1": 144, 4: 176, "ln2": 192}
G0 = 2 * NE * FC


def build(nc, d, out):
    with ExitStack() as ctx:
        def sb(name, shape, dt=F32):
            return ctx.enter_context(nc.sbuf_tensor(name, shape, dt))

        x = sb("x", [P, NB, P])
        h_all = sb("h_all", [P, NB, P])
        xT_all = sb("xT_all", [P, NB, P])
        w1_sb = sb("w1_sb", [P, NE, FF])
        w2_sb = sb("w2_sb", [P, NE, FC, P])
        cpack = sb("cpack", [P, 3 * P + NG + HG + NE + 2])
        ident, hada, onesf = cpack[:, 0:P], cpack[:, P:2 * P], cpack[:, 2 * P:3 * P]
        groupmask, inmask = cpack[:, 3 * P:3 * P + NG], cpack[:, 3 * P + NG:3 * P + NG + HG]
        descend = cpack[:, 3 * P + NG + HG:3 * P + NG + HG + NE]
        behind = cpack[:, 3 * P + NG + HG + NE:]
        identb = sb("identb", [P, P], BF16)
        causalb = sb("causalb", [P, 2, P], BF16)
        trib = sb("trib", [P, P], BF16)
        onesb = sb("onesb", [P, P], BF16)
        selb = sb("selb", [P, NH, P], BF16)
        wm = sb("wm", [P, 4, P])
        cols = sb("cols", [P, 10])
        qscale = sb("qscale", [P, 5, NG])
        qbias = sb("qbias", [P, 5, NG])
        rows = sb("rows", [P, 2, P])
        stats = sb("stats", [P, NB, 6])
        rstd = sb("rstd", [P, NB])
        nmr = sb("nmr", [P, NB])
        t1 = sb("t1", [P, NB])
        t2 = sb("t2", [P, NB])
        dscale = sb("dscale", [P, 1])
        xn = sb("xn", [P, 4, P])
        ctx_sb = sb("ctx_sb", [NC, 2, P])
        braw = sb("braw", [P, 2, NC])
        braw_u = sb("braw_u", [P, 2, NC], U8)
        biasf = sb("biasf", [P, 2, NC])
        biasb = sb("biasb", [P, 2, NC], BF16)
        bias2 = sb("bias2", [P, 2, NC], BF16)
        bias3 = sb("bias3", [P, 2, NC], BF16)
        xcT = sb("xcT", [P, 2, 2 * P])
        qk = sb("qk", [P, 4, FF])
        qgrp = qk[:, 0:2, :].rearrange("p a (g n) -> p a g n", g=NG)
        kblk = qk[:, 2:4, :]
        vf = sb("vf", [P, 2, P])
        vparts = sb("vparts", [P, 2, NH, 3, DH + 1], BF16)
        vleft = sb("vleft", [P, P])
        osum = sb("osum", [P, 2, NH, DH + 1])
        negmax = sb("negmax", [P, 2, NH])
        mparts = sb("mparts", [P, 2, P], BF16)
        mT = sb("mT", [P, 2, P], BF16)
        ex = sb("ex", [P, 2, NH * P])
        exl = sb("exl", [P, 2, NH * P], F16)
        rec = sb("rec", [P, 2, NH])
        o_sb = sb("o_sb", [P, 2, P])
        oT = sb("oT", [P, 2, P])
        y_sb = sb("y_sb", [P, 2, P])
        work = qk[:, :, :]
        workb = exl[:, 0, :].bitcast(BF16).rearrange("p (a n) -> p a n", a=4)
        qT = exl[:, 1, :].bitcast(BF16).rearrange("p (a n) -> p a n", a=4)
        xqT = sb("xqT", [P, 4, P + 2])
        sc = sb("sc", [P, 8, 4])
        nrm4, nT4, round4, scaled4 = (ex[:, k // 2, (k % 2) * 1024:(k % 2 + 1) * 1024]
                                      .rearrange("p (b a n) -> p b a n", b=2, a=4) for k in range(4))
        nrm = ex[:, 0, 0:4 * P].rearrange("p (a n) -> p a n", a=4)
        logs = xT_all[:, :, 0:NC]
        wconv = h_all[:, 0:12, :].rearrange("p a n -> p (a n)").rearrange("p (k n) -> p k n", k=3)
        convb = h_all[0:3, 12:14, :].rearrange("p a n -> p (a n)").bitcast(BF16)
        wscale = h_all[:, 16, :]
        w2q = h_all[:, 17:19, :].rearrange("p a n -> p (a n)").bitcast(BF16).rearrange("p (c n) -> p c n", c=FC)
        ternT = h_all[:, 19, 0:P // 2].bitcast(BF16)
        sm = sb("sm", [P, 12])
        b1c = sb("b1c", [P, NE, FC])
        b2c = sb("b2c", [P, NE])
        router = sb("router", [P, NE])
        coef = xcT[:, :, :].rearrange("p a n -> p (a n)").rearrange("p (b e) -> p b e", e=NE)
        hid = ex[:, :, :].rearrange("p a (c n) -> p a c n", c=FC)
        ra, rb, rc_, rd = (work[:, k, :].rearrange("p (s e) -> p s e", e=NE) for k in range(4))
        selbf = workb[:, 0, :]

        ps = ctx.enter_context(nc.psum_tensor("ps", [P, 8, 512], F32))
        a_ps = [ps[:, 0, :], ps[:, 1, :]]
        b_ps = [ps[:, 2:4, :].rearrange("p a n -> p (a n)"), ps[:, 4:6, :].rearrange("p a n -> p (a n)")]
        front, back = ps[:, 6, :], ps[:, 7, :]
        mT_ps = ps[:, 0, 0:64].bitcast(BF16)
        oT_ps = ps[:, 1, 0:P]

        u_dram = nc.dram_tensor("u_dram", [NB, P, P], F32, kind="Internal").ap()
        y_dram = nc.dram_tensor("y_dram", [NB, P, P], F32, kind="Internal").ap()

        names = """consts_in weights_in stage_w_in u_out ctx_in0 ctx_in1 bias_in0 bias_in1 u_in0 u_in1
            y_out0 y_out1 y_in0 y_in1 y_in2 y_in3 moe_w_in out_done stage_go sq_in sq_out dve_step setup_dve setup_pe
            xn_ready T_ready xcT_ready proj_ready vproj_ready vf_ready v1_ready vleft_ready v2_ready vparts_ready osum_ready el_ready q_ready k_ready bln_ready
            biasf_ready bias_ready bleft_ready bias2_ready bias3_ready a_ready max_ready mparts_ready mT_out mT_ready b_ready e_ready pv_ready rec_ready eps_ready
            o_ready oT_out oT_ready wo_ready xbo_ready x_done
            f_nrm f_o f_scale q0_step scaled qx_step qh_step f_xn f_T f_xT f_mm f_q f_qT f_qTs f_out f_act f_up f_gelu f_down f_acc f_cp f_back f_backT
            f_lg f_copied h_ready un_ready hn_ready hn_scaled u_made y_added x_added x_in0 x_in1 dist_in0 dist_in1 dist_in2 dist_in3 tiny_ready pool_step route_dve route_pe route_act ffn2_done sp_step""".split()
        S = {n: ctx.enter_context(nc.semaphore(n)) for n in names}

        ATT = [0, 1, 2, 3, 4]
        USES = {n: ATT for n in names}
        USES.update({n: [0, 1, 2, 3] for n in ("xn_ready", "xbo_ready", "ctx_in0", "ctx_in1")})
        USES.update({n: [0, 1, 3] for n in ("bias_ready",)})
        USES.update({n: [1, 3] for n in ("bias_in0", "bias_in1")})
        USES.update({n: [0] for n in ("bln_ready", "biasf_ready", "bleft_ready", "bias2_ready", "bias3_ready")})
        USES.update({n: [0, 1, 2, 4] for n in ("oT_out", "oT_ready", "wo_ready", "rec_ready")})
        USES.update({n: [4] for n in ("u_in0", "u_in1", "y_out0", "y_out1")})
        USES.update({n: [10, 11, 12, 13] for n in ("f_T", "f_xT")})
        USES.update({n: [11, 12, 13] for n in ("f_xn",)})
        USES.update({n: [10, 11] for n in ("f_mm", "f_q", "f_qT", "f_qTs", "f_out", "f_nrm", "f_o")})
        USES.update({n: [11] for n in ("f_act", "f_scale")})

        def nth(name, s, i, k=1, n=1):
            return (USES[name].index(s) * NB + i) * n + k

        def nth_dma(name, s, t):
            return 16 * (USES[name].index(s) * (NB // 2) + t + 1)

        def bc(ap, n):
            return ap.unsqueeze(1).to_broadcast([ap.shape[0], n, ap.shape[1]])

        def bl(ap, n):
            return ap.unsqueeze(2).to_broadcast([ap.shape[0], ap.shape[1], n])

        def high(ap):
            return ap.bitcast(BF16).rearrange("p (n two) -> p n two", two=2)[:, :, 1]

        def item(I, k):
            t, j = I
            return t + (j + k) // 2, (j + k) % 2

        def num(I):
            return 2 * I[0] + I[1]

        def at(tensor, i):
            if isinstance(i, int):
                return tensor[:, i, :]
            return tensor[:, bass.ds(i, 1), :].rearrange("p a n -> p (a n)")

        def at4(tensor, t):
            return tensor[:, bass.ds(4 * t, 4), :]

        def col(tensor, i):
            return tensor[:, bass.ds(i, 1)]

        def steps(eng, body, n=NB, before=0, after=2):
            def peeled(i):
                body((i // 2, i % 2), lambda k: 0 <= i + k < n)

            for i in range(-before, 2):
                peeled(i)
            turns = (n - 6) // 4
            with eng.Fori(0, turns) as t:
                for k in range(2, 6):
                    body((2 * t + k // 2, k % 2), lambda k: True)
            for i in range(2 + 4 * turns, n + after):
                peeled(i)

        def nkeys(s):
            return P if s == 4 else NC

        block = ctx.enter_context(nc.Block())

        N_CONSTS, N_WEIGHTS = 6, 9

        @block.sync
        def _(sp):
            sp.dma_start(cpack[:], d["cpack"]).then_inc(S["consts_in"], 16)
            sp.dma_start(h_all[:, 32:36, :], d["bpack"]).then_inc(S["consts_in"], 16)
            sp.dma_start(h_all[:, 36:36 + NH, :], d["selpack"]).then_inc(S["consts_in"], 16)
            sp.dma_start(cols[:], d["cols"]).then_inc(S["consts_in"], 16)
            sp.dma_start(dscale[:], d["dscale"].to_broadcast([P, 1])).then_inc(S["consts_in"], 16)
            sp.dma_start(router[:], d["router"]).then_inc(S["consts_in"], 16)
            for c in range(2):
                part = slice(c * NB // 2, (c + 1) * NB // 2)
                sp.dma_start(x[:, part, :], d["x"][part].rearrange("b s n -> s b n")).then_inc(S[f"x_in{c}"], 16)
            sp.dma_start(work[:, 0, 0:P], d["L0_w"]).then_inc(S["weights_in"], 16)
            sp.dma_start(work[:, 1, :], d["w1T"]).then_inc(S["weights_in"], 16)
            sp.dma_start(work[:, 2, :].rearrange("p (c n) -> p c n", c=FC), d["w2T"]).then_inc(S["weights_in"], 16)
            for k in range(3):
                sp.dma_start(ex[:, 0, k * FF:(k + 1) * FF],
                             d["convT"][k:k + 1, :].to_broadcast([P, FF])).then_inc(S["weights_in"], 16)
            sp.dma_start(ex[0:3, 1, 0:FF], d["convb"].to_broadcast([3, FF])).then_inc(S["weights_in"], 16)
            sp.dma_start(b1c[:], d["b1c"]).then_inc(S["weights_in"], 16)
            sp.dma_start(b2c[:], d["b2c"]).then_inc(S["weights_in"], 16)
            for c in range(4):
                part = slice(c * NB // 4, (c + 1) * NB // 4)
                sp.dma_start(logs[:, part, :], d["dist"][part].rearrange("b q k -> q b k")
                             ).then_inc(S[f"dist_in{c}"], 16)
            sp.dma_start(w1_sb[:], d["L2_W1"].rearrange("e p f -> p e f")).then_inc(S["moe_w_in"], 16)
            for e in range(NE):
                sp.dma_start(w2_sb[:, e, :, :],
                             d["L2_W2"][e].rearrange("(c p) n -> p c n", p=P)).then_inc(S["moe_w_in"], 16)

            def att_loads(s, I):
                t, j = I
                if s < 4:
                    sp.dma_start(ctx_sb[:, j, :], d["ctx"][bass.ds(num(I), 1)].rearrange("a k n -> (a k) n")
                                 ).then_inc(S[f"ctx_in{j}"], 16)
                if s == 1:
                    sp.dma_start(braw[:, j, :].bitcast(I32), d["mask1"][bass.ds(num(I), 1)].rearrange("a q k -> (a q) k")
                                 ).then_inc(S[f"bias_in{j}"], 16)
                if s == 3:
                    sp.dma_start(braw_u[:, j, :], d["mask3"][bass.ds(num(I), 1)].rearrange("a q k -> (a q) k")
                                 ).then_inc(S[f"bias_in{j}"], 16)
                if s == 4:
                    for c in range(2):
                        sp.dma_start(xn[c * NB:(c + 1) * NB, j, :],
                                     u_dram[:, bass.ds(2 * num(I) + c, 1), :].rearrange("s a n -> s (a n)")
                                     ).then_inc(S[f"u_in{j}"], 16)

            def attention(s):
                if s:
                    sp.wait_ge(S["stage_go"], GO[s])
                sp.dma_start(wm[:], d["wm"][s].rearrange("m p n -> p m n")).then_inc(S["stage_w_in"], 16)
                sp.dma_start(rows[:], d["rows"][s].unsqueeze(0).to_broadcast([P, 2, P])).then_inc(S["stage_w_in"], 16)
                if s == 4:
                    sp.wait_ge(S["u_out"], 64)
                att_loads(s, (0, 0))
                att_loads(s, (0, 1))

                def reload(I):
                    i = num(I)
                    sp.wait_ge(S["T_ready"], nth("T_ready", s, i))
                    sp.sem_inc(S["sp_step"], 1)
                    if s in (1, 3):
                        sp.wait_ge(S["bias_ready"], nth("bias_ready", s, i))
                    sp.sem_inc(S["sp_step"], 1)
                    att_loads(s, item(I, 2))

                reload((0, 0))

                def body(I, has):
                    if has(3):
                        reload(item(I, 1))
                    if has(-2) and s == 4:
                        store_y(item(I, -2))

                def store_y(I):
                    sp.wait_ge(S["x_done"], nth("x_done", s, num(I)))
                    sp.sem_inc(S["sp_step"], 1)
                    for c in range(2):
                        sp.dma_start(y_dram[:, bass.ds(2 * num(I) + c, 1), :].rearrange("s a n -> s (a n)"),
                                     y_sb[c * NB:(c + 1) * NB, I[1], :]).then_inc(S[f"y_out{I[1]}"], 16)

                steps(sp, body)

            for s in range(4):
                attention(s)
            sp.wait_ge(S["ffn2_done"], 1)
            sp.dma_start(w1_sb[:], d["L3_W1"].rearrange("e p f -> p e f")).then_inc(S["moe_w_in"], 16)
            for e in range(NE):
                sp.dma_start(w2_sb[:, e, :, :],
                             d["L3_W2"][e].rearrange("(c p) n -> p c n", p=P)).then_inc(S["moe_w_in"], 16)
            sp.wait_ge(S["stage_go"], GO["ln1"])
            sp.dma_start(rows[:], d["rows"][5].unsqueeze(0).to_broadcast([P, 2, P])).then_inc(S["stage_w_in"], 16)
            for c in range(4):
                sp.wait_ge(S["u_made"], NB // 16 * (c + 1))
                part = slice(c * NB // 4, (c + 1) * NB // 4)
                sp.dma_start(u_dram[part].rearrange("s b n -> b s n"), xT_all[:, part, :]).then_inc(S["u_out"], 16)
            attention(4)
            for j in range(2):
                sp.wait_ge(S[f"y_out{j}"], 2 * nth_dma("y_out0", 4, NB // 2 - 1))
            sp.dma_start(rows[:], d["rows"][6].unsqueeze(0).to_broadcast([P, 2, P])).then_inc(S["stage_w_in"], 16)
            for c in range(4):
                part = slice(c * NB // 4, (c + 1) * NB // 4)
                sp.dma_start(xT_all[:, part, :], y_dram[part].rearrange("s b n -> b s n")).then_inc(S[f"y_in{c}"], 16)
            sp.wait_ge(S["stage_go"], GO["end"])
            sp.dma_start(out.rearrange("b s n -> s b n"), x[:]).then_inc(S["out_done"], 16)
            sp.wait_ge(S["out_done"], 16)

        @block.tensor
        def _(pe):
            pe.wait_ge(S["setup_dve"], 1)
            pe.transpose(ps[:, 0, 0:64].bitcast(BF16), workb[:, 0, 0:P], identb[:]).then_inc(S["setup_pe"], 1)
            pe.matmul(ps[:, 1, 0:P], onesf, work[:, 3, 0:P], start=True, stop=True)
            pe.matmul(ps[:, 2, 0:2], onesf, sm[:, 0:2], start=True, stop=True).then_inc(S["setup_pe"], 1)

            def attention(s):
                nk = nkeys(s)
                bias = {0: biasb, 1: biasb, 3: biasb}.get(s)

                def turn(I, first=False, out_read=False):
                    t, j = I
                    i = num(I)
                    if out_read and s != 3:
                        pe.wait_ge(S["x_done"], nth("x_done", s, i - 4))
                    if not first:
                        pe.wait_ge(S["vf_ready"], nth("vf_ready", s, i - 1))
                    if s < 4:
                        pe.wait_ge(S["xn_ready"], nth("xn_ready", s, i))
                        pe.wait_ge(S[f"ctx_in{j}"], nth_dma("ctx_in0", s, t))
                    else:
                        pe.wait_ge(S[f"u_in{j}"], 2 * nth_dma("u_in0", s, t))
                    mm = pe.transpose(front[:, 0:P], xn[:, j, :], ident)
                    if s < 4:
                        mm = pe.transpose(front[:, P:P + NC], ctx_sb[:, j, :], ident[0:NC, 0:NC])
                    mm.then_inc(S["T_ready"], 1)

                def kv_src(j):
                    return xcT[:, j, 0:P] if s == 4 else xcT[:, j, P:P + NC]

                def project(I):
                    t, j = I
                    pe.wait_ge(S["xcT_ready"], nth("xcT_ready", s, num(I)))
                    pe.matmul(front[:, 0:P], wm[:, 0, :], xcT[:, j, 0:P], start=True, stop=True)
                    pe.matmul(front[:, P:P + nk], wm[:, 1, :], kv_src(j), start=True, stop=True
                              ).then_inc(S["proj_ready"], 1)

                def project_v(I):
                    t, j = I
                    pe.wait_ge(S["q_ready"], nth("q_ready", s, num(I)))
                    pe.wait_ge(S["k_ready"], nth("k_ready", s, num(I)))
                    pe.matmul(front[0:nk, 2 * P:3 * P], kv_src(j), wm[:, 2, :], start=True, stop=True
                              ).then_inc(S["vproj_ready"], 1)

                def scores_by_query(I, first, groups):
                    t, j = I
                    i = num(I)
                    if 0 in groups:
                        pe.wait_ge(S["q_ready"], nth("q_ready", s, i))
                        pe.wait_ge(S["k_ready"], nth("k_ready", s, i))
                        if bias is not None:
                            pe.wait_ge(S["bias_ready"], nth("bias_ready", s, i))
                    b = biasb[:, j, 0:nk] if bias is not None else causalb[:, (0 if s == 2 else 1), 0:nk]
                    for g in groups:
                        if not (first and g < 2):
                            pe.wait_ge(S["max_ready"], nth("max_ready", s, i, g - 1, NG))
                        pe.matmul(a_ps[g % 2][:, 0:HG * nk], identb[:], bc(b, HG), start=True, stop=False)
                        pe.matmul(a_ps[g % 2][:, 0:HG * nk], high(qgrp[:, j, g, :]),
                                  high(kblk[:, j, 0:HG * nk]), start=False, stop=True
                                  ).then_inc(S["a_ready"], 1)

                def turn_max(I):
                    t, j = I
                    pe.wait_ge(S["mparts_ready"], nth("mparts_ready", s, num(I), 2, 2))
                    pe.transpose(mT_ps, mparts[:, j, :], identb[:]).then_inc(S["mT_out"], 1)

                def scores_by_key(I, first, k):
                    t, j = I
                    i = num(I)
                    if s == 0 and k == 0:
                        pe.wait_ge(S["bias3_ready"], nth("bias3_ready", s, i))
                    if k % 2 == 0 and not first:
                        pe.wait_ge(S["e_ready"], nth("e_ready", s, i - 1, k // 2 + 1, 2))
                    o = b_ps[k // 2][0:nk, (k % 2) * 512:(k % 2) * 512 + 512]
                    b = biasb[:, j, 0:nk] if bias is not None else causalb[:, (0 if s == 2 else 1), 0:nk]
                    pe.matmul(o, b, bc(identb[:], NG), start=True, stop=False, skip_group_check=True)
                    if s == 0:
                        for part in (bias2, bias3):
                            pe.matmul(o, part[:, j, :], bc(identb[:], NG), start=False, stop=False,
                                      skip_group_check=True)
                    pe.matmul(o, kblk[:, j, k * nk:(k + 1) * nk], qgrp[:, j, :, :], start=False, stop=False,
                              skip_group_check=True)

                def less_max(I, k):
                    t, j = I
                    if k == 0:
                        pe.wait_ge(S["mT_ready"], nth("mT_ready", s, num(I)))
                    o = b_ps[k // 2][0:nk, (k % 2) * 512:(k % 2) * 512 + 512]
                    for g in range(NG):
                        mm = pe.matmul(o[:, g * P:(g + 1) * P], selb[:, HG * g + k, 0:nk], mT[:, j, :],
                                       start=False, stop=True, skip_group_check=True)
                    if k % 2:
                        mm.then_inc(S["b_ready"], 1)

                def values(I, first, half):
                    t, j = I
                    i = num(I)
                    if half == 0:
                        pe.wait_ge(S["vparts_ready"], nth("vparts_ready", s, i))
                        if not first:
                            pe.wait_ge(S["osum_ready"], nth("osum_ready", s, i - 1))
                    pe.wait_ge(S["el_ready"], nth("el_ready", s, i, half + 1, 2))
                    for block in range(8 * half, 8 * half + 8):
                        h = block % NG * HG + block // NG
                        o, q = back[:, h * 27:h * 27 + 27], slice(block * P, (block + 1) * P)
                        v = vparts[0:nk, j, h, :, :].rearrange("p a e -> p (a e)")
                        pe.matmul(o, high(ex[0:nk, j, q]), v, start=True, stop=False)
                        mm = pe.matmul(o, exl[0:nk, j, q], v, start=False, stop=True)
                    if half:
                        mm.then_inc(S["pv_ready"], 1)

                def turn_out(I):
                    if s == 3:
                        return
                    t, j = I
                    pe.wait_ge(S["o_ready"], nth("o_ready", s, num(I)))
                    pe.transpose(oT_ps, o_sb[:, j, :], ident).then_inc(S["oT_out"], 1)

                def project_out(I):
                    if s == 3:
                        return
                    t, j = I
                    pe.wait_ge(S["oT_ready"], nth("oT_ready", s, num(I)))
                    pe.matmul(front[:, 3 * P:4 * P], oT[:, j, :], wm[:, 3, :], start=True, stop=True
                              ).then_inc(S["wo_ready"], 1)

                def body(I, has):
                    now, done, last, nxt, far = I, item(I, -2), item(I, -1), item(I, 1), item(I, 2)
                    first = not has(-1)
                    if has(0):
                        scores_by_key(now, first, 0)
                        turn_max(now)
                        scores_by_key(now, first, 1)
                    if has(-2):
                        turn_out(done)
                    if has(0):
                        less_max(now, 0)
                        less_max(now, 1)
                        scores_by_key(now, first, 2)
                    if has(1):
                        project_v(nxt)
                    if has(-2):
                        project_out(done)
                    if has(1):
                        scores_by_query(nxt, False, (0, 1))
                    if has(0):
                        less_max(now, 2)
                    if has(-1):
                        values(last, not has(-2), 0)
                    if has(2):
                        turn(far, False, has(-2))
                    if has(0):
                        scores_by_key(now, first, 3)
                        less_max(now, 3)
                    if has(1):
                        scores_by_query(nxt, False, (2, 3))
                    if has(2):
                        project(far)
                    if has(-1):
                        values(last, not has(-2), 1)

                pe.wait_ge(S["stage_go"], GO[s])
                pe.wait_ge(S["stage_w_in"], W_IN[s])
                turn((0, 0), True)
                project((0, 0))
                project_v((0, 0))
                scores_by_query((0, 0), True, range(NG))
                turn((0, 1))
                project((0, 1))
                steps(pe, body)

            def wait4(name, s, t, j, back_by=0):
                pe.wait_ge(S[name], nth(name, s, 4 * t + j - back_by))

            def hadamard_ffn():
                def four(name, I, k=3):
                    pe.wait_ge(S[name], nth(name, 10, 4 * num(I) + k))

                def turn(I, used):
                    if used:
                        four("f_xT", item(I, -1))
                    for k in range(4):
                        four("f_nrm", I, k)
                        pe.transpose(ps[:, 0, k * P:(k + 1) * P], nrm4[:, I[1], k, :], ident).then_inc(S["f_T"], 1)

                def rotate(I, used):
                    if used:
                        four("f_q", item(I, -2))
                    for k in range(4):
                        four("f_xT", I, k)
                        pe.matmul(ps[:, 1 + I[1], k * P:(k + 1) * P], nT4[:, I[1], k, :], hada,
                                  start=True, stop=True).then_inc(S["f_mm"], 1)

                def turn_rounded(I, used):
                    if used:
                        four("f_qTs", item(I, -1))
                    for k in range(4):
                        four("f_q", I, k)
                        pe.transpose(ps[:, 3, k * 64:(k + 1) * 64].bitcast(BF16),
                                     workb[:, k, I[1] * P:(I[1] + 1) * P], identb[:]).then_inc(S["f_qT"], 1)

                def down(I, used):
                    if used:
                        four("f_o", item(I, -1))
                    for k in range(4):
                        four("f_qTs", I, k)
                        pe.matmul(ps[:, 4, k * P:(k + 1) * P], qT[:, k, I[1] * P:(I[1] + 1) * P], ternT,
                                  start=True, stop=True).then_inc(S["f_out"], 1)

                def body(I, has):
                    if has(1):
                        rotate(item(I, 1), has(-1))
                    if has(2):
                        turn(item(I, 2), has(1))
                    if has(0):
                        turn_rounded(I, has(-1))
                        down(I, has(-1))

                pe.wait_ge(S["stage_go"], GO[10])
                steps(pe, body, NB // 4, 3, 1)

            def pair(name, I, k=1):
                pe.wait_ge(S[name], nth(name, 11, 2 * num(I) + k))

            def conv_ffn():
                def turn(I, used):
                    for k in range(2):
                        pair("f_xn", I, k)
                        if used and not k:
                            pair("f_xT", item(I, -1))
                        pe.transpose(ps[:, 6, k * P:(k + 1) * P], xn[:, 2 * I[1] + k, :], ident
                                     ).then_inc(S["f_T"], 1)

                def conv(I, used):
                    for k in range(2):
                        j = 2 * I[1] + k
                        pair("f_xT", I, k)
                        if used:
                            pair("f_act", item(I, -2), k)
                        pe.matmul(ps[:, j, :], onesb[0:3, :], convb, start=True, stop=False)
                        for tap in range(3):
                            mm = pe.matmul(ps[:, j, :], xqT[:, j, tap:tap + P], wconv[:, tap, :],
                                           start=False, stop=tap == 2)
                        mm.then_inc(S["f_mm"], 1)

                def turn_hidden(I, used):
                    for k in range(2):
                        pair("f_q", I, k)
                        if used and not k:
                            pair("f_qTs", item(I, -1))
                        for c in range(FC):
                            mm = pe.transpose(ps[:, 4, 256 * k + 64 * c:256 * k + 64 * c + 64].bitcast(BF16),
                                              workb[:, 2 * I[1] + k, c * P:(c + 1) * P], identb[:])
                        mm.then_inc(S["f_qT"], 1)

                def down(I, used):
                    for k in range(2):
                        pair("f_qTs", I, k)
                        if used and not k:
                            pair("f_o", item(I, -1))
                        for c in range(FC):
                            mm = pe.matmul(ps[:, 5, k * P:(k + 1) * P], qT[:, 2 * I[1] + k, c * P:(c + 1) * P],
                                           w2q[:, c, :], start=c == 0, stop=c == FC - 1)
                        mm.then_inc(S["f_out"], 1)

                def body(I, has):
                    if has(1):
                        conv(item(I, 1), has(-1))
                    if has(0):
                        turn_hidden(I, has(-1))
                    if has(2):
                        turn(item(I, 2), has(1))
                    if has(0):
                        down(I, has(-1))

                pe.wait_ge(S["stage_go"], GO[11])
                steps(pe, body, NB // 2, 3, 1)

            def expert_ffn():
                def turn(t, bank):
                    for j in range(4):
                        wait4("f_xn", 12, t, j)
                        if bank is None:
                            wait4("f_xT", 12, t, j, 4)
                        elif not j:
                            wait4("f_xT", 12, t, 3, 4)
                        o = ps[:, j, 0:P] if bank is None else ps[:, bank, j * P:(j + 1) * P]
                        pe.transpose(o, xn[:, j, :], ident).then_inc(S["f_T"], 1)

                def turn_back(t):
                    for j in range(4):
                        pe.wait_ge(S["f_cp"], 4 * t + 4)
                        pe.transpose(ps[:, 7, j * P:(j + 1) * P], work[:, j, 0:P], ident
                                     ).then_inc(S["f_backT"], 1)

                pe.wait_ge(S["stage_go"], GO[12])
                with pe.Fori(0, NB // 8) as t:
                    turn(t, None)
                pe.wait_ge(S["f_xT"], nth("f_xT", 12, NB // 2 - 1))
                pe.wait_ge(S["moe_w_in"], 16 * (NE + 1))
                units = [(e, half) for half in range(2) for e in range(NE)]

                def up(u):
                    e, half = units[u]
                    rhs = xT_all[:, half * 32:half * 32 + 32, e * 16:e * 16 + 16]
                    for c in range(FC):
                        if u:
                            pe.wait_ge(S["f_gelu"], (u - 1) * FC + c + 1)
                        pe.matmul(ps[:, c, :], w1_sb[:, e, c * P:(c + 1) * P], rhs, start=True, stop=True
                                  ).then_inc(S["f_up"], 1)

                def down(u):
                    e, half = units[u]
                    if u >= 2:
                        pe.wait_ge(S["f_acc"], u - 1)
                    for c in range(FC):
                        pe.wait_ge(S["f_gelu"], u * FC + c + 1)
                        mm = pe.matmul(ps[:, 4 + u % 2, :], w2_sb[:, e, c, :], hid[:, u % 2, c, :],
                                       start=c == 0, stop=c == FC - 1)
                    mm.then_inc(S["f_down"], 1)

                up(0)
                for u in range(2 * NE):
                    if u < NE:
                        turn(NB // 8 + u, 6)
                    if u == NE - 1:
                        pe.wait_ge(S["f_xT"], nth("f_xT", 12, NB - 1))
                    if u + 1 < 2 * NE:
                        up(u + 1)
                    down(u)
                    if u >= NE:
                        turn_back(u - NE)
                with pe.Fori(NB // 8, NB // 4) as t:
                    turn_back(t)

            def moe():
                turn_all_moe()
                def rank():
                    pe.wait_ge(S["route_dve"], 1)
                    pe.matmul(ps[:, 6, :], trib[:], selbf, start=True, stop=True)
                    pe.matmul(ps[:, 7, :], onesb[:], selbf, start=True, stop=True).then_inc(S["route_pe"], 1)

                pe.wait_ge(S["f_cp"], 2 * NB)
                pe.wait_ge(S["moe_w_in"], 16 * (2 * NE + 2))

                def up(t, e):
                    rhs = at4(xT_all, t).rearrange("p a n -> p (a n)")
                    n = t * (NE * FC) + e * FC
                    for c in range(FC):
                        pe.wait_ge(S["f_gelu"], G0 + n + c + 1 - FC)
                        pe.matmul(ps[:, c, :], w1_sb[:, e, c * P:(c + 1) * P], rhs, start=True, stop=True
                                  ).then_inc(S["f_up"], 1)

                def down(t, e):
                    n = t * NE + e
                    pe.wait_ge(S["f_acc"], G0 // FC + n - 1)
                    pe.wait_ge(S["f_gelu"], G0 + (n + 1) * FC)
                    for r in range(4):
                        for c in range(FC):
                            mm = pe.matmul(ps[:, 4 + e % 2, r * P:(r + 1) * P], hid[:, e % 2, c, r * P:(r + 1) * P],
                                           w2_sb[:, e, c, :], start=c == 0, stop=c == FC - 1)
                    mm.then_inc(S["f_down"], 1)

                def group(t, between=None):
                    up(t, 0)
                    if between:
                        between()
                    for e in range(NE):
                        if e + 1 < NE:
                            up(t, e + 1)
                        down(t, e)

                group(0, rank)
                with pe.Fori(1, NB // 4) as t:
                    group(t)

            def turn_all_moe():
                with pe.Fori(0, NB // 4) as t:
                    for j in range(4):
                        wait4("f_xn", 13, t, j)
                        wait4("f_xT", 13, t, j, 4)
                        pe.transpose(ps[:, j, 0:P], xn[:, j, :], ident).then_inc(S["f_T"], 1)
                    for j in range(4):
                        wait4("f_xT", 13, t, j)
                        pe.matmul(ps[:, 7, bass.ds((4 * t + j) * NE, NE)], work[:, j, 0:P], router[:],
                                  start=True, stop=True).then_inc(S["f_lg"], 1)

            attention(0)
            hadamard_ffn()
            attention(1)
            conv_ffn()
            attention(2)
            expert_ffn()
            attention(3)
            attention(4)
            moe()

        @block.scalar
        def _(act):
            def sqrt_stats(n):
                act.wait_ge(S["sq_in"], n)
                act.activation(t1[:], t1[:], ACT.Sqrt).then_inc(S["sq_out"], 1)

            def attention(s):
                nk = nkeys(s)

                def copy_turned(I):
                    t, j = I
                    act.wait_ge(S["T_ready"], nth("T_ready", s, num(I)))
                    w = P if s == 4 else P + NC
                    act.copy(xcT[:, j, 0:w], front[:, 0:w]).then_inc(S["xcT_ready"], 1)

                def scale_q(I):
                    t, j = I
                    act.wait_ge(S["proj_ready"], nth("proj_ready", s, num(I)))
                    for g in range(NG):
                        ins = act.activation(qgrp[:, j, g, :], front[:, 0:P], ACT.Identity,
                                             bias=qbias[:, s, g:g + 1], scale=qscale[:, s, g:g + 1])
                    ins.then_inc(S["q_ready"], 1)

                def copy_max(I):
                    t, j = I
                    act.wait_ge(S["mT_out"], nth("mT_out", s, num(I)))
                    act.copy(mT[:, j, :], mT_ps).then_inc(S["mT_ready"], 1)

                def exps(I, c):
                    t, j = I
                    act.wait_ge(S["b_ready"], nth("b_ready", s, num(I), c + 1, 2))
                    act.activation(ex[0:nk, j, c * 1024:(c + 1) * 1024], b_ps[c][0:nk, :], ACT.Exp
                                   ).then_inc(S["e_ready"], 1)

                def copy_out(I):
                    t, j = I
                    if s == 3:
                        return
                    act.wait_ge(S["oT_out"], nth("oT_out", s, num(I)))
                    act.copy(oT[:, j, :], oT_ps).then_inc(S["oT_ready"], 1)

                def norm_in(I, wait=True):
                    t, j = I
                    if s == 4:
                        return
                    if wait:
                        act.wait_ge(S["T_ready"], nth("T_ready", s, num(I) - 2))
                    act.activation(xn[:, j, :], at(x, num(I)), ACT.Identity, bias=col(nmr, num(I)),
                                   scale=col(rstd, num(I))).then_inc(S["xn_ready"], 1)

                def body(I, has):
                    if has(0):
                        copy_max(I)
                    if has(-2):
                        copy_out(item(I, -2))
                    if has(0):
                        exps(I, 0)
                    if has(3):
                        norm_in(item(I, 3))
                    if has(2):
                        copy_turned(item(I, 2))
                    if has(0):
                        exps(I, 1)
                    if has(2):
                        scale_q(item(I, 2))

                act.wait_ge(S["stage_go"], GO[s])
                norm_in((0, 0), False)
                norm_in((0, 1), False)
                copy_turned((0, 0))
                norm_in((1, 0))
                scale_q((0, 0))
                copy_turned((0, 1))
                scale_q((0, 1))
                steps(act, body)

            def turned(s, dst):
                def f(t):
                    for j in range(4):
                        act.wait_ge(S["f_T"], nth("f_T", s, 4 * t + j))
                        act.copy(dst(t, j), ps[:, j, 0:P]).then_inc(S["f_xT"], 1)
                return f

            def hadamard_ffn():
                def four(name, I, k=3):
                    act.wait_ge(S[name], nth(name, 10, 4 * num(I) + k))

                def body(I, has):
                    if has(3):
                        new = item(I, 3)
                        if has(1):
                            four("f_T", item(I, 1))
                        for k in range(4):
                            i = 4 * num(new) + k
                            act.activation(nrm4[:, new[1], k, :], at(x, i), ACT.Identity, bias=col(nmr, i),
                                           scale=col(rstd, i)).then_inc(S["f_nrm"], 1)
                    if has(2):
                        far = item(I, 2)
                        four("f_T", far)
                        if has(0):
                            four("f_mm", I)
                        for k in range(4):
                            act.copy(nT4[:, far[1], k, :], ps[:, 0, k * P:(k + 1) * P]).then_inc(S["f_xT"], 1)
                    if has(0):
                        four("f_qT", I)
                        if has(-2):
                            four("f_out", item(I, -2))
                        for k in range(4):
                            act.copy(qT[:, k, I[1] * P:(I[1] + 1) * P], ps[:, 3, k * 64:(k + 1) * 64].bitcast(BF16)
                                     ).then_inc(S["f_qTs"], 1)

                act.wait_ge(S["stage_go"], GO[10])
                steps(act, body, NB // 4, 3, 1)

            def conv_ffn():
                def pair(name, I, k=1):
                    act.wait_ge(S[name], nth(name, 11, 2 * num(I) + k))

                def norm(I, used):
                    for k in range(2):
                        i = 2 * num(I) + k
                        if used:
                            pair("f_xn", item(I, -2), k)
                        act.activation(nrm[:, 2 * I[1] + k, :], at(x, i), ACT.Identity, bias=col(nmr, i),
                                       scale=col(rstd, i)).then_inc(S["f_nrm"], 1)

                def body(I, has):
                    if has(3):
                        norm(item(I, 3), has(1))
                    if has(1):
                        nxt = item(I, 1)
                        for k in range(2):
                            if has(-1):
                                pair("f_q", item(I, -1), k)
                            pair("f_mm", nxt, k)
                            act.activation(work[:, 2 * nxt[1] + k, :], ps[:, 2 * nxt[1] + k, :], ACT.Silu
                                           ).then_inc(S["f_act"], 1)
                    if has(0):
                        for k in range(2):
                            pair("f_qT", I)
                            if has(-2):
                                pair("f_out", item(I, -2), k)
                            act.copy(qT[:, 2 * I[1] + k, :], ps[:, 4, 256 * k:256 * k + 256].bitcast(BF16)
                                     ).then_inc(S["f_qTs"], 1)
                    if has(2):
                        far = item(I, 2)
                        for k in range(2):
                            pair("f_T", far)
                            if has(0):
                                pair("f_mm", I, k)
                            act.copy(xqT[:, 2 * far[1] + k, 1:1 + P], ps[:, 6, k * P:(k + 1) * P]
                                     ).then_inc(S["f_xT"], 1)

                act.wait_ge(S["stage_go"], GO[11])
                steps(act, body, NB // 2, 3, 1)

            def expert_ffn():
                act.wait_ge(S["stage_go"], GO[12])
                copy = turned(12, lambda t, j: at(xT_all, 4 * t + j))
                with act.Fori(0, NB // 8) as t:
                    copy(t)
                for u in range(2 * NE):
                    if u >= 2:
                        act.wait_ge(S["f_down"], u - 1)
                    for c in range(FC):
                        act.wait_ge(S["f_up"], u * FC + c + 1)
                        act.activation(hid[:, u % 2, c, :], ps[:, c, :], ACT.Gelu_apprx_tanh,
                                       bias=b1c[:, u % NE, c:c + 1]).then_inc(S["f_gelu"], 1)
                    if u < NE:
                        t = NB // 8 + u
                        act.wait_ge(S["f_T"], nth("f_T", 12, 4 * t + 3))
                        for j in range(4):
                            act.copy(at(xT_all, 4 * t + j), ps[:, 6, j * P:(j + 1) * P]).then_inc(S["f_xT"], 1)

            def hidden_in():
                def norm(dst, src, done):
                    with act.Fori(0, NB // 8) as t:
                        for j in range(8):
                            i = 8 * t + j
                            act.activation(at(dst, i), at(src, i), ACT.Identity, bias=col(nmr, i),
                                           scale=col(rstd, i)).then_inc(S[done], 1)

                act.wait_ge(S["stage_go"], GO["ln1"])
                norm(h_all, x, "h_ready")
                sqrt_stats(9)
                act.wait_ge(S["stage_go"], GO["ln1b"])
                norm(xT_all, h_all, "un_ready")

            def moe():
                copy = turned(13, lambda t, j: work[:, j, 0:P])

                def body(I, has):
                    if has(1):
                        new = item(I, 1)
                        if has(-1):
                            act.wait_ge(S["f_xn"], nth("f_xn", 13, 4 * num(new) - 5))
                        for k in range(4):
                            i = 4 * num(new) + k
                            act.activation(nrm4[:, new[1], k, :], at(h_all, i), ACT.Identity, bias=col(nmr, i),
                                           scale=col(rstd, i)).then_inc(S["hn_ready"], 1)
                    if has(0):
                        act.wait_ge(S["f_copied"], 4 * num(I) + 4)
                        copy(num(I))

                act.wait_ge(S["stage_go"], GO[13])
                steps(act, body, NB // 4, 1, 0)
                act.wait_ge(S["route_act"], 1)
                act.activation(t2[:], t2[:], ACT.Exp).then_inc(S["route_act"], 1)
                with act.Fori(0, NB // 4) as t:
                    for e in range(NE):
                        n = t * NE + e
                        act.wait_ge(S["f_down"], G0 // FC + n - 1)
                        for c in range(FC):
                            act.wait_ge(S["f_up"], G0 + n * FC + c + 1)
                            act.activation(hid[:, e % 2, c, :], ps[:, c, :], ACT.Gelu).then_inc(S["f_gelu"], 1)

            act.wait_ge(S["tiny_ready"], 1)
            for c in range(4):
                act.wait_ge(S[f"dist_in{c}"], 16)
                with act.Fori(c * NB // 32, (c + 1) * NB // 32) as t:
                    for j in range(8):
                        o = at(logs, 8 * t + j)
                        act.activation(o, o, ACT.Ln, bias=sm[:, 11:12]).then_inc(S["bln_ready"], 1)
            sqrt_stats(1)
            attention(0)
            sqrt_stats(2)
            hadamard_ffn()
            sqrt_stats(3)
            attention(1)
            sqrt_stats(4)
            conv_ffn()
            sqrt_stats(5)
            attention(2)
            sqrt_stats(6)
            expert_ffn()
            sqrt_stats(7)
            attention(3)
            sqrt_stats(8)
            hidden_in()
            attention(4)
            sqrt_stats(10)
            moe()

        @block.vector
        def _(dve):
            chain = [0]

            def link(ins):
                chain[0] += 1
                ins.then_inc(S["dve_step"], 1)
                dve.wait_ge(S["dve_step"], chain[0])

            class Loop:
                def __init__(self, times, per):
                    self.times, self.per, self.base = times, per, chain[0]
                    chain[0] += times * per

                def turn(self, t):
                    self.t, self.k = t, 0

                def mark(self, ins):
                    self.k += 1
                    ins.then_inc(S["dve_step"], 1)

                def hold(self):
                    dve.wait_ge(S["dve_step"], self.base + self.t * self.per + self.k)

                def end(self):
                    assert self.k == self.per, (self.k, self.per)

            go = [0]

            def finish_stats(n):
                me, mo, ve, vo = stats[:, :, 1], stats[:, :, 4], stats[:, :, 2], stats[:, :, 5]
                link(dve.tensor_tensor(t1[:], ve, vo, ALU.add))
                link(dve.tensor_tensor(t2[:], me, mo, ALU.subtract))
                link(dve.tensor_tensor(t2[:], t2[:], t2[:], ALU.mult))
                link(dve.tensor_scalar(t1[:], t1[:], 1.0 / P, EPS, ALU.mult, ALU.add))
                link(dve.scalar_tensor_tensor(t1[:], t2[:], 0.25, t1[:], ALU.mult, ALU.add))
                dve.tensor_tensor(t2[:], me, mo, ALU.add).then_inc(S["sq_in"], 1)
                dve.wait_ge(S["sq_in"], n)
                dve.wait_ge(S["sq_out"], n)
                link(dve.reciprocal(rstd[:], t1[:]))
                ins = dve.scalar_tensor_tensor(nmr[:], t2[:], -0.5, rstd[:], ALU.mult, ALU.mult)
                link_go(ins)

            def link_go(ins):
                go[0] += 1
                ins.then_inc(S["stage_go"], 1)
                dve.wait_ge(S["stage_go"], go[0])

            def normalise(dst, i, src=x):
                return dve.tensor_scalar(dst, at(src, i), col(rstd, i), col(nmr, i), ALU.mult, ALU.add)

            def bn(i, src=x):
                o = stats[:, i, :] if isinstance(i, int) else stats[:, bass.ds(i, 1), :].rearrange("p a n -> p (a n)")
                return dve.bn_stats(o, at(src, i))

            def all_stats(src, first, last):
                with dve.Fori(first // 8, last // 8) as t:
                    for j in range(8):
                        bn(8 * t + j, src).then_inc(S["dve_step"], 1)
                chain[0] += last - first
                dve.wait_ge(S["dve_step"], chain[0])

            dve.memset(sm[:, 11:12], 1e-9).then_inc(S["tiny_ready"], 1)
            dve.wait_ge(S["consts_in"], 16 * N_CONSTS)
            link(dve.tensor_copy(identb[:], cpack[:, 0:P]))
            dve.tensor_copy(causalb[:], h_all[:, 32:34, :])
            dve.tensor_copy(trib[:], h_all[:, 34, :])
            dve.tensor_copy(onesb[:], h_all[:, 35, :])
            dve.tensor_copy(selb[:], h_all[:, 36:36 + NH, :])
            dve.memset(mparts[:], 0.0)
            link(dve.memset(vparts[:], 0.0))
            dve.memset(vparts[:, :, :, 0, DH:DH + 1], 1.0)
            dve.memset(xqT[:], 0.0)
            for s in range(5):
                dve.tensor_scalar(qscale[:, s, :], groupmask, QSCALE[s], None, ALU.mult)
                dve.tensor_scalar(qbias[:, s, :], groupmask, cols[:, 2 * s:2 * s + 1], QSCALE[s], ALU.mult, ALU.mult)
            link(dve.scalar_tensor_tensor(dscale[:], dscale[:], -1.0, dscale[:], ALU.mult, ALU.min))
            for c in range(2):
                dve.wait_ge(S[f"x_in{c}"], 16)
                all_stats(x, c * NB // 2, (c + 1) * NB // 2)
            dve.wait_ge(S["weights_in"], 16 * N_WEIGHTS)
            w0, w1, w2 = work[:, 0, 0:P], work[:, 1, :], work[:, 2, :]
            dve.tensor_reduce(sm[:, 0:1], w1, AX.X, ALU.add, apply_absolute_value=True)
            dve.tensor_reduce(sm[:, 1:2], w2, AX.X, ALU.add, apply_absolute_value=True)
            link(dve.tensor_reduce(sm[:, 2:3], w0, AX.X, ALU.add, apply_absolute_value=True))
            link(dve.tensor_scalar(sm[:, 2:3], sm[:, 2:3], 1.0 / P, 1e-5, ALU.mult, ALU.max))
            link(dve.reciprocal(sm[:, 3:4], sm[:, 2:3]))
            dve.tensor_scalar(work[:, 3, 0:P], ident, sm[:, 2:3], None, ALU.mult)
            link(dve.tensor_scalar(work[:, 3, P:2 * P], w0, sm[:, 3:4], 0.5, ALU.mult, ALU.is_gt))
            link(dve.tensor_scalar(work[:, 3, 2 * P:3 * P], w0, sm[:, 3:4], -0.5, ALU.mult, ALU.is_lt))
            dve.tensor_tensor(workb[:, 0, 0:P], work[:, 3, P:2 * P], work[:, 3, 2 * P:3 * P], ALU.subtract
                              ).then_inc(S["setup_dve"], 1)
            dve.wait_ge(S["setup_pe"], 2)
            dve.tensor_copy(ternT, ps[:, 0, 0:64].bitcast(BF16))
            dve.tensor_copy(wscale, ps[:, 1, 0:P])
            link(dve.tensor_scalar(sm[:, 4:6], ps[:, 2, 0:2], 1.0 / (P * FF), 1e-5, ALU.mult, ALU.max))
            link(dve.reciprocal(sm[:, 6:8], sm[:, 4:6]))
            for k, w in ((0, w1), (1, w2)):
                link(dve.tensor_scalar(w, w, sm[:, 6 + k:7 + k], ROUND, ALU.mult, ALU.add))
                link(dve.tensor_scalar(w, w, -ROUND, -1.0, ALU.add, ALU.max))
            link(dve.tensor_scalar(w1, w1, 1.0, sm[:, 4:5], ALU.min, ALU.mult))
            link(dve.tensor_scalar(w2q.rearrange("p c n -> p (c n)"), w2, 1.0, None, ALU.min))
            for k in range(3):
                link(dve.tensor_tensor(wconv[:, k, :], w1, ex[:, 0, k * FF:(k + 1) * FF], ALU.mult))
            bias_left = ex[0:3, 1, 0:FF]
            link(dve.tensor_copy(convb, bias_left))
            for r in range(2):
                link(dve.scalar_tensor_tensor(bias_left, convb, behind[0:3, r:r + 1], bias_left, ALU.mult, ALU.add))
                link(dve.tensor_copy(convb, bias_left))
            finish_stats(1)

            def attention(s):
                nk = nkeys(s)

                def keys(I):
                    t, j = I
                    dve.wait_ge(S["q_ready"], nth("q_ready", s, num(I)))
                    dve.wait_ge(S["proj_ready"], nth("proj_ready", s, num(I)))
                    dve.scalar_tensor_tensor(
                        kblk[:, j, 0:HG * nk].rearrange("p (a n) -> p a n", a=HG), bc(front[:, P:P + nk], HG),
                        cols[:, 2 * s + 1:2 * s + 2], bl(inmask, nk), ALU.add, ALU.mult
                    ).then_inc(S["k_ready"], 1)

                def values_in(I, used, out=False):
                    t, j = I
                    if used:
                        dve.wait_ge(S["vparts_ready"], nth("vparts_ready", s, num(I) - 2))
                    if out:
                        dve.wait_ge(S["wo_ready"], nth("wo_ready", s, num(I) - 3))
                    dve.wait_ge(S["vproj_ready"], nth("vproj_ready", s, num(I)))
                    dve.tensor_tensor(vf[0:nk, j, :], front[0:nk, 2 * P:3 * P], rows[0:nk, 0, :], ALU.add
                                      ).then_inc(S["vf_ready"], 1)

                def low_parts(I, c):
                    t, j = I
                    dve.wait_ge(S["e_ready"], nth("e_ready", s, num(I), c + 1, 2))
                    e = ex[0:nk, j, c * 1024:(c + 1) * 1024]
                    dve.tensor_tensor(exl[0:nk, j, c * 1024:(c + 1) * 1024], e, high(e), ALU.subtract
                                      ).then_inc(S["el_ready"], 1)

                def maxima(I, groups):
                    t, j = I
                    i = num(I)
                    for g in groups:
                        dve.wait_ge(S["a_ready"], nth("a_ready", s, i, g + 1, NG))
                        dve.tensor_reduce(negmax[:, j, HG * g:HG * g + HG],
                                          a_ps[g % 2][:, 0:HG * nk].rearrange("p (a n) -> p a n", a=HG),
                                          AX.X, ALU.max, negate=True).then_inc(S["max_ready"], 1)

                def max_parts(I):
                    t, j = I
                    i = num(I)
                    dve.wait_ge(S["max_ready"], nth("max_ready", s, i, NG, NG))
                    hi, low, whole = mparts[:, j, 0:NH], mparts[:, j, NH:2 * NH], negmax[:, j, :]
                    dve.tensor_copy(hi, whole).then_inc(S["mparts_ready"], 1)
                    dve.wait_ge(S["mparts_ready"], nth("mparts_ready", s, i, 1, 2))
                    dve.tensor_tensor(low, whole, hi, ALU.subtract
                                      ).then_inc(S["mparts_ready"], 1)

                def divide(I):
                    t, j = I
                    i = num(I)
                    dve.wait_ge(S["pv_ready"], nth("pv_ready", s, i))
                    pv = osum[:, j, :, :]
                    dve.tensor_reduce(pv, back[:, 0:NH * 27].rearrange("p (h a e) -> p h e a", h=NH, a=3),
                                      AX.X, ALU.add).then_inc(S["osum_ready"], 1)
                    dve.wait_ge(S["osum_ready"], nth("osum_ready", s, i))
                    if s == 3:
                        dve.tensor_scalar(rec[:, j, :], pv[:, :, 8], 1e-6, None, ALU.add).then_inc(S["eps_ready"], 1)
                        dve.wait_ge(S["eps_ready"], nth_o(i, 1))
                        dve.reciprocal(rec[:, j, :], rec[:, j, :]).then_inc(S["eps_ready"], 1)
                        dve.wait_ge(S["eps_ready"], nth_o(i, 2))
                        dve.scalar_tensor_tensor(rec[:, j, :], negmax[:, j, :], -MASKED / 2, rec[:, j, :],
                                                 ALU.is_lt, ALU.mult).then_inc(S["eps_ready"], 1)
                        dve.wait_ge(S["eps_ready"], nth_o(i, 3))
                    else:
                        dve.reciprocal(rec[:, j, :], pv[:, :, 8]).then_inc(S["rec_ready"], 1)
                        dve.wait_ge(S["rec_ready"], nth("rec_ready", s, i))
                    dve.tensor_tensor(o_sb[:, j, :].rearrange("p (h e) -> p h e", e=DH), pv[:, :, 0:DH],
                                      bl(rec[:, j, :], DH), ALU.mult).then_inc(S["o_ready"], 1)

                def nth_o(i, k):
                    return i * 3 + k

                def add_out(I):
                    t, j = I
                    i = num(I)
                    if s == 3:
                        dve.wait_ge(S["o_ready"], nth("o_ready", s, i))
                        ins = dve.tensor_tensor(at(x, i), o_sb[:, j, :], at(x, i), ALU.add)
                    elif s < 3:
                        dve.wait_ge(S["wo_ready"], nth("wo_ready", s, i))
                        dve.wait_ge(S["xbo_ready"], nth("xbo_ready", s, i))
                        ins = dve.tensor_tensor(at(x, i), front[:, 3 * P:4 * P], at(x, i), ALU.add)
                    else:
                        dve.wait_ge(S["wo_ready"], nth("wo_ready", s, i))
                        ins = dve.tensor_copy(y_sb[:, j, :], front[:, 3 * P:4 * P])
                    ins.then_inc(S["x_done"], 1)

                def new_stats(I):
                    i = num(I)
                    if s < 4:
                        dve.wait_ge(S["x_done"], nth("x_done", s, i))
                        bn(i).then_inc(S["dve_step"], 1)

                def body(I, has):
                    done, last, nxt = item(I, -2), item(I, -1), item(I, 1)
                    if has(-2):
                        divide(done)
                    if has(1):
                        keys(nxt)
                    if has(-1):
                        low_parts(last, 0)
                    if has(1):
                        values_in(nxt, has(-1), has(-2) and s != 3)
                    if has(-2):
                        if s == 4 and has(-4):
                            dve.wait_ge(S[f"y_out{done[1]}"], 2 * nth_dma("y_out0", 4, done[0] - 1))
                        add_out(done)
                    if has(-1):
                        low_parts(last, 1)
                    if has(1):
                        maxima(nxt, (0, 1))
                    if has(-2):
                        new_stats(done)
                    if has(1):
                        maxima(nxt, (2, 3))
                        max_parts(nxt)

                dve.wait_ge(S["stage_w_in"], W_IN[s])
                keys((0, 0))
                values_in((0, 0), False)
                maxima((0, 0), range(NG))
                max_parts((0, 0))
                steps(dve, body)
                if s < 4:
                    chain[0] += NB
                    dve.wait_ge(S["dve_step"], chain[0])

            def quantise(n, src, k0, hi, tmp, dst, mark, hold, out, dequant=False):
                for j in range(n):
                    mark(dve.tensor_reduce(sc[:, k0 + j, 0:1], src(j), AX.X, ALU.max, apply_absolute_value=True))
                hold()
                for j in range(n):
                    mark(dve.tensor_scalar(sc[:, k0 + j, 1:2], sc[:, k0 + j, 0:1], 1e-5, 1.0 / hi, ALU.max, ALU.mult))
                hold()
                for j in range(n):
                    mark(dve.reciprocal(sc[:, k0 + j, 2:3], sc[:, k0 + j, 1:2]))
                hold()
                for j in range(n):
                    mark(dve.tensor_scalar(tmp(j), src(j), sc[:, k0 + j, 2:3], ROUND, ALU.mult, ALU.add))
                hold()
                for j in range(n):
                    if dequant:
                        ins = dve.tensor_scalar(dst(j), tmp(j), -ROUND, sc[:, k0 + j, 1:2], ALU.add, ALU.mult)
                    else:
                        ins = dve.tensor_scalar(dst(j), tmp(j), -ROUND, None, ALU.add)
                    ins.then_inc(out, 1)

            def hadamard_ffn():
                def four(name, I, k=3):
                    dve.wait_ge(S[name], nth(name, 10, 4 * num(I) + k))

                def rounded(I, used):
                    count = [0]

                    def mark(ins):
                        count[0] += 1
                        ins.then_inc(S["q0_step"], 1)

                    def hold():
                        dve.wait_ge(S["q0_step"], num(I) * 16 + count[0])

                    four("f_mm", I)
                    if used:
                        four("f_qT", item(I, -2))
                    quantise(4, lambda k: ps[:, 1 + I[1], k * P:(k + 1) * P], 4 * I[1], 7.0,
                             lambda k: round4[:, I[1], k, :], lambda k: workb[:, k, I[1] * P:(I[1] + 1) * P],
                             mark, hold, S["f_q"])
                    assert count[0] == 16

                def add_out(I):
                    four("f_out", I)
                    for k in range(4):
                        dve.scalar_tensor_tensor(scaled4[:, I[1], k, :], ps[:, 4, k * P:(k + 1) * P],
                                                 sc[:, 4 * I[1] + k, 1:2], wscale, ALU.mult, ALU.mult
                                                 ).then_inc(S["scaled"], 1)
                    for k in range(4):
                        i = 4 * num(I) + k
                        dve.wait_ge(S["scaled"], i + 1)
                        dve.tensor_tensor(at(x, i), scaled4[:, I[1], k, :], at(x, i), ALU.add
                                          ).then_inc(S["f_o"], 1)
                    for k in range(4):
                        four("f_o", I, k)
                        bn(4 * num(I) + k).then_inc(S["dve_step"], 1)

                def body(I, has):
                    if has(0):
                        rounded(I, has(-2))
                    if has(-1):
                        add_out(item(I, -1))

                steps(dve, body, NB // 4, 3, 1)
                chain[0] += NB
                dve.wait_ge(S["dve_step"], chain[0])

            def conv_ffn():
                def pair(name, I, k=1):
                    dve.wait_ge(S[name], nth(name, 11, 2 * num(I) + k))

                def quantised(name, I, **kw):
                    k = [0]

                    def mark(ins):
                        k[0] += 1
                        ins.then_inc(S[name], 1)

                    def hold():
                        dve.wait_ge(S[name], num(I) * 8 + k[0])

                    quantise(2, mark=mark, hold=hold, **kw)
                    assert k[0] == 8

                def quantise_x(I, used):
                    j = 2 * I[1]
                    if used:
                        pair("f_T", item(I, -2))
                    pair("f_nrm", I)
                    quantised("qx_step", I, src=lambda k: nrm[:, j + k, :], k0=4 + j, hi=127.0,
                              tmp=lambda k: nrm[:, j + k, :], dst=lambda k: xn[:, j + k, :],
                              out=S["f_xn"], dequant=True)

                def quantise_hidden(I, used):
                    j = 2 * I[1]
                    if used:
                        pair("f_qT", item(I, -2))
                    pair("f_act", I)
                    quantised("qh_step", I, src=lambda k: work[:, j + k, :], k0=j, hi=127.0,
                              tmp=lambda k: work[:, j + k, :], dst=lambda k: workb[:, j + k, :],
                              out=S["f_q"])
                    for k in range(2):
                        dve.tensor_scalar(sc[:, j + k, 3:4], sc[:, j + k, 1:2], sm[:, 5:6], None, ALU.mult
                                          ).then_inc(S["f_scale"], 1)

                def add_out(I):
                    j = 2 * I[1]
                    for k in range(2):
                        i = 2 * num(I) + k
                        pair("f_scale", I, k)
                        pair("f_out", I)
                        dve.scalar_tensor_tensor(at(x, i), ps[:, 5, k * P:(k + 1) * P], sc[:, j + k, 3:4],
                                                 at(x, i), ALU.mult, ALU.add).then_inc(S["f_o"], 1)
                    for k in range(2):
                        pair("f_o", I, k)
                        bn(2 * num(I) + k).then_inc(S["dve_step"], 1)

                def body(I, has):
                    if has(0):
                        quantise_hidden(I, has(-2))
                    if has(-1):
                        add_out(item(I, -1))
                    if has(2):
                        quantise_x(item(I, 2), has(0))

                steps(dve, body, NB // 2, 3, 1)
                chain[0] += NB
                dve.wait_ge(S["dve_step"], chain[0])

            def expert_ffn():
                def norm(t):
                    for j in range(4):
                        dve.wait_ge(S["f_T"], nth("f_T", 12, 4 * t + j - 4))
                        normalise(xn[:, j, :], 4 * t + j).then_inc(S["f_xn"], 1)

                L = Loop(NB // 4, 8)

                def add_back(t):
                    L.turn(t)
                    dve.wait_ge(S["f_backT"], 4 * t + 4)
                    for j in range(4):
                        L.mark(dve.tensor_tensor(at(x, 4 * t + j), ps[:, 7, j * P:(j + 1) * P],
                                                 at(x, 4 * t + j), ALU.add))
                    L.hold()
                    dve.sem_inc(S["f_back"], 4)
                    for j in range(4):
                        L.mark(bn(4 * t + j))
                    L.end()

                with dve.Fori(0, NB // 8) as t:
                    norm(t)
                norm(NB // 8)
                for u in range(2 * NE):
                    half, e = u // NE, u % NE
                    if u + 1 < NE:
                        norm(NB // 8 + u + 1)
                    dve.wait_ge(S["f_down"], u + 1)
                    dve.tensor_scalar(h_all[:, half * 32:half * 32 + 32, e * 16:e * 16 + 16],
                                      ps[:, 4 + u % 2, :].rearrange("p (b n) -> p b n", n=16),
                                      b2c[:, e:e + 1], None, ALU.add).then_inc(S["f_acc"], 1)
                    if u >= NE:
                        add_back(u - NE)
                with dve.Fori(NB // 8, NB // 4) as t:
                    add_back(t)
                dve.wait_ge(S["dve_step"], chain[0])

            def hidden_in():
                with dve.Fori(0, NB // 8) as t:
                    for j in range(8):
                        dve.wait_ge(S["h_ready"], 8 * t + j + 1)
                        bn(8 * t + j, h_all).then_inc(S["dve_step"], 1)
                chain[0] += NB
                dve.wait_ge(S["dve_step"], chain[0])
                finish_stats(9)
                dve.wait_ge(S["stage_w_in"], W_IN["ln1"])
                L = Loop(NB // 4, 1)
                with dve.Fori(0, NB // 4) as t:
                    L.turn(t)
                    dve.wait_ge(S["un_ready"], 4 * t + 4)
                    L.mark(dve.tensor_tensor(at4(xT_all, t), at4(xT_all, t), bc(rows[:, 0, :], 4), ALU.mult))
                    L.hold()
                    dve.tensor_tensor(at4(xT_all, t), at4(xT_all, t), bc(rows[:, 1, :], 4), ALU.add
                                      ).then_inc(S["u_made"], 1)
                    L.end()
                dve.wait_ge(S["u_made"], NB // 4)
                link_go(dve.memset(sm[:, 9:10], 0.0))

            def moe():
                for c in range(4):
                    dve.wait_ge(S[f"y_in{c}"], 16)
                    with dve.Fori(c * NB // 16, (c + 1) * NB // 16) as t:
                        dve.tensor_tensor(at4(h_all, t), at4(h_all, t), at4(xT_all, t), ALU.add
                                          ).then_inc(S["y_added"], 1)
                        dve.wait_ge(S["y_added"], t + 1)
                        for j in range(4):
                            bn(4 * t + j, h_all).then_inc(S["dve_step"], 1)
                chain[0] += NB
                dve.wait_ge(S["dve_step"], chain[0])
                finish_stats(10)
                dve.wait_ge(S["stage_w_in"], W_IN["ln2"])

                def body(I, has):
                    i = num(I)
                    normed = nrm4[:, I[1], :, :]
                    dve.wait_ge(S["hn_ready"], 4 * i + 4)
                    dve.tensor_tensor(normed, normed, bc(rows[:, 0, :], 4), ALU.mult).then_inc(S["hn_scaled"], 1)
                    dve.wait_ge(S["hn_scaled"], i + 1)
                    dve.wait_ge(S["f_T"], nth("f_T", 13, 4 * i - 1))
                    dve.tensor_tensor(xn[:], normed, bc(rows[:, 1, :], 4), ALU.add).then_inc(S["f_xn"], 4)

                steps(dve, body, NB // 4, 0, 0)
                dve.wait_ge(S["f_lg"], NB)
                dve.wait_ge(S["f_cp"], 2 * NB)
                lg = ps[:, 7, :].rearrange("p (s e) -> p s e", e=NE)
                m1, m2, top = t1[:], t2[:], nmr[:]

                def pick(logits, m, sel):
                    link(dve.tensor_reduce(m, logits, AX.X, ALU.max))
                    link(dve.tensor_tensor(sel, logits, bl(m, NE), ALU.is_ge))
                    link(dve.tensor_tensor(sel, sel, bc(descend, NB), ALU.mult))
                    link(dve.tensor_reduce(top, sel, AX.X, ALU.max))
                    link(dve.tensor_tensor(sel, sel, bl(top, NE), ALU.is_equal))

                pick(lg, m1, ra)
                link(dve.scalar_tensor_tensor(rb, ra, MASKED, lg, ALU.mult, ALU.add))
                pick(rb, m2, rc_)
                link(dve.tensor_tensor(selbf.rearrange("p (s e) -> p s e", e=NE), ra, rc_, ALU.add))
                dve.tensor_tensor(m2, m2, m1, ALU.subtract).then_inc(S["route_dve"], 1)
                dve.wait_ge(S["route_dve"], 1)
                dve.sem_inc(S["route_act"], 1)
                dve.wait_ge(S["route_act"], 2)
                link(dve.tensor_scalar(m1, m2, 1.0, None, ALU.add))
                link(dve.reciprocal(m1, m1))
                link(dve.tensor_tensor(m2, m2, m1, ALU.mult))
                link(dve.tensor_tensor(ra, ra, bl(m1, NE), ALU.mult))
                link(dve.tensor_tensor(rc_, rc_, bl(m2, NE), ALU.mult))
                link(dve.tensor_tensor(coef, ra, rc_, ALU.add))
                dve.wait_ge(S["route_pe"], 1)
                total = ps[:, 7, :].rearrange("p (s e) -> p s e", e=NE)
                link(dve.tensor_copy(ra, total))
                old, new = ra, rb
                k = 1
                while k < NB:
                    link(dve.tensor_tensor(new[:, k:, :], old[:, k:, :], old[:, :NB - k, :], ALU.add))
                    link(dve.tensor_copy(new[:, 0:k, :], old[:, 0:k, :]))
                    old, new = new, old
                    k *= 2
                link(dve.tensor_tensor(new, old, total, ALU.subtract))
                link(dve.tensor_tensor(new, new, ps[:, 6, :].rearrange("p (s e) -> p s e", e=NE), ALU.add))
                link(dve.scalar_tensor_tensor(coef, new, float(CAP), coef, ALU.is_lt, ALU.mult))
                dve.wait_ge(S["x_added"], NB)
                L = Loop(NB // 4, 4 * NE)
                with dve.Fori(0, NB // 4) as t:
                    L.turn(t)
                    for e in range(NE):
                        dve.wait_ge(S["f_down"], G0 // FC + t * NE + e + 1)
                        for r in range(4):
                            i = 4 * t + r
                            L.mark(dve.scalar_tensor_tensor(
                                at(x, i), ps[:, 4 + e % 2, r * P:(r + 1) * P],
                                coef[:, bass.ds(i, 1), e:e + 1].rearrange("p a n -> p (a n)"), at(x, i),
                                ALU.mult, ALU.add))
                        L.hold()
                        dve.sem_inc(S["f_acc"], 1)
                    L.end()
                link_go(dve.memset(sm[:, 9:10], 0.0))

            attention(0)
            finish_stats(2)
            hadamard_ffn()
            finish_stats(3)
            attention(1)
            finish_stats(4)
            conv_ffn()
            finish_stats(5)
            attention(2)
            finish_stats(6)
            expert_ffn()
            finish_stats(7)
            attention(3)
            finish_stats(8)
            hidden_in()
            attention(4)
            moe()

        @block.gpsimd
        def _(pool):
            def settled():
                pool.sem_inc(S["pool_step"], 1)

            def attention(s):
                nk = nkeys(s)

                def bias(I, used):
                    t, j = I
                    i = num(I)
                    if s not in (0, 1, 3):
                        return
                    if used:
                        pool.wait_ge(S["b_ready"], nth("b_ready", s, i - 2, 2, 2))
                    if s == 0:
                        pool.wait_ge(S["bln_ready"], nth("bln_ready", s, i))
                        settled()
                        pool.tensor_tensor(biasf[:, j, :], at(logs, i), dscale[:, 0:1].to_broadcast([P, NC]), ALU.mult
                                           ).then_inc(S["biasf_ready"], 1)
                        pool.wait_ge(S["biasf_ready"], nth("biasf_ready", s, i))
                        settled()
                        pool.tensor_copy(biasb[:, j, :], biasf[:, j, :]).then_inc(S["bias_ready"], 1)
                        pool.wait_ge(S["bias_ready"], nth("bias_ready", s, i))
                        pool.tensor_tensor(biasf[:, j, :], biasf[:, j, :], biasb[:, j, :], ALU.subtract
                                           ).then_inc(S["bleft_ready"], 1)
                        pool.wait_ge(S["bleft_ready"], nth("bleft_ready", s, i))
                        settled()
                        pool.tensor_copy(bias2[:, j, :], biasf[:, j, :]).then_inc(S["bias2_ready"], 1)
                        pool.wait_ge(S["bias2_ready"], nth("bias2_ready", s, i))
                        pool.tensor_tensor(bias3[:, j, :], biasf[:, j, :], bias2[:, j, :], ALU.subtract
                                           ).then_inc(S["bias3_ready"], 1)
                        return
                    pool.wait_ge(S[f"bias_in{j}"], nth_dma("bias_in0", s, t))
                    raw = braw[:, j, :].bitcast(I32) if s == 1 else braw_u[:, j, :]
                    settled()
                    pool.tensor_scalar(biasb[:, j, :], raw, 0.0, MASKED, ALU.is_equal, ALU.mult
                                       ).then_inc(S["bias_ready"], 1)

                def split_v(I, used):
                    t, j = I
                    i = num(I)
                    v = vf[0:nk, j, :].rearrange("p (h e) -> p h e", e=DH)
                    left = vleft[0:nk, :].rearrange("p (h e) -> p h e", e=DH)
                    v1, v2, v3 = (vparts[0:nk, j, :, k, 0:DH] for k in range(3))
                    pool.wait_ge(S["vf_ready"], nth("vf_ready", s, i))
                    if used:
                        pool.wait_ge(S["pv_ready"], nth("pv_ready", s, i - 2))
                    settled()
                    pool.tensor_copy(v1, v).then_inc(S["v1_ready"], 1)
                    pool.wait_ge(S["v1_ready"], nth("v1_ready", s, i))
                    pool.tensor_tensor(left, v, v1, ALU.subtract).then_inc(S["vleft_ready"], 1)
                    pool.wait_ge(S["vleft_ready"], nth("vleft_ready", s, i))
                    settled()
                    pool.tensor_copy(v2, left).then_inc(S["v2_ready"], 1)
                    pool.wait_ge(S["v2_ready"], nth("v2_ready", s, i))
                    pool.tensor_tensor(v3, left, v2, ALU.subtract).then_inc(S["vparts_ready"], 1)

                def add_bo(I):
                    i = num(I)
                    if s < 3:
                        pool.wait_ge(S["xn_ready"], nth("xn_ready", s, i))
                        pool.tensor_tensor(at(x, i), at(x, i), rows[:, 1, :], ALU.add).then_inc(S["xbo_ready"], 1)
                    if s == 3:
                        pool.wait_ge(S["xn_ready"], nth("xn_ready", s, i))

                def body(I, has):
                    if has(1):
                        bias(item(I, 1), has(-1))
                    if has(0):
                        split_v(I, has(-2))
                        add_bo(I)

                pool.wait_ge(S["stage_go"], GO[s])
                pool.wait_ge(S["stage_w_in"], W_IN[s])
                bias((0, 0), False)
                steps(pool, body)

            def expert_back():
                for half in range(2):
                    pool.wait_ge(S["f_acc"], NE * (half + 1))
                    with pool.Fori(half * NB // 8, (half + 1) * NB // 8) as t:
                        for j in range(4):
                            pool.wait_ge(S["f_back"], 4 * t + j + 1)
                            settled()
                            pool.tensor_copy(work[:, j, 0:P], at(h_all, 4 * t + j)).then_inc(S["f_cp"], 1)

            def add_hidden():
                with pool.Fori(0, NB // 4) as t:
                    pool.wait_ge(S["y_added"], t + 1)
                    for j in range(4):
                        i = 4 * t + j
                        pool.tensor_tensor(at(x, i), at(x, i), at(h_all, i), ALU.add).then_inc(S["x_added"], 1)

            def keep_turned():
                with pool.Fori(0, NB // 4) as t:
                    for j in range(4):
                        pool.wait_ge(S["f_xT"], nth("f_xT", 13, 4 * t + j))
                        settled()
                        pool.tensor_copy(at(xT_all, 4 * t + j), work[:, j, 0:P]).then_inc(S["f_cp"], 1)
                    for j in range(4):
                        pool.wait_ge(S["f_cp"], NB + 4 * t + j + 1)
                        pool.wait_ge(S["f_lg"], 4 * t + j + 1)
                        pool.sem_inc(S["f_copied"], 1)

            pool.sem_inc(S["f_back"], 4)
            pool.sem_inc(S["f_copied"], 4)
            attention(0)
            attention(1)
            attention(2)
            expert_back()
            pool.wait_ge(S["stage_go"], GO[12] + 1)
            pool.sem_inc(S["ffn2_done"], 1)
            attention(3)
            attention(4)
            add_hidden()
            keep_turned()


def kernel(**inputs):
    import concourse.bacc as bacc
    from concourse.bass_utils import run_bass_kernel_spmd as run

    a = {n: np.ascontiguousarray(v) for n, v in inputs.items()}
    f = np.float32
    eye = np.eye(P, dtype=f)
    had = np.array([[1.0]])
    while had.shape[0] < P:
        had = np.block([[had, had], [had, -had]])
    had = (had / np.sqrt(P)).astype(f)
    p = np.arange(P)
    groupmask = (p[:, None] // (HG * DH) == np.arange(NG)[None]).astype(f)
    inmask = (p[:, None] // DH % HG == np.arange(HG)[None]).astype(f)
    descend = np.broadcast_to(np.arange(NE, 0, -1, dtype=f), (P, NE))
    behind = -(p[:, None] > np.arange(2)[None]).astype(f)
    cpack = np.concatenate([eye, had, np.ones((P, P), f), groupmask, inmask, descend, behind], axis=1)
    causal2 = np.where(p[None] <= p[:, None], 0.0, MASKED).astype(f)
    causal4 = np.where((p[None] // NB == p[:, None] // NB) & (p[None] <= p[:, None]), 0.0, MASKED).astype(f)
    tri = (p[:, None] < p[None]).astype(f)
    bpack = np.stack([causal2, causal4, tri, np.ones((P, P), f)], axis=1)
    sel = ((p[:, None] < 2 * NH) & (p[:, None] % NH == np.arange(NH)[None])).astype(f)
    selpack = np.ascontiguousarray(np.broadcast_to(sel[:, :, None], (P, NH, P)))
    h = np.arange(P) // DH
    r = (h // 2) * 4 * DH
    e = np.arange(P) % DH
    qkv = a["L3_ffn_qkv_weight"]
    moe_q, moe_k, moe_v = qkv[r + (h % 2) * DH + e], qkv[r + 2 * DH + e], qkv[r + 3 * DH + e]
    z = np.zeros((P, P), f)
    wm = np.stack([np.stack([w.T for w in ws]) for ws in (
        [a["L0_xattn_W" + c] for c in "qkvo"],
        [a["L1_xattn_W_" + c] for c in "qkvo"],
        [a["L2_xattn_W" + c] for c in "qkvo"],
        [a["L3_xattn_W" + c] for c in "qkv"] + [z],
        [moe_q, moe_k, moe_v, a["L3_ffn_proj_weight"]])])
    zr = np.zeros(P, f)
    cols = np.stack([a["L0_xattn_bq"], a["L0_xattn_bk"], a["L1_xattn_b_q"], a["L1_xattn_b_k"], zr, zr,
                     a["L3_xattn_bq"], a["L3_xattn_bk"], zr, zr], axis=1)
    rows = np.stack([np.stack(v) for v in (
        [a["L0_xattn_bv"], a["L0_xattn_bo"]], [a["L1_xattn_b_v"], a["L1_xattn_b_o"]],
        [zr, a["L2_xattn_bo"]], [a["L3_xattn_bv"], zr], [zr, zr],
        [a["L3_ffn_ln1_weight"], a["L3_ffn_ln1_bias"]], [a["L3_ffn_ln2_weight"], a["L3_ffn_ln2_bias"]])])
    arrays = {
        "x": a["x"], "ctx": a["ctx_1024"], "dist": a["fside_BxSxS2_0"],
        "mask1": a["mask_Bx1xSxS2_ik1"].reshape(NB, P, NC), "mask3": a["mask_BxSxS2_bk1"],
        "cpack": cpack, "bpack": bpack, "selpack": selpack, "wm": wm, "cols": cols, "rows": rows,
        "dscale": a["L0_xattn_distance_scaling"].reshape(1, 1), "router": a["L3_ffn_router_weight"],
        "L0_w": a["L0_ffn_weight"], "w1T": a["L1_ffn_w1"].T,
        "w2T": a["L1_ffn_w2"].T.reshape(FC, P, P).transpose(1, 0, 2),
        "convT": a["L1_ffn_conv_w"][:, 0, :].T, "convb": a["L1_ffn_conv_b"].reshape(1, FF),
        "b1c": a["L2_ffn_b1"].reshape(NE, FC, P).transpose(2, 0, 1), "b2c": a["L2_ffn_b2"].T,
        "L2_W1": a["L2_ffn_W1"], "L2_W2": a["L2_ffn_W2"],
        "L3_W1": a["L3_ffn_moe_w1"], "L3_W2": a["L3_ffn_moe_w2"],
    }
    arrays = {n: np.ascontiguousarray(v) for n, v in arrays.items()}
    nc = bacc.Bacc("TRN2", target_bir_lowering=False, num_devices=1)
    d = {n: nc.dram_tensor("in_" + n, v.shape, mybir.dt.from_np(v.dtype), kind="ExternalInput").ap()
         for n, v in arrays.items()}
    out = nc.dram_tensor("out", (NB, P, P), F32, kind="ExternalOutput").ap()
    build(nc, d, out)
    r = run(nc, [{"in_" + n: v for n, v in arrays.items()}], core_ids=[0])
    return r.results[0]["out"]
```
